# Optimizing a Trainium2 kernel written in Bass

```python
import numpy as np
import jax
import jax.numpy as jnp

def _softmax(x, axis=-1):
    return jax.nn.softmax(x, axis=axis)

def _gelu(x):
    return jax.nn.gelu(x, approximate=True)

def _silu(x):
    return jax.nn.silu(x)

def _sigmoid(x):
    return jax.nn.sigmoid(x)

def _layernorm(x, axis=-1, eps=1e-05):
    m = jnp.mean(x, axis=axis, keepdims=True)
    v = jnp.var(x, axis=axis, keepdims=True)
    return (x - m) / jnp.sqrt(v + eps)

def _scatter_add(tgt, idx, src, axis=0):
    return tgt.at[idx].add(src)

def _segment_sum(src, seg, n):
    return jax.ops.segment_sum(src, seg, n)
kernel_name = 'mk_hybrid_d2_jaxref_r8_eb3349'

def setup_inputs(seed: int=0):
    np.random.seed(seed)
    _w = jnp.asarray

    def _L0_attn_a_setup():
        import jax, jax.numpy as jnp
        import numpy as np
        import math
        N_HEAD = 16

        def _rope_cos_sin(T, head_dim):
            j = jnp.arange(head_dim // 2, dtype=jnp.float32)
            theta = jnp.power(10000.0, -2.0 * j / head_dim)
            t = jnp.arange(T, dtype=jnp.float32)
            ang = t[:, None] * theta[None, :]
            return (jnp.cos(ang), jnp.sin(ang))

        def _apply_rope(u, cos, sin):
            B, H, T, d = u.shape
            u = u.reshape(B, H, T, d // 2, 2)
            u0, u1 = (u[..., 0], u[..., 1])
            r0 = u0 * cos - u1 * sin
            r1 = u0 * sin + u1 * cos
            return jnp.stack([r0, r1], axis=-1).reshape(B, H, T, d)
        key = jax.random.key(seed)
        ks = jax.random.split(key, 9)
        C = 128
        s = 1.0 / math.sqrt(C)
        return {'x': jax.random.normal(ks[0], (4, 256, C), dtype=jnp.float32), 'wq': jax.random.normal(ks[1], (C, C), dtype=jnp.float32) * s, 'bq': jax.random.normal(ks[2], (C,), dtype=jnp.float32) * s, 'wk': jax.random.normal(ks[3], (C, C), dtype=jnp.float32) * s, 'bk': jax.random.normal(ks[4], (C,), dtype=jnp.float32) * s, 'wv': jax.random.normal(ks[5], (C, C), dtype=jnp.float32) * s, 'bv': jax.random.normal(ks[6], (C,), dtype=jnp.float32) * s, 'wp': jax.random.normal(ks[7], (C, C), dtype=jnp.float32) * s, 'bp': jax.random.normal(ks[8], (C,), dtype=jnp.float32) * s}
    _L0_attn_a_in = _L0_attn_a_setup()

    def _L0_attn_b_setup():
        import jax, jax.numpy as jnp
        import numpy as np
        B, N, DE, H, DH = (2, 128, 128, 16, 64)
        DK = H * DH
        MIN_EXP = -30.0
        EPS = 0.0001
        key = jax.random.key(seed)
        ks = jax.random.split(key, 8)

        def g(i, shape, sc=1.0):
            return jax.random.normal(ks[i], shape, jnp.float32) * sc
        freqs = 10000.0 ** (-np.arange(DH // 2, dtype=np.float64) / (DH // 2))
        omega = jnp.asarray(np.tile(freqs[None, :], (H, 1)), jnp.float32)
        return {'x': g(0, (B, N, DE)), 'Wq': g(1, (DE, 2 * DK), 1.0 / np.sqrt(DE)), 'Wk': g(2, (DE, 2 * DK), 1.0 / np.sqrt(DE)), 'Wv': g(3, (DE, 2 * DK), 1.0 / np.sqrt(DE)), 'Wo': g(4, (2 * DK, DE), 1.0 / np.sqrt(2 * DK)), 'omega': omega, 'mu_raw': g(5, (H,)) - 2.0, 'sigma_raw': g(6, (H,)), 'eta_raw': jnp.ones((H,), jnp.float32), 'gamma_raw': jnp.ones((H,), jnp.float32), 'tau': jnp.ones((H,), jnp.float32), 'nu_raw': jnp.ones((H,), jnp.float32) * 4.0}
    _L0_attn_b_in = _L0_attn_b_setup()

    def _L0_ffn_setup():
        import jax, jax.numpy as jnp
        import numpy as np
        D_MODEL = 128
        HIDDEN = 512
        NUM_EXPERTS = 8
        TOP_K = 2
        key = jax.random.key(seed)
        k_x, k_g, k_in, k_out = jax.random.split(key, 4)
        bound_in = 1.0 / HIDDEN
        bound_out = 1.0 / D_MODEL
        x = jax.random.normal(k_x, (2, 256, D_MODEL), dtype=jnp.float32)
        w_gate = jax.random.uniform(k_g, (NUM_EXPERTS, D_MODEL), dtype=jnp.float32, minval=-D_MODEL ** (-0.5), maxval=D_MODEL ** (-0.5))
        w_in = jax.random.uniform(k_in, (NUM_EXPERTS, HIDDEN, D_MODEL), dtype=jnp.float32, minval=-bound_in, maxval=bound_in)
        w_out = jax.random.uniform(k_out, (NUM_EXPERTS, D_MODEL, HIDDEN), dtype=jnp.float32, minval=-bound_out, maxval=bound_out)
        return {'x': x, 'w_gate': w_gate, 'w_in': w_in, 'w_out': w_out}
    _L0_ffn_in = _L0_ffn_setup()

    def _L1_attn_a_setup():
        import jax, jax.numpy as jnp
        import numpy as np
        H, KV, D = (8, 2, 32)
        RD = D // 4
        ROPE_THETA = 10000.0

        def _rope_cos_sin(seq_len, dtype):
            inv_freq = 1.0 / ROPE_THETA ** (jnp.arange(0, RD, 2, dtype=jnp.float32) / RD)
            pos = jnp.arange(seq_len, dtype=jnp.float32)
            freqs = pos[:, None] * inv_freq[None, :]
            emb = jnp.concatenate([freqs, freqs], axis=-1)
            return (jnp.cos(emb).astype(dtype), jnp.sin(emb).astype(dtype))

        def _apply_partial_rope(x, cos, sin):
            x_rot, x_pass = (x[..., :RD], x[..., RD:])
            half = RD // 2
            rot = jnp.concatenate([-x_rot[..., half:], x_rot[..., :half]], axis=-1)
            x_rot = x_rot * cos[None, None] + rot * sin[None, None]
            return jnp.concatenate([x_rot, x_pass], axis=-1)
        key = jax.random.key(seed)
        ks = jax.random.split(key, 5)
        B, S, hid = (4, 256, 128)
        s = 0.02
        return {'hidden_states': jax.random.normal(ks[0], (B, S, hid), jnp.float32), 'Wq': jax.random.normal(ks[1], (hid, H * D * 2), jnp.float32) * s, 'Wk': jax.random.normal(ks[2], (hid, KV * D), jnp.float32) * s, 'Wv': jax.random.normal(ks[3], (hid, KV * D), jnp.float32) * s, 'Wo': jax.random.normal(ks[4], (H * D, hid), jnp.float32) * s}
    _L1_attn_a_in = _L1_attn_a_setup()

    def _L1_attn_b_setup():
        import jax, jax.numpy as jnp
        import numpy as np
        B, T, E, H = (2, 256, 128, 16)
        D = E // H
        key = jax.random.key(seed)
        k = jax.random.split(key, 6)
        return {'x': jax.random.normal(k[0], (B, T, E), dtype=jnp.float32), 'w_att_val': jax.random.normal(k[1], (H, D, D), dtype=jnp.float32) * (6.0 / D) ** 0.5, 'wv_w': jax.random.normal(k[2], (E, E), dtype=jnp.float32) * E ** (-0.5), 'wv_b': jnp.zeros((E,), dtype=jnp.float32), 'out_w': jax.random.normal(k[3], (E, E), dtype=jnp.float32) * E ** (-0.5), 'out_b': jnp.zeros((E,), dtype=jnp.float32)}
    _L1_attn_b_in = _L1_attn_b_setup()

    def _L1_ffn_setup():
        import jax, jax.numpy as jnp
        import numpy as np
        NUM_EXPERTS_TOTAL = 9
        TOP_K = 2
        key = jax.random.key(seed)
        k0, k1, k2, k3, k4 = jax.random.split(key, 5)
        B, S, H, I = (2, 256, 128, 352)
        E = NUM_EXPERTS_TOTAL
        x = jax.random.normal(k0, (B, S, H), dtype=jnp.float32)
        Wr = jax.random.normal(k1, (H, E), dtype=jnp.float32) * 0.02
        Wg = jax.random.normal(k2, (E, H, I), dtype=jnp.float32) * 0.02
        Wu = jax.random.normal(k3, (E, H, I), dtype=jnp.float32) * 0.02
        Wd = jax.random.normal(k4, (E, I, H), dtype=jnp.float32) * 0.02
        return {'x': x, 'Wr': Wr, 'Wg': Wg, 'Wu': Wu, 'Wd': Wd}
    _L1_ffn_in = _L1_ffn_setup()
    _d = {'L0_attn_a_x': _L0_attn_a_in['x'], 'L0_attn_a_wq': _L0_attn_a_in['wq'], 'L0_attn_a_bq': _L0_attn_a_in['bq'], 'L0_attn_a_wk': _L0_attn_a_in['wk'], 'L0_attn_a_bk': _L0_attn_a_in['bk'], 'L0_attn_a_wv': _L0_attn_a_in['wv'], 'L0_attn_a_bv': _L0_attn_a_in['bv'], 'L0_attn_a_wp': _L0_attn_a_in['wp'], 'L0_attn_a_bp': _L0_attn_a_in['bp'], 'L0_attn_b_Wq': _L0_attn_b_in['Wq'], 'L0_attn_b_Wk': _L0_attn_b_in['Wk'], 'L0_attn_b_Wv': _L0_attn_b_in['Wv'], 'L0_attn_b_Wo': _L0_attn_b_in['Wo'], 'L0_attn_b_omega': _L0_attn_b_in['omega'], 'L0_attn_b_mu_raw': _L0_attn_b_in['mu_raw'], 'L0_attn_b_sigma_raw': _L0_attn_b_in['sigma_raw'], 'L0_attn_b_eta_raw': _L0_attn_b_in['eta_raw'], 'L0_attn_b_gamma_raw': _L0_attn_b_in['gamma_raw'], 'L0_attn_b_tau': _L0_attn_b_in['tau'], 'L0_attn_b_nu_raw': _L0_attn_b_in['nu_raw'], 'L0_ffn_w_gate': _L0_ffn_in['w_gate'], 'L0_ffn_w_in': _L0_ffn_in['w_in'], 'L0_ffn_w_out': _L0_ffn_in['w_out'], 'L1_attn_a_Wq': _L1_attn_a_in['Wq'], 'L1_attn_a_Wk': _L1_attn_a_in['Wk'], 'L1_attn_a_Wv': _L1_attn_a_in['Wv'], 'L1_attn_a_Wo': _L1_attn_a_in['Wo'], 'L1_attn_b_w_att_val': _L1_attn_b_in['w_att_val'], 'L1_attn_b_wv_w': _L1_attn_b_in['wv_w'], 'L1_attn_b_wv_b': _L1_attn_b_in['wv_b'], 'L1_attn_b_out_w': _L1_attn_b_in['out_w'], 'L1_attn_b_out_b': _L1_attn_b_in['out_b'], 'L1_ffn_Wr': _L1_ffn_in['Wr'], 'L1_ffn_Wg': _L1_ffn_in['Wg'], 'L1_ffn_Wu': _L1_ffn_in['Wu'], 'L1_ffn_Wd': _L1_ffn_in['Wd']}
    _x0 = _d['L0_attn_a_x']
    _d['L0_attn_a_x'] = jax.random.normal(jax.random.fold_in(jax.random.key(seed), 1), (8, 512, 128), dtype=_x0.dtype)
    del _x0
    return _d

def reference(L0_attn_a_x, L0_attn_a_wq, L0_attn_a_bq, L0_attn_a_wk, L0_attn_a_bk, L0_attn_a_wv, L0_attn_a_bv, L0_attn_a_wp, L0_attn_a_bp, L0_attn_b_Wq, L0_attn_b_Wk, L0_attn_b_Wv, L0_attn_b_Wo, L0_attn_b_omega, L0_attn_b_mu_raw, L0_attn_b_sigma_raw, L0_attn_b_eta_raw, L0_attn_b_gamma_raw, L0_attn_b_tau, L0_attn_b_nu_raw, L0_ffn_w_gate, L0_ffn_w_in, L0_ffn_w_out, L1_attn_a_Wq, L1_attn_a_Wk, L1_attn_a_Wv, L1_attn_a_Wo, L1_attn_b_w_att_val, L1_attn_b_wv_w, L1_attn_b_wv_b, L1_attn_b_out_w, L1_attn_b_out_b, L1_ffn_Wr, L1_ffn_Wg, L1_ffn_Wu, L1_ffn_Wd):

    def _L0_attn_a_ref(x, wq, bq, wk, bk, wv, bv, wp, bp):
        import jax, jax.numpy as jnp
        import numpy as np
        import math
        N_HEAD = 16

        def _rope_cos_sin(T, head_dim):
            j = jnp.arange(head_dim // 2, dtype=jnp.float32)
            theta = jnp.power(10000.0, -2.0 * j / head_dim)
            t = jnp.arange(T, dtype=jnp.float32)
            ang = t[:, None] * theta[None, :]
            return (jnp.cos(ang), jnp.sin(ang))

        def _apply_rope(u, cos, sin):
            B, H, T, d = u.shape
            u = u.reshape(B, H, T, d // 2, 2)
            u0, u1 = (u[..., 0], u[..., 1])
            r0 = u0 * cos - u1 * sin
            r1 = u0 * sin + u1 * cos
            return jnp.stack([r0, r1], axis=-1).reshape(B, H, T, d)
        B, T, C = x.shape
        H = N_HEAD
        d = C // H

        def proj(w, b):
            return (jnp.einsum('btc,oc->bto', x, w) + b).reshape(B, T, H, d).transpose(0, 2, 1, 3)
        q, k, v = (proj(wq, bq), proj(wk, bk), proj(wv, bv))
        cos, sin = _rope_cos_sin(T, d)
        q = _apply_rope(q, cos, sin)
        k = _apply_rope(k, cos, sin)
        att = jnp.einsum('bhqd,bhkd->bhqk', q, k) * (1.0 / math.sqrt(d))
        causal = jnp.tril(jnp.ones((T, T), dtype=bool))
        att = jnp.where(causal, att, jnp.finfo(att.dtype).min)
        att = jax.nn.softmax(att, axis=-1)
        y = jnp.einsum('bhqk,bhkd->bhqd', att, v)
        y = y.transpose(0, 2, 1, 3).reshape(B, T, C)
        return jnp.einsum('btc,oc->bto', y, wp) + bp

    def _L0_attn_b_ref(x, Wq, Wk, Wv, Wo, omega, mu_raw, sigma_raw, eta_raw, gamma_raw, tau, nu_raw):
        import jax, jax.numpy as jnp
        import numpy as np
        B, N, DE, H, DH = (2, 128, 128, 16, 64)
        DK = H * DH
        MIN_EXP = -30.0
        EPS = 0.0001
        B_, N_, _ = x.shape
        H_, d_half = omega.shape
        DH_ = 2 * d_half
        DKt = H_ * DH_

        def cproj(W):
            z = x @ W
            D = W.shape[1] // 2
            zc = jax.lax.complex(z[..., :D], z[..., D:])
            return zc.reshape(B_, N_, H_, DH_)
        q, k, v = (cproj(Wq), cproj(Wk), cproj(Wv))
        om = jnp.concatenate([omega, -omega], axis=-1)
        t = jnp.arange(N_, dtype=jnp.float32)
        ang = t[:, None, None] * om[None]
        phase = jax.lax.complex(jnp.cos(ang), jnp.sin(ang))
        qr = q * phase[None]
        kr = k * phase[None]
        mu = jax.nn.sigmoid(mu_raw) + EPS
        dt = jnp.abs(t[:, None] - t[None, :])
        E = jnp.exp(jnp.clip(-mu[:, None, None] * dt[None], MIN_EXP, 0.0))
        s = jnp.einsum('bihd,bjhd->bhij', qr, jnp.conj(kr)).real
        qn = (q.real ** 2 + q.imag ** 2).sum(-1).transpose(0, 2, 1)
        kn = (k.real ** 2 + k.imag ** 2).sum(-1).transpose(0, 2, 1)
        sigma_sq = jax.nn.softplus(sigma_raw)
        eta_sq = jax.nn.softplus(eta_raw)
        gamma_sq = jax.nn.softplus(gamma_raw)
        V = (sigma_sq / (2.0 * mu))[:, None, None] * (1.0 - E * E) + (eta_sq + gamma_sq)[:, None, None]
        maha = jnp.maximum(qn[..., None] + (E * E)[None] * kn[:, :, None, :] - 2.0 * E[None] * s, 0.0) / V[None]
        nu = jax.nn.softplus(nu_raw)
        coef = (-0.5 * tau * (nu + DH_))[None, :, None, None]
        logits = coef * jnp.log1p(maha / nu[None, :, None, None]) - 0.5 * DH_ * jnp.log(V)[None]
        causal = t[:, None] >= t[None, :]
        logits = jnp.where(causal[None, None], logits, -jnp.inf)
        A = jax.nn.softmax(logits, axis=-1)
        out = jnp.einsum('bhij,bjhd->bihd', A.astype(v.dtype), v)
        y = jnp.concatenate([out.real.reshape(B_, N_, DKt), out.imag.reshape(B_, N_, DKt)], axis=-1)
        return y @ Wo

    def _L0_ffn_ref(x, w_gate, w_in, w_out):
        import jax, jax.numpy as jnp
        import numpy as np
        D_MODEL = 128
        HIDDEN = 512
        NUM_EXPERTS = 8
        TOP_K = 2
        B, S, D = x.shape
        E = w_in.shape[0]
        xt = x.reshape(-1, D)
        logits = (xt @ w_gate.T).astype(jnp.float32)
        top_logits, top_idx = jax.lax.top_k(logits, TOP_K)
        top_gates = jax.nn.softmax(top_logits, axis=-1).astype(x.dtype)
        gates = (jax.nn.one_hot(top_idx, E, dtype=x.dtype) * top_gates[..., None]).sum(axis=1)
        y = jnp.zeros_like(xt)
        for e in range(E):
            h = xt @ w_in[e].T
            y = y + gates[:, e:e + 1] * (h @ w_out[e].T)
        return y.reshape(B, S, D)

    def _L1_attn_a_ref(hidden_states, Wq, Wk, Wv, Wo):
        import jax, jax.numpy as jnp
        import numpy as np
        H, KV, D = (8, 2, 32)
        RD = D // 4
        ROPE_THETA = 10000.0

        def _rope_cos_sin(seq_len, dtype):
            inv_freq = 1.0 / ROPE_THETA ** (jnp.arange(0, RD, 2, dtype=jnp.float32) / RD)
            pos = jnp.arange(seq_len, dtype=jnp.float32)
            freqs = pos[:, None] * inv_freq[None, :]
            emb = jnp.concatenate([freqs, freqs], axis=-1)
            return (jnp.cos(emb).astype(dtype), jnp.sin(emb).astype(dtype))

        def _apply_partial_rope(x, cos, sin):
            x_rot, x_pass = (x[..., :RD], x[..., RD:])
            half = RD // 2
            rot = jnp.concatenate([-x_rot[..., half:], x_rot[..., :half]], axis=-1)
            x_rot = x_rot * cos[None, None] + rot * sin[None, None]
            return jnp.concatenate([x_rot, x_pass], axis=-1)
        B, S, _ = hidden_states.shape
        G = H // KV
        qg = hidden_states @ Wq
        q, gate = (qg[..., :H * D], qg[..., H * D:])
        k = hidden_states @ Wk
        v = hidden_states @ Wv
        q = q.reshape(B, S, H, D).transpose(0, 2, 1, 3)
        k = k.reshape(B, S, KV, D).transpose(0, 2, 1, 3)
        v = v.reshape(B, S, KV, D).transpose(0, 2, 1, 3)
        cos, sin = _rope_cos_sin(S, q.dtype)
        q = _apply_partial_rope(q, cos, sin)
        k = _apply_partial_rope(k, cos, sin)
        qg4 = q.reshape(B, KV, G, S, D)
        scores = jnp.einsum('bkgsd,bktd->bkgst', qg4, k) / jnp.sqrt(jnp.asarray(D, q.dtype))
        attn = jax.nn.softmax(scores, axis=-1)
        out = jnp.einsum('bkgst,bktd->bkgsd', attn, v)
        out = out.reshape(B, H, S, D).transpose(0, 2, 1, 3).reshape(B, S, H * D)
        out = out * jax.nn.silu(gate)
        return out @ Wo

    def _L1_attn_b_ref(x, w_att_val, wv_w, wv_b, out_w, out_b):
        import jax, jax.numpy as jnp
        import numpy as np
        B, T, E, H = (2, 256, 128, 16)
        D = E // H
        b, t, e = x.shape
        h, d, _ = w_att_val.shape
        x_h = x.reshape(b, t, h, d).transpose(0, 2, 1, 3)
        xw = jnp.einsum('bhtd,hde->bhte', x_h, w_att_val)
        att = jnp.einsum('bhte,bhse->bhts', xw, x_h) / jnp.sqrt(jnp.asarray(d, x.dtype))
        att = jax.nn.softmax(att, axis=-1)
        vx = x @ wv_w.T + wv_b
        vx = vx.reshape(b, t, h, d).transpose(0, 2, 1, 3)
        o = jnp.einsum('bhts,bhsd->bhtd', att, vx)
        o = o.transpose(0, 2, 1, 3).reshape(b, t, e)
        return o @ out_w.T + out_b

    def _L1_ffn_ref(x, Wr, Wg, Wu, Wd):
        import jax, jax.numpy as jnp
        import numpy as np
        NUM_EXPERTS_TOTAL = 9
        TOP_K = 2
        B, S, H = x.shape
        E = NUM_EXPERTS_TOTAL
        T = B * S
        logits = jnp.einsum('bsh,he->bse', x, Wr)
        probs = jax.nn.softmax(logits, axis=-1)
        topk_w, topk_idx = jax.lax.top_k(probs, TOP_K)
        topk_w = topk_w / jnp.sum(topk_w, axis=-1, keepdims=True)
        xf = x.reshape(T, H)
        wf = topk_w.reshape(T, TOP_K)
        idxf = topk_idx.reshape(T, TOP_K)
        cw = jnp.zeros((T, E), dtype=x.dtype).at[jnp.arange(T)[:, None], idxf].add(wf)
        gate = jax.nn.silu(jnp.einsum('th,ehi->tei', xf, Wg))
        hidden = gate * jnp.einsum('th,ehi->tei', xf, Wu)
        out = jnp.einsum('tei,eih,te->th', hidden, Wd, cw)
        return out.reshape(B, S, H)
    x = L0_attn_a_x
    x = x + _L0_attn_a_ref(_layernorm(x, axis=-1), L0_attn_a_wq, L0_attn_a_bq, L0_attn_a_wk, L0_attn_a_bk, L0_attn_a_wv, L0_attn_a_bv, L0_attn_a_wp, L0_attn_a_bp)
    x = x + _L0_ffn_ref(_layernorm(x, axis=-1), L0_ffn_w_gate, L0_ffn_w_in, L0_ffn_w_out)
    x = x + _L0_attn_b_ref(_layernorm(x, axis=-1), L0_attn_b_Wq, L0_attn_b_Wk, L0_attn_b_Wv, L0_attn_b_Wo, L0_attn_b_omega, L0_attn_b_mu_raw, L0_attn_b_sigma_raw, L0_attn_b_eta_raw, L0_attn_b_gamma_raw, L0_attn_b_tau, L0_attn_b_nu_raw)
    x = x + _L0_ffn_ref(_layernorm(x, axis=-1), L0_ffn_w_gate, L0_ffn_w_in, L0_ffn_w_out)
    x = x + _L1_attn_a_ref(_layernorm(x, axis=-1), L1_attn_a_Wq, L1_attn_a_Wk, L1_attn_a_Wv, L1_attn_a_Wo)
    x = x + _L1_ffn_ref(_layernorm(x, axis=-1), L1_ffn_Wr, L1_ffn_Wg, L1_ffn_Wu, L1_ffn_Wd)
    x = x + _L1_attn_b_ref(_layernorm(x, axis=-1), L1_attn_b_w_att_val, L1_attn_b_wv_w, L1_attn_b_wv_b, L1_attn_b_out_w, L1_attn_b_out_b)
    x = x + _L1_ffn_ref(_layernorm(x, axis=-1), L1_ffn_Wr, L1_ffn_Wg, L1_ffn_Wu, L1_ffn_Wd)
    return x

_drawn_inputs = setup_inputs


def setup_inputs(seed=0):
    import zlib

    import numpy as np

    out = dict(_drawn_inputs(seed))
    spreads = {'L0_attn_b_eta_raw': (1.0, 0.6),
     'L0_attn_b_gamma_raw': (1.0, 0.6),
     'L0_attn_b_tau': (1.0, 0.2),
     'L0_attn_b_nu_raw': (4.0, 0.6),
     'L1_attn_b_wv_b': (0.0, 0.1),
     'L1_attn_b_out_b': (0.0, 0.1)}
    factors = {'L0_attn_a_bq': 2.873,
     'L0_attn_a_bk': 4.831,
     'L0_ffn_w_gate': 8.0,
     'L0_ffn_w_in': 8.0,
     'L0_ffn_w_out': 8.0,
     'L1_attn_a_Wq': 8.0,
     'L1_attn_a_Wk': 8.0,
     'L1_attn_a_Wv': 8.0,
     'L1_attn_a_Wo': 8.0,
     'L1_ffn_Wr': 5.334,
     'L1_ffn_Wg': 4.681,
     'L1_ffn_Wu': 4.647,
     'L1_ffn_Wd': 4.64}
    for name, (base, spread) in spreads.items():
        noise = np.random.default_rng([zlib.crc32(name.encode()), seed]).standard_normal(out[name].shape)
        drawn = base * np.exp(spread * noise) if base else spread * noise
        out[name] = jnp.asarray(drawn.astype(out[name].dtype))
    for name, factor in factors.items():
        out[name] = (out[name] * factor).astype(out[name].dtype)
    return out
```

```python
from contextlib import ExitStack

import numpy as np

import concourse.bass as bass
from concourse import mybir

F32 = mybir.dt.float32
BF16 = mybir.dt.bfloat16
I32 = mybir.dt.int32
U32 = mybir.dt.uint32
ALU = mybir.AluOpType
ACT = mybir.ActivationFunctionType
AX_X = mybir.AxisListType.X

P = 128
B, T, C = 8, 512, 128
TB = T // P
EPS = 1e-5
NORM_STEPS = 2
NEG = -1e30
PLAN = ["attn_rope", "ffn_linear", "attn_decay", "ffn_linear", "attn_gqa", "ffn_gated", "attn_bilinear", "ffn_gated"]


def ds(start, size):
    return bass.ds(start, size)


class Core:

    def __init__(self, nc, ctx, dram):
        self.nc, self.ctx, self.dram = nc, ctx, dram
        self.names = 0
        self.sems, self.open_sems = ExitStack(), []
        self.x = self.sbuf(ctx, "x", [P, B * TB, C])
        self.xT = self.sbuf(ctx, "xT", [P, B * T])
        self.ident = self.sbuf(ctx, "ident", [P, P])
        self.ident16 = self.sbuf(ctx, "ident16", [P, P], BF16)
        self.mask_ij = self.sbuf(ctx, "mask_ij", [P, P], BF16)
        self.mask_ji = self.sbuf(ctx, "mask_ji", [P, P], BF16)
        self.ones_row = self.sbuf(ctx, "ones_row", [1, P])
        self.minus_half = self.sbuf(ctx, "minus_half", [P, TB])
        self.stats = self.sbuf(ctx, "stats", [P, TB, 6])
        self.mean_var = self.sbuf(ctx, "mean_var", [P, TB, 2])
        self.var_eps = self.sbuf(ctx, "var_eps", [P, TB])
        self.pause = self.sbuf(ctx, "pause", [1, 1])
        self.rstd = self.sbuf(ctx, "rstd", [P, TB])
        self.xn = self.sbuf(ctx, "xn", [P, TB, C])

    def sbuf(self, ctx, name, shape, dtype=F32):
        self.names += 1
        return ctx.enter_context(self.nc.sbuf_tensor(f"{name}_{self.names}", shape, dtype))

    def psum(self, ctx, name, shape, dtype=F32):
        self.names += 1
        return ctx.enter_context(self.nc.psum_tensor(f"{name}_{self.names}", shape, dtype))

    def sem(self, name):
        self.names += 1
        made = self.sems.enter_context(self.nc.semaphore(f"{name}_{self.names}"))
        self.open_sems.append(made)
        return made

    def end_stage(self):
        numbers = sorted(s.num for s in self.open_sems)
        with self.nc.Block() as block:
            @block.sync
            def _(sp):
                first = numbers[0]
                for n, after in zip(numbers, numbers[1:] + [None]):
                    if after != n + 1:
                        sp.sem_clear(range(first, n + 1))
                        first = after
        self.sems.close()
        self.open_sems = []


class Count:

    def __init__(self, sem):
        self.sem, self.base, self.n = sem, 0, 0

    def at(self, base):
        self.base, self.n = base, 0

    def inc(self, instruction):
        instruction.then_inc(self.sem, 1)
        self.n += 1

    def settle(self, engine):
        engine.wait_ge(self.sem, self.base + self.n)



def norm_stats(nc, dve, core, chain, b):
    nc.vector.memset(core.pause[:, :], 0.0)
    for j in range(TB):
        last = nc.vector.bn_stats(core.stats[:, j, :], core.x[:, ds(b * TB + j, 1), :].rearrange("p a c -> p (a c)"))
    chain.inc(last)
    chain.settle(dve)
    nc.vector.memset(core.pause[:, :], 0.0)
    for j in range(TB):
        last = nc.vector.bn_aggr(core.mean_var[:, j, :], core.stats[:, j, :])
    chain.inc(last)
    chain.settle(dve)
    return nc.vector.tensor_scalar(core.var_eps[:, :], core.mean_var[:, :, 1], EPS, None, ALU.add)


def norm_rstd(nc, core):
    return nc.gpsimd.tensor_tensor(core.rstd[:, :], core.var_eps[:, :], core.minus_half[:, :], ALU.pow)


def norm_apply(nc, core, b):
    for j in range(TB):
        last = nc.vector.tensor_scalar(core.xn[:, j, :], core.x[:, ds(b * TB + j, 1), :].rearrange("p a c -> p (a c)"),
                                       core.mean_var[:, j, 0:1], core.rstd[:, j:j + 1], ALU.subtract, ALU.mult)
    return last


def norm_turn(nc, core, out):
    for j in range(TB):
        last = nc.tensor.transpose(out[:, j * P:(j + 1) * P], core.xn[:, j, :], core.ident[:, :])
    return last



def stage_load(core):
    nc, d = core.nc, core.dram
    loaded, const_loaded = core.sem("x_loaded"), core.sem("const_loaded")
    made = core.sem("constants_made")
    chain = Count(core.sem("load_chain"))
    var_ready, rstd_ready, xn_ready = core.sem("var_ready"), core.sem("rstd_ready"), core.sem("xn_ready")
    turned, taken = core.sem("turned"), core.sem("taken")
    x_tokens = d["x"].rearrange("b (j p) c -> p (b j) c", p=P)
    with ExitStack() as ctx:
        bank = core.psum(ctx, "turn_bank", [P, 2, T])
        block = ctx.enter_context(nc.Block())

        @block.sync
        def _(sp):
            sp.dma_start(core.ident[:, :], d["ident"]).then_inc(const_loaded, 16)
            sp.dma_start(core.ident16[:, :], d["ident16"]).then_inc(const_loaded, 16)
            sp.dma_start(core.mask_ij[:, :], d["mask_ij"]).then_inc(const_loaded, 16)
            sp.dma_start(core.mask_ji[:, :], d["mask_ji"]).then_inc(const_loaded, 16)
            sp.dma_start(core.x[:, :, :], x_tokens).then_inc(loaded, 16)

        @block.gpsimd
        def _(pool):
            nc.gpsimd.memset(core.minus_half[:, :], -0.5).then_inc(made, 1)
            nc.gpsimd.memset(core.ones_row[:, :], 1.0).then_inc(made, 1)
            pool.wait_ge(made, 2)
            with pool.Fori(0, B) as b:
                pool.wait_ge(var_ready, b + 1)
                norm_rstd(nc, core).then_inc(rstd_ready, 1)

        @block.vector
        def _(dve):
            dve.wait_ge(loaded, 16)
            with dve.Fori(0, B) as b:
                chain.at(b * NORM_STEPS)
                norm_stats(nc, dve, core, chain, b).then_inc(var_ready, 1)
                dve.wait_ge(rstd_ready, b + 1)
                dve.wait_ge(turned, b + 1)
                norm_apply(nc, core, b).then_inc(xn_ready, 1)

        @block.tensor
        def _(pe):
            pe.sem_inc(turned, 1)
            pe.wait_ge(const_loaded, 64)
            with pe.Fori(0, B // 2) as i:
                for u in range(2):
                    b = i * 2 + u
                    pe.wait_ge(xn_ready, b + 1)
                    pe.wait_ge(taken, b + 1)
                    norm_turn(nc, core, bank[:, u, :]).then_inc(turned, 1)

        @block.scalar
        def _(act):
            act.sem_inc(taken, 1)
            with act.Fori(0, B // 2) as i:
                for u in range(2):
                    b = i * 2 + u
                    act.wait_ge(turned, b + 2)
                    nc.scalar.copy(core.xT[:, ds(b * T, T)], bank[:, u, :]).then_inc(taken, 1)


def stage_store(core):
    nc = core.nc
    stored = core.sem("x_stored")
    with nc.Block() as block:
        @block.sync
        def _(sp):
            sp.dma_start(core.dram["out"].rearrange("b (j p) c -> p (b j) c", p=P), core.x[:, :, :]).then_inc(stored, 16)
            sp.wait_ge(stored, 16)



class Attention:

    def __init__(self, heads, dim, kv_heads, causal, rope, bias, gate):
        self.heads, self.dim, self.kv_heads = heads, dim, kv_heads
        self.causal, self.rope, self.bias, self.gate = causal, rope, bias, gate
        self.groups = 4
        self.per_group = heads // self.groups
        self.stride = P // self.per_group
        self.width = heads * dim
        self.halves = self.width // P
        self.kgroups = self.groups if kv_heads == heads else kv_heads
        self.scale = float(dim) ** -0.5
        pairs = self.per_group // 2
        cuts = [[0], [1, 3], [2]] if causal else [[0], [1], [2], [3]]
        self.ops = [(p, cut) for p in range(pairs) for cut in cuts]
        self.units = [(j, r) for j in range(TB) for r in range(self.per_group)]

    def kgroup(self, g):
        return g if self.kgroups == self.groups else g * self.kgroups // self.groups

    def vhead(self, h):
        return h * self.kv_heads // self.heads

    def segments(self, cut):
        at, out = 0, []
        for j in cut:
            first = j if self.causal else 0
            out.append((j, first, at))
            at += (TB - first) * P
        return out, at

    def prep(self):
        items = []
        for g in range(self.groups):
            if self.kgroups == self.groups or g % 2 == 0:
                items += [("k", self.kgroup(g), s) for s in range(1 + self.rope)]
            items += [("q", g, s) for s in range(1 + self.rope)]
        items.append(("v", 0, 0))
        if self.gate:
            items += [("gate", 0, 0), ("gate", 1, 0)]
        return items

    def qk_needed(self, g):
        n = 0
        for what, at, swapped in self.prep():
            if what in "qk" and swapped == self.rope:
                n += 1
            if (what, at, swapped) == ("q", g, int(self.rope)):
                return n

    def qk_tiles(self):
        return self.groups + self.kgroups

    def batch_of(self, item, b, g):
        if item[0] == "turn_out" and g > 0:
            return b
        return b - 1 if item in self.end() else b + 1

    def end(self):
        return [("turn_out", self.groups - 1, 0)] + [("turn_y", h, 0) for h in range(self.halves)] + [("project", 0, 0), ("norm", 0, 0)]

    def plan(self, epilogue, prep):
        n_ops = len(self.ops)
        slots = [[[] for _ in range(n_ops)] for _ in range(self.groups)]
        if epilogue:
            for n, item in enumerate([("turn_y", h, 0) for h in range(self.halves)] + [("project", 0, 0)]):
                slots[0][min(2 + n, n_ops - 1)].append(item)
            slots[1][n_ops // 2].append(("norm", 0, 0))
        if prep:
            items = self.prep()
            places = [(g, k) for g in range(3) for k in range(n_ops) if (g, k) >= (0, 1)]
            for n, item in enumerate(items):
                g, k = places[n * len(places) // len(items)]
                slots[g][k].append(item)
        for g in range(0 if epilogue else 1, self.groups):
            slots[g][1].insert(0, ("turn_out", (g - 1) % self.groups, 0))
        return slots


def stage_attention(core, cfg, w):
    nc = core.nc
    G, HG, D, NOPS, NUNITS = cfg.groups, cfg.per_group, cfg.dim, len(cfg.ops), len(cfg.units)
    KG, KV, ST = cfg.kgroups, cfg.kv_heads, cfg.stride
    SLOTS = 4
    TILES = cfg.qk_tiles()
    PREP = cfg.prep()
    ENDS = cfg.halves + 3
    MIDDLE = len(PREP) + ENDS + G + G - 1
    BEFORE = len(PREP) + 1

    names = ("weights_loaded", "cleared", "xcur_even", "xcur_odd", "bias_ready", "bank_full", "bank_free", "qk_ready",
             "max_full", "max_free", "scores_full", "exp_done", "pv_done", "out_copied", "recip_ready", "gated",
             "var_ready", "rstd_ready", "xn_ready", "gate_sum_ready", "gate_recip_ready", "gate_ready")
    (weights_loaded, cleared, xcur_even, xcur_odd, bias_ready, bank_full, bank_free, qk_ready,
     max_full, max_free, scores_full, exp_done, pv_done, out_copied, recip_ready, gated,
     var_ready, rstd_ready, xn_ready, gate_sum_ready, gate_recip_ready, gate_ready) = (core.sem(n) for n in names)
    xcur_ready = [xcur_even, xcur_odd]
    chain = Count(core.sem("end_chain"))

    def start(b):
        return BEFORE if isinstance(b, int) and b == 0 else BEFORE + MIDDLE - ENDS + (b - 1) * MIDDLE

    LAST = start(B - 1) + MIDDLE - len(PREP) - 1

    def bodies(eng, emit):
        emit(0, 0, False, True)
        with eng.Fori(0, (B - 2) // 2) as i:
            emit(i * 2 + 1, 1, True, True)
            emit(i * 2 + 2, 0, True, True)
        emit(B - 1, 1, True, False)

    def units_at(k):
        return range(k * NUNITS // NOPS, (k + 1) * NUNITS // NOPS)

    with ExitStack() as ctx:
        def sb(name, shape, dtype=F32):
            return core.sbuf(ctx, name, shape, dtype)

        wq, wk = sb("wq", [P, 1 + cfg.rope, G, P]), sb("wk", [P, 1 + cfg.rope, KG, P])
        wv, wo = sb("wv", [P, KV * D]), sb("wo", [P, cfg.halves, C])
        kaug = sb("kaug", [P, 1])
        if cfg.rope:
            cos, sin = sb("cos", [P, T]), sb("sin", [P, T])
            parts = sb("parts", [P, 2, 2, T])
            qbias, kbias = sb("qbias", [P, 2, G]), sb("kbias", [P, 2, G])
        if cfg.bias:
            vbias, obias = sb("vbias", [1, C]), sb("obias", [1, C])
        if cfg.gate:
            wg = sb("wg", [P, cfg.width])
            gate, gate_sig = sb("gate", [P, 2, TB, cfg.width]), sb("gate_sig", [P, TB, cfg.width])
        xcur = sb("xcur", [P, 2, T])
        q, k = sb("q", [P, 2, G, T]), sb("k", [P, 2, KG, T])
        v = sb("v", [P, 2, TB, KV, ST])
        v_cols = v[:].rearrange("p b j h d -> p (b j h) d")
        out_T = sb("out_T", [P, T])
        maxima = sb("maxima", [P, TB, P])
        probs = sb("probs", [P, SLOTS, 2, T])
        recip = sb("recip", [P, TB, HG])
        y, yT = sb("y", [P, TB, cfg.width]), sb("yT", [P, cfg.halves, T])

        max_bank = core.psum(ctx, "max_bank", [P, 2, T])
        score_bank = core.psum(ctx, "score_bank", [P, 2, 2, T])
        out_bank = core.psum(ctx, "out_bank", [P, T])
        spare = core.psum(ctx, "spare_bank", [P, T])
        outs = spare[:, :].rearrange("p (j r d) -> p j r d", j=TB, r=HG)

        loads = [(kaug[:, :], w["kaug"]), (wv[:, :], w["wv"]), (wo[:, :, :], w["wo"].rearrange("(h p) c -> p h c", p=P))]
        for sw in range(1 + cfg.rope):
            tail = "_swap" if sw else ""
            for r in range(HG):
                rows = slice(ST * r, ST * r + D)
                loads.append((wq[:, sw, :, rows], w["wq" + tail].rearrange("c (g r d) -> r c g d", g=G, r=HG)[r]))
                if KG == G:
                    loads.append((wk[:, sw, :, rows], w["wk" + tail].rearrange("c (g r d) -> r c g d", g=G, r=HG)[r]))
                else:
                    loads.append((wk[:, sw, :, rows], w["wk" + tail].rearrange("c (g d) -> c g d", d=D)))
                if cfg.rope and cfg.bias:
                    loads.append((qbias[rows, sw, :], w["bq" + tail][r]))
                    loads.append((kbias[rows, sw, :], w["bk" + tail][r]))
        if cfg.rope:
            loads += [(cos[:, :], w["cos"]), (sin[:, :], w["sin"])]
        if cfg.bias:
            loads += [(vbias[:, :], w["bv"].rearrange("(a c) -> a c", a=1)), (obias[:, :], w["bo"].rearrange("(a c) -> a c", a=1))]
        if cfg.gate:
            loads.append((wg[:, :], w["wg"]))
        LOADED = 16 * len(loads)
        clears = [(wq[:], 0.0), (wk[:], 0.0), (maxima[:], 0.0), (v_cols[:, :, D:D + 1], 1.0), (v_cols[:, :, D + 1:ST], 0.0)]
        clears += [(qbias[:], 0.0), (kbias[:], 0.0)] if cfg.rope else []

        block = ctx.enter_context(nc.Block())

        @block.sync
        def _(sp):
            sp.wait_ge(cleared, len(clears))
            for b in (0, 1):
                sp.dma_start(xcur[:, b, :], core.xT[:, b * T:(b + 1) * T]).then_inc(xcur_ready[b], 16)
            for dst, src in loads:
                sp.dma_start(dst, src).then_inc(weights_loaded, 16)

            def refill(b, place):
                sp.wait_ge(bank_full, start(b))
                sp.dma_start(xcur[:, place, :], core.xT[:, ds((b + 2) * T, T)]).then_inc(xcur_ready[place], 16)

            refill(0, 0)
            with sp.Fori(0, (B - 4) // 2) as i:
                refill(i * 2 + 1, 1)
                refill(i * 2 + 2, 0)
            refill(B - 3, 1)

        @block.tensor
        def _(pe):
            def bank_item(index, b, item, place):
                what, at, swapped = item
                if not (isinstance(index, int) and index == 0):
                    pe.wait_ge(bank_free, index)
                if item == PREP[0]:
                    pe.wait_ge(xcur_ready[place], (b - place) * 8 + 16)
                if what in "qk":
                    weights = wq if what == "q" else wk
                    last = nc.tensor.matmul(spare[:, :], weights[:, swapped, at, :], xcur[:, place, :], start=True, stop=True)
                elif what == "v":
                    n = KV * D
                    for j in range(TB):
                        out = spare[:, j * n:(j + 1) * n]
                        last = nc.tensor.matmul(out, xcur[:, place, j * P:(j + 1) * P], wv[:, :], start=True, stop=not cfg.bias)
                        if cfg.bias:
                            last = nc.tensor.matmul(out, core.ones_row[:, :], vbias[:, :], start=False, stop=True)
                elif what == "gate":
                    n = cfg.width
                    for j in range(2):
                        last = nc.tensor.matmul(spare[:, j * n:(j + 1) * n], xcur[:, place, (2 * at + j) * P:(2 * at + j + 1) * P],
                                                wg[:, :], start=True, stop=True)
                elif what == "turn_out":
                    pe.wait_ge(out_copied, b * G + at + 1)
                    for j in range(TB):
                        last = nc.tensor.transpose(spare[:, j * P:(j + 1) * P], out_T[:, j * P:(j + 1) * P], core.ident[:, :])
                elif what == "turn_y":
                    if at == 0 and cfg.gate:
                        pe.wait_ge(gated, b + 1)
                    for j in range(TB):
                        last = nc.tensor.transpose(spare[:, j * P:(j + 1) * P], y[:, j, at * P:(at + 1) * P], core.ident[:, :])
                elif what == "project":
                    for j in range(TB):
                        out = spare[:, j * P:(j + 1) * P]
                        for h in range(cfg.halves):
                            last = nc.tensor.matmul(out, yT[:, h, j * P:(j + 1) * P], wo[:, h, :], start=(h == 0),
                                                    stop=(h == cfg.halves - 1 and not cfg.bias))
                        if cfg.bias:
                            last = nc.tensor.matmul(out, core.ones_row[:, :], obias[:, :], start=False, stop=True)
                elif what == "norm":
                    pe.wait_ge(xn_ready, b + 1)
                    last = norm_turn(nc, core, spare)
                last.then_inc(bank_full, 1)

            def unit(n, g, place, u):
                j, r = cfg.units[u]
                rows = slice(ST * r, ST * (r + 1))
                if not (isinstance(n, int) and n == 0 and u < 2):
                    pe.wait_ge(max_free, n * NUNITS + u - 1)
                cols = (j + 1) * P if cfg.causal else T
                bank = max_bank[:, u % 2, :]
                last = nc.tensor.matmul(bank[:, 0:cols], q[rows, place, g, j * P:(j + 1) * P],
                                        k[rows, place, cfg.kgroup(g), 0:cols], start=True, stop=not cfg.causal)
                if cfg.causal:
                    last = nc.tensor.matmul(bank[:, j * P:(j + 1) * P], core.ident16[:, :], core.mask_ij[:, :],
                                            start=False, stop=True)
                last.then_inc(max_full, 1)

            def turn_maxima(index, n):
                pe.wait_ge(max_free, (n + 1) * NUNITS)
                pe.wait_ge(bank_free, index)
                for j in range(TB):
                    last = nc.tensor.transpose(spare[:, j * P:(j + 1) * P], maxima[:, j, :], core.ident[:, :])
                last.then_inc(bank_full, 1)

            def scores(n, g, place, o, turned):
                pair, cut = cfg.ops[o]
                if o == 0:
                    pe.wait_ge(bank_free, turned)
                if not (isinstance(n, int) and n == 0 and o < 2):
                    pe.wait_ge(exp_done, n * NOPS + o - 1)
                for e in range(2):
                    r = 2 * pair + e
                    rows = slice(ST * r, ST * (r + 1))
                    for j, first, at in cfg.segments(cut)[0]:
                        width = T - first * P
                        bank = score_bank[:, o % 2, e, at:at + width]
                        last = nc.tensor.matmul(bank, k[rows, place, cfg.kgroup(g), j * P:(j + 1) * P],
                                                q[rows, place, g, first * P:T], start=True, stop=not cfg.causal)
                        if cfg.causal:
                            last = nc.tensor.matmul(bank[:, 0:P], core.ident16[:, :], core.mask_ji[:, :],
                                                    start=False, stop=True)
                last.then_inc(scores_full, 1)

            def values(n, g, place, o):
                pair, cut = cfg.ops[o]
                pe.wait_ge(exp_done, n * NOPS + o + 1)
                if o == 0 and not (isinstance(n, int) and n == 0):
                    pe.wait_ge(out_copied, n)
                slot = (g * NOPS + o) % SLOTS
                for e in range(2):
                    r = 2 * pair + e
                    for j, first, at in cfg.segments(cut)[0]:
                        last = nc.tensor.matmul(out_bank[ST * r:ST * (r + 1), first * P:T], v[:, place, j, cfg.vhead(g * HG + r), :],
                                                probs[:, slot, e, at:at + T - first * P],
                                                start=(j == 0), stop=(j == TB - 1 or cut == cfg.ops[-1][1] and j == cut[-1]),
                                                skip_group_check=True)
                last.then_inc(pv_done, 1)

            def body(b, place, epilogue, prep):
                plan = cfg.plan(epilogue, prep)
                index = 0
                for g in range(G):
                    n = b * G + g
                    more = prep or g < G - 1
                    g1, place1, b1 = (g + 1, place, b) if g < G - 1 else (0, 1 - place, b + 1)
                    for o in range(NOPS):
                        scores(n, g, place, o, start(b) + index)
                        if more:
                            if o == 0 and cfg.rope:
                                pe.wait_ge(qk_ready, b1 * TILES + cfg.qk_needed(g1))
                            for u in units_at(o):
                                unit(n + 1, g1, place1, u)
                        for item in plan[g][o]:
                            bank_item(start(b) + index, cfg.batch_of(item, b, g), item, 1 - place)
                            index += 1
                        if o > 0:
                            values(n, g, place, o - 1)
                        elif g > 0:
                            values(n - 1, g - 1, place, NOPS - 1)
                        elif epilogue:
                            values(n - 1, G - 1, 1 - place, NOPS - 1)
                    if more:
                        turn_maxima(start(b) + index, n + 1)
                        index += 1

            pe.wait_ge(weights_loaded, LOADED)
            for index, item in enumerate(PREP):
                bank_item(index, 0, item, 0)
            if cfg.rope:
                pe.wait_ge(qk_ready, cfg.qk_needed(0))
            pe.wait_ge(bank_free, len(PREP))
            for u in range(NUNITS):
                unit(0, 0, 0, u)
            turn_maxima(len(PREP), 0)
            bodies(pe, body)
            values(B * G - 1, G - 1, 1, NOPS - 1)
            for n, item in enumerate(cfg.end()):
                bank_item(LAST + n, B - 1, item, 1)

        @block.scalar
        def _(act):
            def bank_item(index, b, item, place):
                what, at, swapped = item
                if what in ("turn_y", "norm", "v", "gate") or (what in "qk" and not cfg.rope):
                    act.wait_ge(bank_full, index + 1)
                if what == "turn_y":
                    nc.scalar.copy(yT[:, at, :], spare[:, :]).then_inc(bank_free, 1)
                elif what == "norm":
                    nc.scalar.copy(core.xT[:, ds(b * T, T)], spare[:, :]).then_inc(bank_free, 1)
                elif what == "v":
                    nc.scalar.copy(v[:, place, :, :, 0:D], spare[:, 0:TB * KV * D].rearrange("p (j h d) -> p j h d", j=TB, h=KV))\
                      .then_inc(bank_free, 1)
                elif what == "gate":
                    raw = spare[:, :].rearrange("p (j c) -> p j c", j=2)
                    nc.scalar.activation(gate_sig[:, 2 * at:2 * at + 2, :], raw, ACT.Exp, scale=-1.0)
                    nc.scalar.copy(gate[:, place, 2 * at:2 * at + 2, :], raw).then_inc(bank_free, 1)
                elif what == "q" and not cfg.rope:
                    nc.scalar.copy(q[:, place, at, :], spare[:, :]).then_inc(bank_free, 1)
                elif what == "k" and not cfg.rope:
                    nc.scalar.activation(k[:, place, at, :], spare[:, :], ACT.Identity, bias=kaug[:, 0:1]).then_inc(bank_free, 1)

            def exponentials(n, g, o):
                width = cfg.segments(cfg.ops[o][1])[1]
                slot = (g * NOPS + o) % SLOTS
                act.wait_ge(scores_full, n * NOPS + o + 1)
                if not (isinstance(n, int) and n * NOPS + o < SLOTS):
                    act.wait_ge(pv_done, n * NOPS + o + 1 - SLOTS)
                nc.scalar.activation(probs[:, slot, :, 0:width], score_bank[:, o % 2, :, 0:width], ACT.Exp,
                                     scale=cfg.scale).then_inc(exp_done, 1)

            def copy_outputs(n):
                act.wait_ge(pv_done, (n + 1) * NOPS)
                if not (isinstance(n, int) and n == 0):
                    act.wait_ge(recip_ready, n)
                nc.scalar.copy(out_T[:, :], out_bank[:, :]).then_inc(out_copied, 1)

            def body(b, place, epilogue, prep):
                plan = cfg.plan(epilogue, prep)
                index = 0
                for g in range(G):
                    for o in range(NOPS):
                        exponentials(b * G + g, g, o)
                        if o == 0 and (g > 0 or epilogue):
                            copy_outputs(b * G + g - 1)
                        for item in plan[g][o]:
                            bank_item(start(b) + index, cfg.batch_of(item, b, g), item, 1 - place)
                            index += 1
                    index += 1

            act.wait_ge(weights_loaded, LOADED)
            for index, item in enumerate(PREP):
                bank_item(index, 0, item, 0)
            bodies(act, body)
            copy_outputs(B * G - 1)
            for n, item in enumerate(cfg.end()):
                bank_item(LAST + n, B - 1, item, 1)

        @block.gpsimd
        def _(pool):
            for tile, value in clears:
                nc.gpsimd.memset(tile, value).then_inc(cleared, 1)

            def bank_item(index, b, item, place, tile):
                what, at, swapped = item
                if what in "qk" and swapped:
                    pool.wait_ge(bank_free, index + 1)
                    out = q if what == "q" else k
                    nc.gpsimd.tensor_tensor(out[:, place, at, :], parts[:, tile % 2, 0, :], parts[:, tile % 2, 1, :],
                                            ALU.add).then_inc(qk_ready, 1)
                    return 1
                if what == "gate" and at == 1:
                    pool.wait_ge(gate_recip_ready, b + 1)
                    nc.gpsimd.tensor_tensor(gate[:, place], gate[:, place], gate_sig[:, :, :], ALU.mult).then_inc(gate_ready, 1)
                if what == "turn_out" and at == G - 1 and cfg.gate:
                    pool.wait_ge(bank_free, index + 1)
                    pool.wait_ge(gate_ready, b + 1)
                    nc.gpsimd.tensor_tensor(y[:, :, :], y[:, :, :], gate[:, place], ALU.mult).then_inc(gated, 1)
                if what == "project":
                    pool.wait_ge(var_ready, b + 1)
                    norm_rstd(nc, core).then_inc(rstd_ready, 1)
                return 0

            def body(b, place, epilogue, prep):
                plan = cfg.plan(epilogue, prep)
                index = tile = 0
                for g in range(G):
                    for o in range(NOPS):
                        for item in plan[g][o]:
                            tile += bank_item(start(b) + index, cfg.batch_of(item, b, g), item, 1 - place, tile)
                            index += 1
                    index += 1

            tile = 0
            for index, item in enumerate(PREP):
                tile += bank_item(index, 0, item, 0, tile)
            bodies(pool, body)
            for n, item in enumerate(cfg.end()):
                bank_item(LAST + n, B - 1, item, 1, 0)

        @block.vector
        def _(dve):
            def bank_item(index, b, item, place, tile):
                what, at, swapped = item
                if what in "qk" and cfg.rope:
                    dve.wait_ge(bank_full, index + 1)
                    if not swapped and not (isinstance(b, int) and b == 0 and tile < 2):
                        dve.wait_ge(qk_ready, b * TILES + tile - 1)
                    bias = (qbias if what == "q" else kbias)[:, swapped, at:at + 1]
                    nc.vector.scalar_tensor_tensor(parts[:, tile % 2, swapped, :], spare[:, :], bias,
                                                   (sin if swapped else cos)[:, :], ALU.add, ALU.mult).then_inc(bank_free, 1)
                    return swapped
                if what == "gate" and at == 1:
                    dve.wait_ge(bank_free, index + 1)
                    nc.vector.tensor_scalar(gate_sig[:, :, :], gate_sig[:, :, :], 1.0, None, ALU.add).then_inc(gate_sum_ready, 1)
                    dve.wait_ge(gate_sum_ready, b + 1)
                    nc.vector.reciprocal(gate_sig[:, :, :], gate_sig[:, :, :]).then_inc(gate_recip_ready, 1)
                if what == "turn_out":
                    take_outputs(index, b * G + at, at)
                if what == "project":
                    dve.wait_ge(bank_full, index + 1)
                    tokens = core.x[:, ds(b * TB, TB), :]
                    nc.vector.tensor_tensor(tokens, spare[:, :].rearrange("p (j c) -> p j c", j=TB), tokens, ALU.add)\
                      .then_inc(bank_free, 1)
                    dve.wait_ge(bank_free, index + 1)
                    chain.at(b * NORM_STEPS)
                    norm_stats(nc, dve, core, chain, b).then_inc(var_ready, 1)
                return 0

            def reduce(n, u):
                j, r = cfg.units[u]
                dve.wait_ge(max_full, n * NUNITS + u + 1)
                cols = (j + 1) * P if cfg.causal else T
                at = ST * r + D
                nc.vector.tensor_reduce(maxima[:, j, at:at + 1], max_bank[:, u % 2, 0:cols], AX_X, ALU.max).then_inc(max_free, 1)

            def add_maxima(index, g, place):
                dve.wait_ge(bank_full, index + 1)
                nc.vector.tensor_tensor(q[:, place, g, :], q[:, place, g, :], spare[:, :], ALU.add).then_inc(bank_free, 1)

            def take_outputs(index, n, g):
                dve.wait_ge(bank_full, index + 1)
                nc.vector.reciprocal(recip[:, :, :], outs[:, :, :, D]).then_inc(recip_ready, 1)
                dve.wait_ge(recip_ready, n + 1)
                mine = y[:, :, g * HG * D:(g + 1) * HG * D].rearrange("p j (r d) -> p j r d", r=HG)
                nc.vector.tensor_tensor(mine, outs[:, :, :, 0:D], recip[:, :, :].unsqueeze(3).to_broadcast([P, TB, HG, D]),
                                        ALU.mult).then_inc(bank_free, 1)

            def apply_norm(b):
                dve.wait_ge(rstd_ready, b + 1)
                norm_apply(nc, core, b).then_inc(xn_ready, 1)

            def body(b, place, epilogue, prep):
                plan = cfg.plan(epilogue, prep)
                index = tile = 0
                for g in range(G):
                    n = b * G + g
                    more = prep or g < G - 1
                    g1, place1 = (g + 1, place) if g < G - 1 else (0, 1 - place)
                    for o in range(NOPS):
                        if more:
                            for u in units_at(o):
                                reduce(n + 1, u)
                        if epilogue and g == 1 and o == 0:
                            apply_norm(b - 1)
                        for item in plan[g][o]:
                            tile += bank_item(start(b) + index, cfg.batch_of(item, b, g), item, 1 - place, tile)
                            index += 1
                    if more:
                        add_maxima(start(b) + index, g1, place1)
                        index += 1

            dve.wait_ge(weights_loaded, LOADED)
            if cfg.rope:
                for g in range(KG):
                    last = nc.vector.tensor_tensor(kbias[:, 0, g:g + 1], kbias[:, 0, g:g + 1], kaug[:, :], ALU.add)
                last.then_inc(bias_ready, 1)
                dve.wait_ge(bias_ready, 1)
            tile = 0
            for index, item in enumerate(PREP):
                tile += bank_item(index, 0, item, 0, tile)
            for u in range(NUNITS):
                reduce(0, u)
            add_maxima(len(PREP), 0, 0)
            bodies(dve, body)
            for n, item in enumerate(cfg.end()):
                bank_item(LAST + n, B - 1, item, 1, 0)
            apply_norm(B - 1)



def choose(nc, dve, chain, left, scratch, order, best, top, onehot):
    shape = [P, B * TB, left.shape[2]]
    chain.inc(nc.vector.tensor_reduce(top, left, AX_X, ALU.max))
    chain.settle(dve)
    chain.inc(nc.vector.tensor_tensor(scratch, left, top.unsqueeze(2).to_broadcast(shape), ALU.is_equal))
    chain.settle(dve)
    chain.inc(nc.vector.tensor_tensor(scratch, scratch, order.unsqueeze(1).to_broadcast(shape), ALU.mult))
    chain.settle(dve)
    chain.inc(nc.vector.tensor_reduce(best, scratch, AX_X, ALU.max))
    chain.settle(dve)
    chain.inc(nc.vector.tensor_tensor(onehot, scratch, best.unsqueeze(2).to_broadcast(shape), ALU.is_equal))
    chain.settle(dve)


def stage_ffn(core, w, experts, hidden):
    nc = core.nc
    E = experts
    gated = hidden is not None
    CHUNKS = -(-hidden // P) if gated else 0
    H = [min(P, hidden - c * P) for c in range(CHUNKS)] if gated else []
    names = ("weights_loaded", "xcur_even", "xcur_odd", "order_ready", "logits_full", "diff_ready", "exp_ready",
             "up_full", "silu_done", "hidden_done", "down_full", "combined", "var_ready", "rstd_ready", "xn_ready",
             "turned", "taken", "mixed_full", "mixed_taken")
    (weights_loaded, xcur_even, xcur_odd, order_ready, logits_full, diff_ready, exp_ready, up_full, silu_done,
     hidden_done, down_full, combined, var_ready, rstd_ready, xn_ready, turned, taken, mixed_full,
     mixed_taken) = (core.sem(n) for n in names)
    xcur_ready = [xcur_even, xcur_odd]
    route_chain, chain = Count(core.sem("route_chain")), Count(core.sem("ffn_chain"))

    with ExitStack() as ctx:
        def sb(name, shape, dtype=F32):
            return core.sbuf(ctx, name, shape, dtype)

        N = B * TB
        router = sb("router", [P, E])
        logits, scratch = sb("logits", [P, N, E]), sb("scratch", [P, N, E])
        first, second, gates = sb("first", [P, N, E]), sb("second", [P, N, E]), sb("gates", [P, N, E])
        top, best = sb("top", [P, 2, N]), sb("best", [P, N])
        share, total = sb("share", [P, 2, N]), sb("total", [P, N])
        order = sb("order", [P, E])
        xcur = sb("xcur", [P, 2, T])
        loads = [(router[:, :], w["router"])]
        if gated:
            wg, wu, wd = sb("wg", [P, E, hidden]), sb("wu", [P, E, hidden]), sb("wd", [P, E, CHUNKS, C])
            silu, hid = sb("silu", [P, 2, T]), sb("hidden", [P, 2, CHUNKS, T])
            gate_bank, up_bank = core.psum(ctx, "gate_bank", [P, 2, T]), core.psum(ctx, "up_bank", [P, 2, T])
            loads += [(wg[:, :, :], w["wg"].rearrange("e c i -> c e i")), (wu[:, :, :], w["wu"].rearrange("e c i -> c e i"))]
            loads += [(wd[0:H[c], :, c, :], w["wd"][:, c * P:c * P + H[c], :].rearrange("e i c -> i e c")) for c in range(CHUNKS)]
        else:
            F = w["w_in"].shape[1] // P
            w_in, w_out, both = sb("w_in", [P, E, F, C]), sb("w_out", [P, E, F, C]), sb("w_both", [P, E, C])
            mixed_bank = core.psum(ctx, "mixed_bank", [P, 2, T])
            loads += [(w_in[:, :, :, :], w["w_in"].rearrange("e (f p) c -> p e f c", p=P)),
                      (w_out[:, :, :, :], w["w_out"].rearrange("e (f p) c -> p e f c", p=P))]
        down_bank = core.psum(ctx, "down_bank", [P, 2, T])
        logits_bank, norm_bank = core.psum(ctx, "logits_bank", [P, T]), core.psum(ctx, "norm_bank", [P, T])
        logits_view = logits_bank[:, 0:N * E].rearrange("p (n e) -> p n e", e=E)

        def bodies(eng, emit):
            emit(0, 0, True)
            with eng.Fori(0, (B - 2) // 2) as i:
                emit(i * 2 + 1, 1, False)
                emit(i * 2 + 2, 0, False)
            emit(B - 1, 1, False)

        def e_parity(place, e):
            return (place * E + e) % 2

        def chunk_parity(place, m):
            return (place * E * CHUNKS + m) % 2

        block = ctx.enter_context(nc.Block())

        @block.sync
        def _(sp):
            for dst, src in loads:
                sp.dma_start(dst, src).then_inc(weights_loaded, 16)
            for b in (0, 1):
                sp.dma_start(xcur[:, b, :], core.xT[:, b * T:(b + 1) * T]).then_inc(xcur_ready[b], 16)
            with sp.Fori(0, (B - 2) // 2) as i:
                for u in range(2):
                    sp.wait_ge(down_full, (i * 2 + u + 1) * E)
                    sp.dma_start(xcur[:, u, :], core.xT[:, ds((i * 2 + u + 2) * T, T)]).then_inc(xcur_ready[u], 16)

        @block.gpsimd
        def _(pool):
            nc.gpsimd.iota(order[:, :], pattern=[[-1, E]], base=E, channel_multiplier=0,
                           allow_small_or_imprecise_dtypes=True).then_inc(order_ready, 1)
            with pool.Fori(0, B) as b:
                pool.wait_ge(var_ready, b + 1)
                norm_rstd(nc, core).then_inc(rstd_ready, 1)

        @block.tensor
        def _(pe):
            def down(b, place, e):
                if not (isinstance(b, int) and b == 0 and e < 2):
                    pe.wait_ge(combined, b * E + e - 1)
                if gated:
                    pe.wait_ge(hidden_done, (b * E + e + 1) * CHUNKS)
                for j in range(TB):
                    out = down_bank[:, e_parity(place, e), j * C:(j + 1) * C]
                    if gated:
                        for c in range(CHUNKS):
                            last = nc.tensor.matmul(out, hid[0:H[c], e_parity(place, e), c, j * P:(j + 1) * P],
                                                    wd[0:H[c], e, c, :], start=(c == 0), stop=(c == CHUNKS - 1))
                    else:
                        last = nc.tensor.matmul(out, xcur[:, place, j * P:(j + 1) * P], both[:, e, :], start=True, stop=True)
                last.then_inc(down_full, 1)

            def up(b, place, e):
                for c in range(CHUNKS):
                    m = e * CHUNKS + c
                    if not (isinstance(b, int) and b == 0 and m < 2):
                        pe.wait_ge(hidden_done, b * E * CHUNKS + m - 1)
                    cols = slice(c * P, c * P + H[c])
                    bank = chunk_parity(place, m)
                    nc.tensor.matmul(gate_bank[0:H[c], bank, :], wg[:, e, cols], xcur[:, place, :], start=True, stop=True)
                    nc.tensor.matmul(up_bank[0:H[c], bank, :], wu[:, e, cols], xcur[:, place, :],
                                     start=True, stop=True).then_inc(up_full, 1)

            def turn(b):
                pe.wait_ge(xn_ready, b + 1)
                if not (isinstance(b, int) and b == 0):
                    pe.wait_ge(taken, b)
                norm_turn(nc, core, norm_bank).then_inc(turned, 1)

            def body(b, place, is_first):
                pe.wait_ge(xcur_ready[place], (b - place) * 8 + 16)
                if gated:
                    up(b, place, 0)
                for e in range(E):
                    if gated and e + 1 < E:
                        up(b, place, e + 1)
                    down(b, place, e)
                    if e == 1 and not is_first:
                        turn(b - 1)

            pe.wait_ge(weights_loaded, 16 * len(loads))
            for n in range(N):
                last = nc.tensor.matmul(logits_view[:, n, :], core.xT[:, n * P:(n + 1) * P], router[:, :], start=True, stop=True)
            last.then_inc(logits_full, 1)
            if not gated:
                for e in range(E):
                    if e >= 2:
                        pe.wait_ge(mixed_taken, e - 1)
                    for f in range(F):
                        last = nc.tensor.matmul(mixed_bank[:, e % 2, 0:C], w_in[:, e, f, :], w_out[:, e, f, :],
                                                start=(f == 0), stop=(f == F - 1))
                    last.then_inc(mixed_full, 1)
                pe.wait_ge(mixed_taken, E)
            bodies(pe, body)
            turn(B - 1)

        @block.scalar
        def _(act):
            if not gated:
                for e in range(E):
                    act.wait_ge(mixed_full, e + 1)
                    nc.scalar.copy(both[:, e, :], mixed_bank[:, e % 2, 0:C]).then_inc(mixed_taken, 1)
            act.wait_ge(diff_ready, 1)
            nc.scalar.activation(share[:, 1, :], share[:, 1, :], ACT.Exp).then_inc(exp_ready, 1)

            def take(b):
                act.wait_ge(turned, b + 1)
                nc.scalar.copy(core.xT[:, ds(b * T, T)], norm_bank[:, :]).then_inc(taken, 1)

            def body(b, place, is_first):
                for m in range(E * CHUNKS):
                    rows = H[m % CHUNKS]
                    bank = chunk_parity(place, m)
                    act.wait_ge(up_full, b * E * CHUNKS + m + 1)
                    if not (isinstance(b, int) and b == 0 and m < 2):
                        act.wait_ge(hidden_done, b * E * CHUNKS + m - 1)
                    nc.scalar.activation(silu[0:rows, bank, :], gate_bank[0:rows, bank, :], ACT.Silu).then_inc(silu_done, 1)
                    if m == 3 * CHUNKS and not is_first:
                        take(b - 1)
                if not gated and not is_first:
                    take(b - 1)

            bodies(act, body)
            take(B - 1)

        @block.vector
        def _(dve):
            def multiply(b, place, e):
                for c in range(CHUNKS):
                    m = e * CHUNKS + c
                    bank = chunk_parity(place, m)
                    if c == 0 and not (isinstance(b, int) and b == 0 and e < 2):
                        dve.wait_ge(down_full, b * E + e - 1)
                    dve.wait_ge(silu_done, b * E * CHUNKS + m + 1)
                    nc.vector.tensor_tensor(hid[0:H[c], e_parity(place, e), c, :], up_bank[0:H[c], bank, :],
                                            silu[0:H[c], bank, :], ALU.mult).then_inc(hidden_done, 1)

            def combine(b, place, e):
                dve.wait_ge(down_full, b * E + e + 1)
                if not (isinstance(b, int) and b == 0 and e == 0):
                    dve.wait_ge(combined, b * E + e)
                for j in range(TB):
                    tokens = core.x[:, ds(b * TB + j, 1), :].rearrange("p a c -> p (a c)")
                    last = nc.vector.scalar_tensor_tensor(
                        tokens, down_bank[:, e_parity(place, e), j * C:(j + 1) * C],
                        gates[:, ds(b * TB + j, 1), e:e + 1].rearrange("p a c -> p (a c)"), tokens, ALU.mult, ALU.add)
                last.then_inc(combined, 1)

            def body(b, place, is_first):
                if gated:
                    multiply(b, place, 0)
                for e in range(E):
                    if gated and e + 1 < E:
                        multiply(b, place, e + 1)
                    combine(b, place, e)
                dve.wait_ge(combined, (b + 1) * E)
                chain.at(b * NORM_STEPS)
                norm_stats(nc, dve, core, chain, b).then_inc(var_ready, 1)
                dve.wait_ge(rstd_ready, b + 1)
                if not is_first:
                    dve.wait_ge(turned, b)
                norm_apply(nc, core, b).then_inc(xn_ready, 1)

            def step(instruction):
                route_chain.inc(instruction)
                route_chain.settle(dve)

            dve.wait_ge(order_ready, 1)
            dve.wait_ge(logits_full, 1)
            step(nc.vector.tensor_copy(logits[:, :, :], logits_view))
            choose(nc, dve, route_chain, logits[:, :, :], scratch[:, :, :], order[:, :], best[:, :], top[:, 0, :], first[:, :, :])
            step(nc.vector.scalar_tensor_tensor(logits[:, :, :], first[:, :, :], -3e38, logits[:, :, :], ALU.mult, ALU.add))
            choose(nc, dve, route_chain, logits[:, :, :], scratch[:, :, :], order[:, :], best[:, :], top[:, 1, :], second[:, :, :])
            nc.vector.tensor_tensor(share[:, 1, :], top[:, 1, :], top[:, 0, :], ALU.subtract).then_inc(diff_ready, 1)
            dve.wait_ge(exp_ready, 1)
            step(nc.vector.tensor_scalar(total[:, :], share[:, 1, :], 1.0, None, ALU.add))
            step(nc.vector.reciprocal(share[:, 0, :], total[:, :]))
            step(nc.vector.tensor_tensor(share[:, 1, :], share[:, 1, :], share[:, 0, :], ALU.mult))
            step(nc.vector.tensor_tensor(first[:, :, :], first[:, :, :], share[:, 0, :].unsqueeze(2).to_broadcast([P, N, E]), ALU.mult))
            step(nc.vector.tensor_tensor(second[:, :, :], second[:, :, :], share[:, 1, :].unsqueeze(2).to_broadcast([P, N, E]), ALU.mult))
            step(nc.vector.tensor_tensor(gates[:, :, :], first[:, :, :], second[:, :, :], ALU.add))
            bodies(dve, body)



def stage_decay(core, w):
    nc = core.nc
    H, DH = 16, 64
    UNROLL = 2
    BLOCKS = (3, 2, 1, 0)
    WIDTH = [(i + 1) * P for i in range(TB)]
    START = [0, P, 3 * P, 6 * P]
    TOTAL = 10 * P
    ITEMS = ("k", "k_swap", "q", "q_swap", "v", "knorm", "qnorm")
    FREE = (4, 3)
    TABLE_STEPS = 11
    TWO_PI = 6.283185307179586
    C1 = 6.28125
    C2 = float(np.round((TWO_PI - C1) * 2**21) / 2**21)
    C3 = TWO_PI - C1 - C2
    ROUND = 12582912.0
    HALF_PI, BOUND = TWO_PI / 4, 3.1415925

    names = ("inputs_loaded", "pack_even", "pack_odd", "wo_even", "wo_odd", "const_ready", "params_ready", "proj_full",
             "proj_free_0", "proj_free_1", "rotated", "squared", "g_ready", "s_full", "a1_done", "a2_done", "relu_done",
             "r_done", "ln_done", "logit_done", "max_done", "exp_done", "t_full", "pt_free_0", "pt_free_1", "pv_full",
             "ot_done", "y_full", "x_done", "recip_done", "angle_ready", "phase_ready", "z_ready", "etab_ready",
             "v_ready", "lnv_ready", "tables_ready", "var_ready", "rstd_ready", "xn_ready", "turned", "taken",
             "soft_exp", "soft_ln", "mu_exp")
    S = {n: core.sem(n) for n in names}
    proj_free, pt_free = (S["proj_free_0"], S["proj_free_1"]), (S["pt_free_0"], S["pt_free_1"])
    pack_ready, wo_ready = (S["pack_even"], S["pack_odd"]), (S["wo_even"], S["wo_odd"])
    table_chain, const_chain, chain = Count(core.sem("table_chain")), Count(core.sem("const_chain")), Count(core.sem("norm_chain"))

    def wait(eng, name, value):
        if not (isinstance(value, int) and value <= 0):
            eng.wait_ge(S[name] if isinstance(name, str) else name, value)

    with ExitStack() as ctx:
        def sb(name, shape, dtype=F32):
            return core.sbuf(ctx, name, shape, dtype)

        pack, wo = sb("pack", [P, 2, 5, P]), sb("wo", [P, 2, C])
        cos, sin = sb("cos", [P, 2, T]), sb("sin", [P, 2, T])
        e_tab, r_tab, l_tab = sb("e_tab", [P, 2, T]), sb("r_tab", [P, 2, T]), sb("l_tab", [P, 2, T])
        steps, dist, mask = sb("steps", [P, T]), sb("dist", [P, T]), sb("mask", [P, T])
        angle, turns, folded = sb("angle", [P, T]), sb("turns", [P, T]), sb("folded", [P, T])
        z, var, lnv = sb("z", [P, T]), sb("var", [P, T]), sb("lnv", [P, T])
        ones, quarter = sb("ones", [P, P]), sb("quarter", [P, 1])
        sign, half_pi = sb("sign", [P, 1]), sb("half_pi", [P, 1])
        omega = sb("omega", [P, H])
        raw, soft, tmp = sb("raw", [P, 4, H]), sb("soft", [P, 4, H]), sb("tmp", [P, 4, H])
        mu_raw, tau, mu = sb("mu_raw", [P, H]), sb("tau", [P, H]), sb("mu", [P, H])
        neg_mu, amp, floor, coef, mu_recip = (sb(n, [P, H]) for n in ("neg_mu", "amp", "floor", "coef", "mu_recip"))
        parts = sb("parts", [P, 2, 2, T])
        q, k = sb("q", [P, 2, T]), sb("k", [P, 2, T])
        qsq, ksq = sb("qsq", [P, T]), sb("ksq", [P, T])
        knorm, g = sb("knorm", [P, T]), sb("g", [P, 2, TOTAL])
        qnorm = sb("qnorm", [P, 2, TB])
        v = sb("v", [P, 4, TB, P])
        u = sb("u", [P, 4, TOTAL])
        neg_max, rowsum, recip = sb("neg_max", [P, 4, TB]), sb("rowsum", [P, 4, TB]), sb("recip", [P, 2, TB])
        pT, oT = sb("pT", [P, 2, TB, T]), sb("oT", [P, 2, T])

        proj_bank = core.psum(ctx, "proj_bank", [P, 2, T])
        s_bank, t_bank = core.psum(ctx, "s_bank", [P, 2, T]), core.psum(ctx, "t_bank", [P, 2, T])
        o_bank, y_bank = core.psum(ctx, "o_bank", [P, T]), core.psum(ctx, "y_bank", [P, T])

        inputs = [(raw[:, n, :], w[name].partition_broadcast(P)) for n, name in enumerate(("sigma", "eta", "gamma", "nu"))]
        inputs += [(mu_raw[:, :], w["mu"].partition_broadcast(P)), (tau[:, :], w["tau"].partition_broadcast(P))]
        inputs += [(omega[32 * r:32 * r + 32, :], w["omega"]) for r in range(4)]

        def part(tile, i):
            return tile[:, START[i]:START[i] + WIDTH[i]]

        def table(tab, h, i):
            return tab[:, h, T - WIDTH[i]:T]

        def pipeline(eng, step):
            def body(i, last):
                for m in range(UNROLL * B):
                    step(i * (UNROLL * B) + m, m, i * UNROLL + m // B, m % B, last and m == UNROLL * B - 1)
            body(0, False)
            with eng.Fori(1, H // UNROLL - 1) as i:
                body(i, False)
            body(H // UNROLL - 1, True)

        def exists(n):
            return not (isinstance(n, int) and n < 0)

        def tables_wanted(h):
            return not (isinstance(h, int) and h == H - 1)

        def head_of(m):
            return (m // B) % 2

        block = ctx.enter_context(nc.Block())

        @block.sync
        def _(sp):
            for dst, src in inputs:
                sp.dma_start(dst, src).then_inc(S["inputs_loaded"], 16)
            for h in range(2):
                sp.dma_start(pack[:, h], w["pack"][h]).then_inc(pack_ready[h], 16)
                sp.dma_start(wo[:, h, :], w["wo"][h]).then_inc(wo_ready[h], 16)
            with sp.Fori(0, H // 2 - 1) as i:
                for p in range(2):
                    h = i * 2 + p
                    sp.wait_ge(S["proj_full"], (h + 1) * (B * len(ITEMS)))
                    sp.dma_start(pack[:, p], w["pack"][ds(h + 2, 1)].rearrange("a c m n -> (a c) m n")).then_inc(pack_ready[p], 16)
                    sp.wait_ge(S["y_full"], (h + 1) * B)
                    sp.dma_start(wo[:, p, :], w["wo"][ds(h + 2, 1)].rearrange("a c n -> (a c) n")).then_inc(wo_ready[p], 16)

        @block.tensor
        def _(pe):
            def project(n, m, h, b, items):
                p = head_of(m)
                for idx in items:
                    what = ITEMS[idx]
                    if idx == 0 and b == 0:
                        pe.wait_ge(pack_ready[p], (h - p) * 8 + 16)
                    wait(pe, proj_free[idx % 2], n * FREE[idx % 2] + idx // 2)
                    bank = proj_bank[:, idx % 2, :]
                    if idx < 4:
                        last = nc.tensor.matmul(bank, pack[:, p, idx, :], core.xT[:, b * T:(b + 1) * T], start=True, stop=True)
                    elif what == "v":
                        for j in range(TB):
                            last = nc.tensor.matmul(bank[:, j * P:(j + 1) * P], core.xT[:, b * T + j * P:b * T + (j + 1) * P],
                                                    pack[:, p, 4, :], start=True, stop=True)
                    elif what == "knorm":
                        pe.wait_ge(S["squared"], n * 2 + 1)
                        last = nc.tensor.matmul(bank, ones[:, :], ksq[:, :], start=True, stop=True)
                    else:
                        pe.wait_ge(S["squared"], n * 2 + 2)
                        for j in range(TB):
                            last = nc.tensor.matmul(bank[:, j:j + 1], qsq[:, j * P:(j + 1) * P], quarter[:, :], start=True, stop=True)
                    last.then_inc(S["proj_full"], 1)

            def scores(n, m, s):
                i = BLOCKS[s]
                if s == 0:
                    pe.wait_ge(S["rotated"], n * 2 + 2)
                wait(pe, "a1_done", n * 4 + s - 1)
                nc.tensor.matmul(s_bank[:, s % 2, 0:WIDTH[i]], q[:, m % 2, i * P:(i + 1) * P], k[:, m % 2, 0:WIDTH[i]],
                                 start=True, stop=True).then_inc(S["s_full"], 1)

            def turn_probs(n, m, s):
                i = BLOCKS[s]
                pe.wait_ge(S["exp_done"], n * 4 + s + 1)
                wait(pe, pt_free[s % 2], n * 2 + s // 2)
                for j in range(i + 1):
                    last = nc.tensor.transpose(t_bank[:, s % 2, j * P:(j + 1) * P], part(u[:, m % 4], i)[:, j * P:(j + 1) * P],
                                               core.ident[:, :])
                last.then_inc(S["t_full"], 1)

            def values(n, m):
                pe.wait_ge(pt_free[0], n * 2 + 2)
                pe.wait_ge(pt_free[1], n * 2 + 2)
                wait(pe, "ot_done", n)
                for j in range(TB):
                    last = nc.tensor.matmul(o_bank[:, j * P:T], v[:, m % 4, j, :], pT[:, m % 2, j, j * P:T],
                                            start=(j == 0), stop=(j == TB - 1))
                last.then_inc(S["pv_full"], 1)

            def output(n, m, h, b):
                p = head_of(m)
                if b == 0:
                    pe.wait_ge(wo_ready[p], (h - p) * 8 + 16)
                pe.wait_ge(S["ot_done"], n + 1)
                wait(pe, "x_done", n)
                for j in range(TB):
                    last = nc.tensor.matmul(y_bank[:, j * P:(j + 1) * P], oT[:, m % 2, j * P:(j + 1) * P], wo[:, p, :],
                                            start=True, stop=True)
                last.then_inc(S["y_full"], 1)

            def step(n, m, h, b, last):
                nxt = (n + 1, (m + 1) % (UNROLL * B), h + (1 if b == B - 1 else 0), (b + 1) % B)
                old = (n - 2, (m - 2) % (UNROLL * B), h - (1 if b < 2 else 0), (b - 2) % B)
                scores(n, m, 0)
                scores(n, m, 1)
                if not last:
                    project(*nxt, (0, 1))
                scores(n, m, 2)
                scores(n, m, 3)
                if exists(old[0]):
                    turn_probs(*old[:2], 0)
                    turn_probs(*old[:2], 1)
                if not last:
                    project(*nxt, (2, 3))
                if exists(old[0]):
                    turn_probs(*old[:2], 2)
                    turn_probs(*old[:2], 3)
                if not last:
                    project(*nxt, (4,))
                if exists(old[0]):
                    values(*old[:2])
                if not last:
                    project(*nxt, (5, 6))
                if exists(old[0]):
                    output(*old)

            pe.wait_ge(S["const_ready"], 9)
            project(0, 0, 0, 0, range(7))
            pipeline(pe, step)
            for n in (H * B - 2, H * B - 1):
                m = n % (UNROLL * B)
                for s in range(4):
                    turn_probs(n, m, s)
                values(n, m)
                output(n, m, n // B, n % B)
            pe.sem_inc(S["turned"], 1)
            with pe.Fori(0, B) as b:
                pe.wait_ge(S["xn_ready"], b + 1)
                pe.wait_ge(S["taken"], b + 1)
                norm_turn(nc, core, proj_bank[:, 0, :]).then_inc(S["turned"], 1)


        def angles(dve, t, p):
            def count(instruction):
                table_chain.inc(instruction)
                table_chain.settle(dve)

            table_chain.at(t * TABLE_STEPS)
            om = omega[:, ds(t, 1)]
            wait(dve, "phase_ready", t)
            wait(dve, "etab_ready", t)
            count(nc.vector.tensor_scalar(angle[:, :], steps[:, :], om, None, ALU.mult))
            count(nc.vector.tensor_scalar(turns[:, :], angle[:, :], 1.0 / TWO_PI, ROUND, ALU.mult, ALU.add))
            count(nc.vector.tensor_scalar(turns[:, :], turns[:, :], ROUND, None, ALU.subtract))
            for c in (C1, C2, C3):
                count(nc.vector.scalar_tensor_tensor(angle[:, :], turns[:, :], -c, angle[:, :], ALU.mult, ALU.add))
            count(nc.vector.tensor_scalar(angle[:, :], angle[:, :], BOUND, -BOUND, ALU.min, ALU.max))
            nc.vector.scalar_tensor_tensor(folded[:, :], angle[:, :], -1.0, angle[:, :], ALU.mult, ALU.max).then_inc(S["angle_ready"], 1)
            nc.vector.tensor_scalar(z[:, :], dist[:, :], neg_mu[:, ds(t, 1)], -30.0, ALU.mult, ALU.max).then_inc(S["z_ready"], 1)

        def phases(act, t, p):
            act.wait_ge(S["angle_ready"], t + 1)
            wait(act, proj_free[1], (t - 1) * (B * FREE[1]))
            nc.scalar.activation(sin[:, p, :], angle[:, :], ACT.Sin, scale=sign[:, 0:1])
            nc.scalar.activation(cos[:, p, :], folded[:, :], ACT.Sin, scale=-1.0, bias=half_pi[:, 0:1]).then_inc(S["phase_ready"], 1)

        def decays(act, t, p):
            act.wait_ge(S["z_ready"], t + 1)
            wait(act, "a2_done", (t - 1) * (B * 4))
            wait(act, "g_ready", (t - 1) * B)
            nc.scalar.activation(e_tab[:, p, :], z[:, :], ACT.Exp).then_inc(S["etab_ready"], 1)

        def variances(dve, t, p):
            def count(instruction):
                table_chain.inc(instruction)
                table_chain.settle(dve)

            table_chain.at(t * TABLE_STEPS + 7)
            dve.wait_ge(S["etab_ready"], t + 1)
            wait(dve, "lnv_ready", t)
            wait(dve, "r_done", (t - 1) * (B * 4))
            count(nc.vector.tensor_tensor(var[:, :], e_tab[:, p, :], e_tab[:, p, :], ALU.mult))
            count(nc.vector.tensor_scalar(var[:, :], var[:, :], -1.0, 1.0, ALU.mult, ALU.add))
            nc.vector.tensor_scalar(var[:, :], var[:, :], amp[:, ds(t, 1)], floor[:, ds(t, 1)], ALU.mult, ALU.add).then_inc(S["v_ready"], 1)
            dve.wait_ge(S["v_ready"], t + 1)
            count(nc.vector.tensor_scalar(r_tab[:, p, :], var[:, :], soft[:, 3, ds(t, 1)], None, ALU.mult))
            count(nc.vector.reciprocal(r_tab[:, p, :], r_tab[:, p, :]))

        def log_variances(act, t, p):
            act.wait_ge(S["v_ready"], t + 1)
            wait(act, "tables_ready", t)
            nc.scalar.activation(lnv[:, :], var[:, :], ACT.Ln).then_inc(S["lnv_ready"], 1)

        def additive(dve, t, p):
            dve.wait_ge(S["lnv_ready"], t + 1)
            wait(dve, "logit_done", (t - 1) * (B * 4))
            nc.vector.scalar_tensor_tensor(l_tab[:, p, :], lnv[:, :], -0.5 * DH, mask[:, :], ALU.mult, ALU.add).then_inc(S["tables_ready"], 1)

        @block.vector
        def _(dve):
            def const(instruction):
                const_chain.inc(instruction)
                const_chain.settle(dve)

            def rotate(n, m, h, which):
                p = head_of(m)
                if which == 0 and m % B == 0:
                    dve.wait_ge(S["phase_ready"], h + 1)
                wait(dve, "rotated", n * 2 - 1 + which)
                for sw in range(2):
                    idx = 2 * which + sw
                    dve.wait_ge(S["proj_full"], n * len(ITEMS) + idx + 1)
                    nc.vector.scalar_tensor_tensor(parts[:, which, sw, :], proj_bank[:, sw, :], -2.0 if which else 1.0,
                                                   (sin if sw else cos)[:, p, :], ALU.mult, ALU.mult).then_inc(proj_free[sw], 1)

            def distances(n, m, s):
                i = BLOCKS[s]
                dve.wait_ge(S["s_full"], n * 4 + s + 1)
                if s == 0:
                    dve.wait_ge(S["g_ready"], n + 1)
                    wait(dve, "t_full", (n - 3) * 4)
                nc.vector.tensor_tensor(part(u[:, m % 4], i), s_bank[:, s % 2, 0:WIDTH[i]], part(g[:, m % 2], i), ALU.add)\
                  .then_inc(S["a1_done"], 1)

            def decay(n, m, s):
                i = BLOCKS[s]
                if s == 0:
                    dve.wait_ge(S["a1_done"], n * 4 + 4)
                here = part(u[:, m % 4], i)
                nc.vector.tensor_tensor(here, here, table(e_tab, head_of(m), i), ALU.mult).then_inc(S["a2_done"], 1)

            def logits(n, m, h, s):
                i = BLOCKS[s]
                if s == 0:
                    dve.wait_ge(S["ln_done"], n + 1)
                    if m % B == 0:
                        dve.wait_ge(S["tables_ready"], h + 1)
                here = part(u[:, m % 4], i)
                nc.vector.scalar_tensor_tensor(here, here, coef[:, ds(h, 1)], table(l_tab, head_of(m), i), ALU.mult, ALU.add)\
                  .then_inc(S["logit_done"], 1)

            def maximum(n, m, s):
                i = BLOCKS[s]
                if s == 0:
                    dve.wait_ge(S["logit_done"], n * 4 + 4)
                nc.vector.tensor_reduce(neg_max[:, m % 4, i:i + 1], part(u[:, m % 4], i), AX_X, ALU.max, negate=True)\
                  .then_inc(S["max_done"], 1)

            def take_turned(n, m, s):
                i = BLOCKS[s]
                dve.wait_ge(S["t_full"], n * 4 + s + 1)
                if s == 0:
                    wait(dve, "pv_full", n - 1)
                nc.vector.tensor_copy(pT[:, m % 2, 0:i + 1, i * P:(i + 1) * P],
                                      t_bank[:, 0, 0:WIDTH[i]].rearrange("p (j c) -> p j c", c=P)).then_inc(pt_free[0], 1)

            def accumulate(n, m, b):
                dve.wait_ge(S["exp_done"], n * 4 + 4)
                nc.vector.reciprocal(recip[:, m % 2, :], rowsum[:, m % 4, :]).then_inc(S["recip_done"], 1)
                dve.wait_ge(S["recip_done"], n + 1)
                dve.wait_ge(S["y_full"], n + 1)
                wait(dve, "x_done", n)
                for j in range(TB):
                    tokens = core.x[:, b * TB + j, :]
                    last = nc.vector.scalar_tensor_tensor(tokens, y_bank[:, j * P:(j + 1) * P], recip[:, m % 2, j:j + 1],
                                                          tokens, ALU.mult, ALU.add)
                last.then_inc(S["x_done"], 1)

            def step(n, m, h, b, last):
                old = (n - 2, (m - 2) % (UNROLL * B))
                mid_head = h - (1 if b == 0 else 0)
                if m % B == 0:
                    dve.wait_ge(S["etab_ready"], h + 1)
                for s in range(4):
                    distances(n, m, s)
                for s in range(4):
                    decay(n, m, s)
                if exists(n - 1):
                    for s in range(4):
                        logits(n - 1, (m - 1) % (UNROLL * B), mid_head, s)
                    for s in range(4):
                        maximum(n - 1, (m - 1) % (UNROLL * B), s)
                if not last:
                    next_head = h + (1 if b == B - 1 else 0)
                    rotate(n + 1, (m + 1) % (UNROLL * B), next_head, 0)
                if exists(old[0]):
                    take_turned(*old, 0)
                if not last:
                    rotate(n + 1, (m + 1) % (UNROLL * B), next_head, 1)
                if exists(old[0]):
                    take_turned(*old, 2)
                if tables_wanted(h):
                    p = 1 - head_of(m)
                    if b == 1:
                        angles(dve, h + 1, p)
                    if b == 4:
                        variances(dve, h + 1, p)
                    if b == 6:
                        additive(dve, h + 1, p)
                if exists(old[0]):
                    accumulate(*old, (b - 2) % B)

            dve.wait_ge(S["inputs_loaded"], 16 * len(inputs))
            for r in (1, 3):
                last = nc.vector.tensor_scalar(omega[32 * r:32 * r + 32, :], omega[32 * r:32 * r + 32, :], -1.0, None, ALU.mult)
            const(last)
            const(nc.vector.scalar_tensor_tensor(tmp[:, :, :], raw[:, :, :], -1.0, raw[:, :, :], ALU.mult, ALU.max))
            dve.wait_ge(S["soft_ln"], 1)
            const(nc.vector.scalar_tensor_tensor(soft[:, :, :], raw[:, :, :], 0.0, tmp[:, :, :], ALU.max, ALU.add))
            dve.wait_ge(S["mu_exp"], 1)
            const(nc.vector.tensor_scalar(mu[:, :], mu[:, :], 1.0, None, ALU.add))
            const(nc.vector.reciprocal(mu[:, :], mu[:, :]))
            const(nc.vector.tensor_scalar(mu[:, :], mu[:, :], 1e-4, None, ALU.add))
            const(nc.vector.tensor_scalar(neg_mu[:, :], mu[:, :], -1.0, None, ALU.mult))
            const(nc.vector.tensor_scalar(mu_recip[:, :], mu[:, :], 2.0, None, ALU.mult))
            const(nc.vector.reciprocal(mu_recip[:, :], mu_recip[:, :]))
            const(nc.vector.tensor_tensor(amp[:, :], soft[:, 0, :], mu_recip[:, :], ALU.mult))
            const(nc.vector.tensor_tensor(floor[:, :], soft[:, 1, :], soft[:, 2, :], ALU.add))
            const(nc.vector.tensor_scalar(coef[:, :], soft[:, 3, :], float(DH), -0.5, ALU.add, ALU.mult))
            const(nc.vector.tensor_tensor(coef[:, :], coef[:, :], tau[:, :], ALU.mult))
            dve.wait_ge(S["const_ready"], 9)
            const(nc.vector.scalar_tensor_tensor(dist[:, :], dist[:, :], -1.0, dist[:, :], ALU.mult, ALU.max))
            angles(dve, 0, 0)
            variances(dve, 0, 0)
            additive(dve, 0, 0)
            rotate(0, 0, 0, 0)
            rotate(0, 0, 0, 1)
            pipeline(dve, step)
            final = H * B
            for s in range(4):
                logits(final - 1, UNROLL * B - 1, H - 1, s)
            for s in range(4):
                maximum(final - 1, UNROLL * B - 1, s)
            for n in (final - 2, final - 1):
                take_turned(n, n % (UNROLL * B), 0)
                take_turned(n, n % (UNROLL * B), 2)
                accumulate(n, n % (UNROLL * B), n % B)
            dve.wait_ge(S["x_done"], final)
            with dve.Fori(0, B) as b:
                chain.at(b * NORM_STEPS)
                norm_stats(nc, dve, core, chain, b).then_inc(S["var_ready"], 1)
                dve.wait_ge(S["rstd_ready"], b + 1)
                dve.wait_ge(S["turned"], b + 1)
                norm_apply(nc, core, b).then_inc(S["xn_ready"], 1)

        @block.scalar
        def _(act):
            def squares(n, m, which):
                wait(act, "proj_full", n * len(ITEMS))
                act.wait_ge(S["rotated"], n * 2 + 1 + which)
                src, dst = (q, qsq) if which else (k, ksq)
                nc.scalar.activation(dst[:, :], src[:, m % 2, :], ACT.Square).then_inc(S["squared"], 1)

            def take(n, m, idx):
                act.wait_ge(S["proj_full"], n * len(ITEMS) + idx + 1)
                bank = proj_bank[:, idx % 2, :]
                if idx == 4:
                    nc.scalar.copy(v[:, m % 4, :, :], bank.rearrange("p (j d) -> p j d", j=TB)).then_inc(proj_free[0], 1)
                elif idx == 5:
                    wait(act, "g_ready", n)
                    nc.scalar.copy(knorm[:, :], bank).then_inc(proj_free[1], 1)
                else:
                    nc.scalar.copy(qnorm[:, m % 2, :], bank[:, 0:TB]).then_inc(proj_free[0], 1)

            def relu(n, m, s):
                i = BLOCKS[s]
                if s == 0:
                    act.wait_ge(proj_free[0], n * FREE[0] + FREE[0])
                act.wait_ge(S["a2_done"], n * 4 + s + 1)
                here = part(u[:, m % 4], i)
                nc.scalar.activation(here, here, ACT.Relu, bias=qnorm[:, m % 2, i:i + 1]).then_inc(S["relu_done"], 1)

            def log(n, m):
                act.wait_ge(S["r_done"], n * 4 + 4)
                nc.scalar.activation(u[:, m % 4, :], u[:, m % 4, :], ACT.Ln, bias=1.0).then_inc(S["ln_done"], 1)

            def exponentials(n, m, s):
                i = BLOCKS[s]
                act.wait_ge(S["max_done"], n * 4 + s + 1)
                here = part(u[:, m % 4], i)
                nc.scalar.activation(here, here, ACT.Exp, bias=neg_max[:, m % 4, i:i + 1],
                                     accum_out=rowsum[:, m % 4, i:i + 1]).then_inc(S["exp_done"], 1)

            def take_turned(n, m, s):
                i = BLOCKS[s]
                act.wait_ge(S["t_full"], n * 4 + s + 1)
                if s == 1:
                    wait(act, "pv_full", n - 1)
                nc.scalar.copy(pT[:, m % 2, 0:i + 1, i * P:(i + 1) * P],
                               t_bank[:, 1, 0:WIDTH[i]].rearrange("p (j c) -> p j c", c=P)).then_inc(pt_free[1], 1)

            def take_outputs(n, m):
                act.wait_ge(S["pv_full"], n + 1)
                wait(act, "y_full", n - 1)
                nc.scalar.copy(oT[:, m % 2, :], o_bank[:, :]).then_inc(S["ot_done"], 1)

            def step(n, m, h, b, last):
                nxt, mid, old = ((m + d) % (UNROLL * B) for d in (1, -1, -2))
                if exists(n - 1):
                    log(n - 1, mid)
                for s in range(4):
                    relu(n, m, s)
                if tables_wanted(h) and b == 5:
                    log_variances(act, h + 1, 1 - head_of(m))
                if exists(n - 1):
                    for s in range(4):
                        exponentials(n - 1, mid, s)
                if tables_wanted(h) and b == 3:
                    decays(act, h + 1, 1 - head_of(m))
                if exists(n - 2):
                    take_turned(n - 2, old, 1)
                if not last:
                    squares(n + 1, nxt, 0)
                if exists(n - 2):
                    take_turned(n - 2, old, 3)
                if not last:
                    squares(n + 1, nxt, 1)
                    take(n + 1, nxt, 4)
                if exists(n - 2):
                    take_outputs(n - 2, old)
                if not last:
                    take(n + 1, nxt, 5)
                    take(n + 1, nxt, 6)
                if tables_wanted(h) and b == 2:
                    phases(act, h + 1, 1 - head_of(m))

            act.wait_ge(const_chain.sem, 2)
            nc.scalar.activation(tmp[:, :, :], tmp[:, :, :], ACT.Exp, scale=-1.0).then_inc(S["soft_exp"], 1)
            nc.scalar.activation(mu[:, :], mu_raw[:, :], ACT.Exp, scale=-1.0).then_inc(S["mu_exp"], 1)
            act.wait_ge(S["soft_exp"], 1)
            nc.scalar.activation(tmp[:, :, :], tmp[:, :, :], ACT.Ln, bias=1.0).then_inc(S["soft_ln"], 1)
            act.wait_ge(S["const_ready"], 9)
            phases(act, 0, 0)
            decays(act, 0, 0)
            log_variances(act, 0, 0)
            squares(0, 0, 0)
            squares(0, 0, 1)
            for idx in (4, 5, 6):
                take(0, 0, idx)
            pipeline(act, step)
            final = H * B
            log(final - 1, UNROLL * B - 1)
            for s in range(4):
                exponentials(final - 1, UNROLL * B - 1, s)
            for n in (final - 2, final - 1):
                take_turned(n, n % (UNROLL * B), 1)
                take_turned(n, n % (UNROLL * B), 3)
                take_outputs(n, n % (UNROLL * B))
            act.sem_inc(S["taken"], 1)
            with act.Fori(0, B) as b:
                act.wait_ge(S["turned"], b + 2)
                nc.scalar.copy(core.xT[:, ds(b * T, T)], proj_bank[:, 0, :]).then_inc(S["taken"], 1)

        @block.gpsimd
        def _(pool):
            def rotated(n, m, which):
                pool.wait_ge(proj_free[1], n * FREE[1] + 1 + which)
                if which == 0:
                    wait(pool, "s_full", (n - 1) * 4)
                nc.gpsimd.tensor_tensor((q if which else k)[:, m % 2, :], parts[:, which, 0, :], parts[:, which, 1, :], ALU.add)\
                  .then_inc(S["rotated"], 1)

            def key_terms(n, m, h, b):
                pool.wait_ge(proj_free[1], n * FREE[1] + 3)
                if b == 0:
                    pool.wait_ge(S["etab_ready"], h + 1)
                wait(pool, "a1_done", (n - 1) * 4)
                for i in BLOCKS:
                    last = nc.gpsimd.tensor_tensor(part(g[:, m % 2], i), knorm[:, 0:WIDTH[i]], table(e_tab, head_of(m), i), ALU.mult)
                last.then_inc(S["g_ready"], 1)

            def over_variance(n, m, h, b, s):
                i = BLOCKS[s]
                if b == 0 and s == 0:
                    pool.wait_ge(S["tables_ready"], h + 1)
                pool.wait_ge(S["relu_done"], n * 4 + s + 1)
                here = part(u[:, m % 4], i)
                nc.gpsimd.tensor_tensor(here, here, table(r_tab, head_of(m), i), ALU.mult).then_inc(S["r_done"], 1)

            def step(n, m, h, b, last):
                nxt = (m + 1) % (UNROLL * B)
                for s in range(4):
                    over_variance(n, m, h, b, s)
                if not last:
                    rotated(n + 1, nxt, 0)
                    rotated(n + 1, nxt, 1)
                    key_terms(n + 1, nxt, h + (1 if b == B - 1 else 0), (b + 1) % B)

            nc.gpsimd.memset(ones[:, :], 1.0).then_inc(S["const_ready"], 1)
            nc.gpsimd.memset(quarter[:, :], 0.25).then_inc(S["const_ready"], 1)
            nc.gpsimd.memset(sign[:, :], 1.0).then_inc(S["const_ready"], 1)
            nc.gpsimd.memset(half_pi[:, :], HALF_PI).then_inc(S["const_ready"], 1)
            nc.gpsimd.memset(mask[:, :], 0.0).then_inc(S["const_ready"], 1)
            nc.gpsimd.iota(steps[:, :], pattern=[[1, T]], base=0, channel_multiplier=0,
                           allow_small_or_imprecise_dtypes=True).then_inc(S["const_ready"], 1)
            nc.gpsimd.iota(dist[:, :], pattern=[[-1, T]], base=T - P, channel_multiplier=1,
                           allow_small_or_imprecise_dtypes=True).then_inc(S["const_ready"], 1)
            pool.wait_ge(S["const_ready"], 7)
            nc.gpsimd.memset(sign[0:DH, :], -1.0).then_inc(S["const_ready"], 1)
            nc.gpsimd.affine_select(out=mask[:, :], in_=mask[:, :], compare_op=ALU.is_ge, fill=NEG, base=T - P,
                                    pattern=[[-1, T]], channel_multiplier=1).then_inc(S["const_ready"], 1)
            rotated(0, 0, 0)
            rotated(0, 0, 1)
            key_terms(0, 0, 0, 0)
            pipeline(pool, step)
            with pool.Fori(0, B) as b:
                pool.wait_ge(S["var_ready"], b + 1)
                norm_rstd(nc, core).then_inc(S["rstd_ready"], 1)


ROPE_CAUSAL = Attention(heads=16, dim=8, kv_heads=16, causal=True, rope=1, bias=True, gate=False)
GROUPED = Attention(heads=8, dim=32, kv_heads=2, causal=False, rope=1, bias=False, gate=True)
BILINEAR = Attention(heads=16, dim=8, kv_heads=16, causal=False, rope=0, bias=True, gate=False)


def build(nc, dram, plan):
    with ExitStack() as ctx:
        core = Core(nc, ctx, dram)
        stage_load(core)
        core.end_stage()
        for stage in plan:
            if stage == "attn_rope":
                stage_attention(core, ROPE_CAUSAL, {n: dram["a_" + n] for n in (
                    "wq", "wq_swap", "wk", "wk_swap", "bq", "bq_swap", "bk", "bk_swap", "wv", "bv", "wo", "bo", "cos", "sin", "kaug")})
            elif stage == "attn_gqa":
                stage_attention(core, GROUPED, {n: dram["g_" + n] for n in (
                    "wq", "wq_swap", "wk", "wk_swap", "wv", "wo", "wg", "cos", "sin", "kaug")})
            elif stage == "attn_bilinear":
                stage_attention(core, BILINEAR, {n: dram["v_" + n] for n in ("wq", "wk", "wv", "bv", "wo", "bo", "kaug")})
            elif stage == "attn_decay":
                stage_decay(core, {n: dram["d_" + n] for n in ("sigma", "eta", "gamma", "nu", "mu", "tau", "omega", "pack", "wo")})
            elif stage == "ffn_linear":
                stage_ffn(core, {n: dram["f_" + n] for n in ("router", "w_in", "w_out")}, 8, None)
            elif stage == "ffn_gated":
                stage_ffn(core, {n: dram["h_" + n] for n in ("router", "wg", "wu", "wd")}, 9, 352)
            core.end_stage()
        stage_store(core)
        core.end_stage()



def _tables(dim, rot, stride, pairs_adjacent, heads_per_group):
    half = rot // 2
    f = np.arange(half, dtype=np.float32)
    theta = np.power(np.float32(10000.0), (np.float32(-2.0) * f / np.float32(rot)).astype(np.float32)).astype(np.float32)
    ang = (np.arange(T, dtype=np.float32)[None, :] * theta[:, None]).astype(np.float32).astype(np.float64)
    cos, sin = np.zeros((P, T), np.float32), np.zeros((P, T), np.float32)
    for r in range(heads_per_group):
        for d in range(dim + 1):
            if d >= rot:
                cos[stride * r + d] = 1.0
                continue
            n, low = (d // 2, d % 2 == 0) if pairs_adjacent else (d % half, d < half)
            cos[stride * r + d] = np.cos(ang[n])
            sin[stride * r + d] = -np.sin(ang[n]) if low else np.sin(ang[n])
    return cos, sin


def kernel(**inputs):
    import ml_dtypes
    import concourse.bacc as _bacc
    from concourse.bass_utils import run_bass_kernel_spmd as _run

    i = {n: np.asarray(a) for n, a in inputs.items()}
    a = {"x": i["L0_attn_a_x"]}
    eye, low = np.eye(P, dtype=np.float32), np.tril(np.ones((P, P), bool))
    a["ident"], a["ident16"] = eye, eye.astype(ml_dtypes.bfloat16)
    a["mask_ij"] = np.where(low, 0.0, NEG).astype(ml_dtypes.bfloat16)
    a["mask_ji"] = np.where(low.T, 0.0, NEG).astype(ml_dtypes.bfloat16)

    def lanes(stride, dim):
        t = np.zeros((P, 1), np.float32)
        t[dim::stride] = -1.0
        return t

    partner = np.arange(C) ^ 1
    for n in "qk":
        wt = i["L0_attn_a_w" + n].T
        a[f"a_w{n}"], a[f"a_w{n}_swap"] = wt, wt[:, partner]
        for tail, bias in (("", i["L0_attn_a_b" + n]), ("_swap", i["L0_attn_a_b" + n][partner])):
            a[f"a_b{n}{tail}"] = bias.reshape(4, 4, 8).transpose(1, 2, 0)
    a["a_wv"], a["a_bv"] = i["L0_attn_a_wv"].T, i["L0_attn_a_bv"]
    a["a_wo"], a["a_bo"] = i["L0_attn_a_wp"].T, i["L0_attn_a_bp"]
    a["a_cos"], a["a_sin"] = _tables(8, 8, 32, True, 4)
    a["a_kaug"] = lanes(32, 8)

    d = np.arange(32)
    within = np.where(d < 8, (d + 4) % 8, d)
    a["g_wq"], a["g_wg"] = i["L1_attn_a_Wq"][:, :256], i["L1_attn_a_Wq"][:, 256:]
    a["g_wq_swap"] = a["g_wq"][:, (np.arange(8)[:, None] * 32 + within).ravel()]
    a["g_wk"] = i["L1_attn_a_Wk"]
    a["g_wk_swap"] = a["g_wk"][:, (np.arange(2)[:, None] * 32 + within).ravel()]
    a["g_wv"], a["g_wo"] = i["L1_attn_a_Wv"], i["L1_attn_a_Wo"]
    a["g_cos"], a["g_sin"] = _tables(32, 8, 64, False, 2)
    a["g_kaug"] = lanes(64, 32)

    wq = np.zeros((C, C), np.float32)
    for h in range(16):
        wq[8 * h:8 * h + 8, 8 * h:8 * h + 8] = i["L1_attn_b_w_att_val"][h]
    a["v_wq"], a["v_wk"] = wq, eye
    a["v_wv"], a["v_bv"] = i["L1_attn_b_wv_w"].T, i["L1_attn_b_wv_b"]
    a["v_wo"], a["v_bo"] = i["L1_attn_b_out_w"].T, i["L1_attn_b_out_b"]
    a["v_kaug"] = lanes(32, 8)

    def by_head(wt):
        return wt.reshape(C, 2, 16, 64).transpose(2, 0, 1, 3)
    wq, wk, wv = (by_head(i["L0_attn_b_W" + n]) for n in "qkv")
    a["d_pack"] = np.stack([t.reshape(16, C, P) for t in (wk, wk[:, :, ::-1], wq, wq[:, :, ::-1], wv)], axis=2)
    a["d_wo"] = i["L0_attn_b_Wo"].reshape(2, 16, 64, C).transpose(1, 0, 2, 3).reshape(16, P, C)
    for n, name in (("sigma", "sigma_raw"), ("eta", "eta_raw"), ("gamma", "gamma_raw"), ("nu", "nu_raw"), ("mu", "mu_raw"), ("tau", "tau")):
        a["d_" + n] = i["L0_attn_b_" + name]
    a["d_omega"] = i["L0_attn_b_omega"].T

    a["f_router"], a["f_w_in"], a["f_w_out"] = i["L0_ffn_w_gate"].T, i["L0_ffn_w_in"], i["L0_ffn_w_out"].transpose(0, 2, 1)
    for n, name in (("router", "Wr"), ("wg", "Wg"), ("wu", "Wu"), ("wd", "Wd")):
        a["h_" + n] = i["L1_ffn_" + name]

    nc = _bacc.Bacc("TRN2", target_bir_lowering=False, num_devices=1)
    arrays, dram = {}, {}
    for n, t in a.items():
        t = np.ascontiguousarray(t)
        arrays[f"in_{n}"] = t
        dram[n] = nc.dram_tensor(f"in_{n}", t.shape, mybir.dt.from_np(t.dtype), kind="ExternalInput").ap()
    dram["out"] = nc.dram_tensor("out_0_dram", (B, T, C), F32, kind="ExternalOutput").ap()
    build(nc, dram, PLAN)
    r = _run(nc, [arrays], core_ids=[0])
    return r.results[0]["out_0_dram"]
```

```python
from contextlib import ExitStack

import numpy as np

import concourse.bass as bass
from concourse import mybir

F32 = mybir.dt.float32
BF16 = mybir.dt.bfloat16
I32 = mybir.dt.int32
U32 = mybir.dt.uint32
ALU = mybir.AluOpType
ACT = mybir.ActivationFunctionType
AX_X = mybir.AxisListType.X

P = 128
B, T, C = 8, 512, 128
TB = T // P
EPS = 1e-5
NORM_STEPS = 2
NEG = -1e30
PLAN = ["attn_rope", "ffn_linear", "attn_decay", "ffn_linear", "attn_gqa", "ffn_gated", "attn_bilinear", "ffn_gated"]


def ds(start, size):
    return bass.ds(start, size)


class Core:

    def __init__(self, nc, ctx, dram):
        self.nc, self.ctx, self.dram = nc, ctx, dram
        self.names = 0
        self.sems, self.open_sems = ExitStack(), []
        self.x = self.sbuf(ctx, "x", [P, B * TB, C])
        self.xT = self.sbuf(ctx, "xT", [P, B * T])
        self.ident = self.sbuf(ctx, "ident", [P, P])
        self.ident16 = self.sbuf(ctx, "ident16", [P, P], BF16)
        self.mask_ij = self.sbuf(ctx, "mask_ij", [P, P], BF16)
        self.mask_ji = self.sbuf(ctx, "mask_ji", [P, P], BF16)
        self.ones_row = self.sbuf(ctx, "ones_row", [1, P])
        self.minus_half = self.sbuf(ctx, "minus_half", [P, TB])
        self.stats = self.sbuf(ctx, "stats", [P, TB, 6])
        self.mean_var = self.sbuf(ctx, "mean_var", [P, TB, 2])
        self.var_eps = self.sbuf(ctx, "var_eps", [P, TB])
        self.pause = self.sbuf(ctx, "pause", [1, 1])
        self.rstd = self.sbuf(ctx, "rstd", [P, TB])
        self.xn = self.sbuf(ctx, "xn", [P, TB, C])

    def sbuf(self, ctx, name, shape, dtype=F32):
        self.names += 1
        return ctx.enter_context(self.nc.sbuf_tensor(f"{name}_{self.names}", shape, dtype))

    def psum(self, ctx, name, shape, dtype=F32):
        self.names += 1
        return ctx.enter_context(self.nc.psum_tensor(f"{name}_{self.names}", shape, dtype))

    def sem(self, name):
        self.names += 1
        made = self.sems.enter_context(self.nc.semaphore(f"{name}_{self.names}"))
        self.open_sems.append(made)
        return made

    def end_stage(self):
        numbers = sorted(s.num for s in self.open_sems)
        with self.nc.Block() as block:
            @block.sync
            def _(sp):
                first = numbers[0]
                for n, after in zip(numbers, numbers[1:] + [None]):
                    if after != n + 1:
                        sp.sem_clear(range(first, n + 1))
                        first = after
        self.sems.close()
        self.open_sems = []


class Count:

    def __init__(self, sem):
        self.sem, self.base, self.n = sem, 0, 0

    def at(self, base):
        self.base, self.n = base, 0

    def inc(self, instruction):
        instruction.then_inc(self.sem, 1)
        self.n += 1

    def settle(self, engine):
        engine.wait_ge(self.sem, self.base + self.n)



def norm_stats(nc, dve, core, chain, b):
    nc.vector.memset(core.pause[:, :], 0.0)
    for j in range(TB):
        last = nc.vector.bn_stats(core.stats[:, j, :], core.x[:, ds(b * TB + j, 1), :].rearrange("p a c -> p (a c)"))
    chain.inc(last)
    chain.settle(dve)
    nc.vector.memset(core.pause[:, :], 0.0)
    for j in range(TB):
        last = nc.vector.bn_aggr(core.mean_var[:, j, :], core.stats[:, j, :])
    chain.inc(last)
    chain.settle(dve)
    return nc.vector.tensor_scalar(core.var_eps[:, :], core.mean_var[:, :, 1], EPS, None, ALU.add)


def norm_rstd(nc, core):
    return nc.gpsimd.tensor_tensor(core.rstd[:, :], core.var_eps[:, :], core.minus_half[:, :], ALU.pow)


def norm_apply(nc, core, b):
    for j in range(TB):
        last = nc.vector.tensor_scalar(core.xn[:, j, :], core.x[:, ds(b * TB + j, 1), :].rearrange("p a c -> p (a c)"),
                                       core.mean_var[:, j, 0:1], core.rstd[:, j:j + 1], ALU.subtract, ALU.mult)
    return last


def norm_turn(nc, core, out):
    for j in range(TB):
        last = nc.tensor.transpose(out[:, j * P:(j + 1) * P], core.xn[:, j, :], core.ident[:, :])
    return last



def stage_load(core):
    nc, d = core.nc, core.dram
    loaded, const_loaded = core.sem("x_loaded"), core.sem("const_loaded")
    made = core.sem("constants_made")
    chain = Count(core.sem("load_chain"))
    var_ready, rstd_ready, xn_ready = core.sem("var_ready"), core.sem("rstd_ready"), core.sem("xn_ready")
    turned, taken = core.sem("turned"), core.sem("taken")
    x_tokens = d["x"].rearrange("b (j p) c -> p (b j) c", p=P)
    with ExitStack() as ctx:
        bank = core.psum(ctx, "turn_bank", [P, 2, T])
        block = ctx.enter_context(nc.Block())

        @block.sync
        def _(sp):
            sp.dma_start(core.ident[:, :], d["ident"]).then_inc(const_loaded, 16)
            sp.dma_start(core.ident16[:, :], d["ident16"]).then_inc(const_loaded, 16)
            sp.dma_start(core.mask_ij[:, :], d["mask_ij"]).then_inc(const_loaded, 16)
            sp.dma_start(core.mask_ji[:, :], d["mask_ji"]).then_inc(const_loaded, 16)
            sp.dma_start(core.x[:, :, :], x_tokens).then_inc(loaded, 16)

        @block.gpsimd
        def _(pool):
            nc.gpsimd.memset(core.minus_half[:, :], -0.5).then_inc(made, 1)
            nc.gpsimd.memset(core.ones_row[:, :], 1.0).then_inc(made, 1)
            pool.wait_ge(made, 2)
            with pool.Fori(0, B) as b:
                pool.wait_ge(var_ready, b + 1)
                norm_rstd(nc, core).then_inc(rstd_ready, 1)

        @block.vector
        def _(dve):
            dve.wait_ge(loaded, 16)
            with dve.Fori(0, B) as b:
                chain.at(b * NORM_STEPS)
                norm_stats(nc, dve, core, chain, b).then_inc(var_ready, 1)
                dve.wait_ge(rstd_ready, b + 1)
                dve.wait_ge(turned, b + 1)
                norm_apply(nc, core, b).then_inc(xn_ready, 1)

        @block.tensor
        def _(pe):
            pe.sem_inc(turned, 1)
            pe.wait_ge(const_loaded, 64)
            with pe.Fori(0, B // 2) as i:
                for u in range(2):
                    b = i * 2 + u
                    pe.wait_ge(xn_ready, b + 1)
                    pe.wait_ge(taken, b + 1)
                    norm_turn(nc, core, bank[:, u, :]).then_inc(turned, 1)

        @block.scalar
        def _(act):
            act.sem_inc(taken, 1)
            with act.Fori(0, B // 2) as i:
                for u in range(2):
                    b = i * 2 + u
                    act.wait_ge(turned, b + 2)
                    nc.scalar.copy(core.xT[:, ds(b * T, T)], bank[:, u, :]).then_inc(taken, 1)


def stage_store(core):
    nc = core.nc
    stored = core.sem("x_stored")
    with nc.Block() as block:
        @block.sync
        def _(sp):
            sp.dma_start(core.dram["out"].rearrange("b (j p) c -> p (b j) c", p=P), core.x[:, :, :]).then_inc(stored, 16)
            sp.wait_ge(stored, 16)



HIGH, MIDDLE_PART, LOW = 0, 1, 2
Q_PARTS = (HIGH, MIDDLE_PART, LOW, HIGH, MIDDLE_PART, HIGH)
K_PARTS = (HIGH, HIGH, HIGH, MIDDLE_PART, MIDDLE_PART, LOW)
MAX_PARTS = 2


class Attention:

    def __init__(self, heads, dim, kv_heads, causal, rope, bias, gate):
        self.heads, self.dim, self.kv_heads = heads, dim, kv_heads
        self.causal, self.rope, self.bias, self.gate = causal, rope, bias, gate
        self.groups = 4
        self.per_group = heads // self.groups
        self.stride = P // self.per_group
        self.width = heads * dim
        self.halves = self.width // P
        self.kv_width = kv_heads * dim
        self.scale = float(dim) ** -0.5
        self.lanes = 2 if len(Q_PARTS) * dim <= P // 2 else 1
        self.lane = P // self.lanes
        per_chunk = self.lane // dim
        self.chunk_parts = [range(c, min(c + per_chunk, len(Q_PARTS))) for c in range(0, len(Q_PARTS), per_chunk)]
        self.chunks = len(self.chunk_parts)
        self.max_row = len(self.chunk_parts[-1]) * dim
        cuts = [[0], [1, 3], [2]] if causal else [[0], [1], [2], [3]]
        self.ops = [(r, cut) for r in range(self.per_group) for cut in cuts]
        self.units = [(j, r) for j in range(TB) for r in range(self.per_group)]
        self.tiles = [("k", 0)] + [("q", c) for c in range(self.halves)]

    def khead(self, h):
        return h * self.kv_heads // self.heads

    def segments(self, cut):
        at, out = 0, []
        for j in cut:
            first = j if self.causal else 0
            out.append((j, first, at))
            at += (TB - first) * P
        return out, at

    def lane_rows(self, head, chunk, with_maximum):
        first = (head % self.lanes) * self.lane
        n = len(self.chunk_parts[chunk]) * self.dim
        return slice(first, first + n + (MAX_PARTS if with_maximum and chunk == self.chunks - 1 else 0))

    def prep(self):
        items = [(what, at, s) for what, at in self.tiles for s in range(1 + self.rope)]
        if self.gate:
            return items + [("v", 0, 0), ("v", 1, 0), ("gate", 0, 0), ("gate", 1, 0)]
        return items + [("v", 0, 0)]

    def v_blocks(self, at):
        return range(at * TB // 2, (at + 1) * TB // 2) if self.gate else range(TB)

    def end(self):
        return [("turn_out", self.groups - 1, 0)] + [("turn_y", h, 0) for h in range(self.halves)] + [("project", 0, 0), ("norm", 0, 0)]

    def batch_of(self, item, b, g):
        if item[0] == "turn_out" and g > 0:
            return b
        return b - 1 if item in self.end() else b + 1

    def plan(self, epilogue, prep):
        n_ops = len(self.ops)
        slots = [[[] for _ in range(n_ops)] for _ in range(self.groups)]
        if epilogue:
            for n, item in enumerate([("turn_y", h, 0) for h in range(self.halves)] + [("project", 0, 0)]):
                slots[0][min(2 + n, n_ops - 1)].append(item)
            slots[1][2].append(("norm", 0, 0))
        if prep:
            places = [(g, k) for g in range(2) for k in range(n_ops) if (g, k) >= (0, n_ops // 2)]
            items = self.prep()
            for n, item in enumerate(items):
                g, k = places[n * len(places) // len(items)]
                slots[g][k].append(item)
        for g in range(0 if epilogue else 1, self.groups):
            slots[g][1].insert(0, ("turn_out", (g - 1) % self.groups, 0))
        return slots


def stage_attention(core, cfg, w):
    nc = core.nc
    G, HG, D, NOPS, NUNITS = cfg.groups, cfg.per_group, cfg.dim, len(cfg.ops), len(cfg.units)
    KV, ST, QT, CH = cfg.kv_heads, cfg.stride, cfg.heads // cfg.lanes, cfg.chunks
    KT = max(KV // cfg.lanes, 1)
    TILES = len(cfg.tiles)
    SLOTS = 4
    SCORE_BANKS = 3
    MAX_TILES = HG // cfg.lanes
    PREP = cfg.prep()
    ENDS = len(cfg.end())
    TURNS = G * MAX_TILES
    MIDDLE = len(PREP) + ENDS + TURNS + G - 1
    BEFORE = len(PREP) + MAX_TILES
    assert MIDDLE % 2 == 0

    names = ("weights_loaded", "cleared", "xcur_even", "xcur_odd", "max_high_ready", "spare_full_even", "spare_full_odd",
             "spare_free_even", "spare_free_odd", "flat_ready", "parts_ready", "stacks_even", "stacks_odd",
             "max_full", "max_free", "max_parts_ready", "scores_full", "exp_done", "pv_done", "out_copied", "recip_ready",
             "gated", "var_ready", "rstd_ready", "xn_ready", "gate_sum_ready", "gate_recip_ready", "gate_ready")
    (weights_loaded, cleared, xcur_even, xcur_odd, max_high_ready, spare_full_even, spare_full_odd,
     spare_free_even, spare_free_odd, flat_ready, parts_ready, stacks_even, stacks_odd,
     max_full, max_free, max_parts_ready, scores_full, exp_done, pv_done, out_copied, recip_ready,
     gated, var_ready, rstd_ready, xn_ready, gate_sum_ready, gate_recip_ready, gate_ready) = (core.sem(n) for n in names)
    xcur_ready, stacks_ready = [xcur_even, xcur_odd], [stacks_even, stacks_odd]
    spare_full, spare_free = [spare_full_even, spare_full_odd], [spare_free_even, spare_free_odd]
    parts_written = [core.sem(f"parts_written_{what}{at}") for what, at in cfg.tiles]
    split_chain, chain = Count(core.sem("split_chain")), Count(core.sem("end_chain"))
    SPLIT_STEPS = 1 + cfg.rope

    def slot(b, n):
        if isinstance(b, int) and b < 0:
            return n % 2, n // 2
        if isinstance(b, int) and b == 0:
            return (BEFORE + n) % 2, (BEFORE + n) // 2
        n += BEFORE + MIDDLE - ENDS
        return n % 2, (b - 1) * (MIDDLE // 2) + n // 2

    LAST = ENDS + TURNS - MAX_TILES + G - 1

    def full(eng, b, n):
        bank, nth = slot(b, n)
        eng.wait_ge(spare_full[bank], nth + 1)

    def out_of_bank(eng, b, n):
        bank, nth = slot(b, n)
        eng.wait_ge(spare_free[bank], nth + 1)

    def bodies(eng, emit):
        emit(0, 0, False, True)
        with eng.Fori(0, (B - 2) // 2) as i:
            emit(i * 2 + 1, 1, True, True)
            emit(i * 2 + 2, 0, True, True)
        emit(B - 1, 1, True, False)

    def units_at(o):
        n = NOPS - 1
        return range(o * NUNITS // n, (o + 1) * NUNITS // n) if o < n else range(0)

    def score_bank_before(n, o):
        if o >= SCORE_BANKS:
            return n * NOPS + o - SCORE_BANKS + 1
        if isinstance(n, int) and n == 0:
            return None
        user = max(u for u in range(NOPS) if u % SCORE_BANKS == o % SCORE_BANKS)
        return (n - 1) * NOPS + user + 1

    def copies(what):
        out = []
        for lane in range(cfg.lanes):
            for c, numbers in enumerate(cfg.chunk_parts):
                for k, number in enumerate(numbers):
                    row = lane * cfg.lane + k * D
                    out.append((slice(row, row + D), c, (Q_PARTS if what == "q" else K_PARTS)[number], lane))
        return out

    READS = len(copies("q")) * cfg.halves + len(copies("k"))

    with ExitStack() as ctx:
        def sb(name, shape, dtype=F32):
            return core.sbuf(ctx, name, shape, dtype)

        wq, wk = sb("wq", [P, 1 + cfg.rope, cfg.halves, P]), sb("wk", [P, 1 + cfg.rope, P])
        wv, wo = sb("wv", [P, KV * D]), sb("wo", [P, cfg.halves, C])
        if cfg.rope:
            cos, sin = sb("cos", [P, T]), sb("sin", [P, T])
            turned = sb("turned", [P, 2, 2, T])
            qbias, kbias = sb("qbias", [P, 2, cfg.halves]), sb("kbias", [P, 2])
        if cfg.bias:
            vbias, obias = sb("vbias", [1, C]), sb("obias", [1, C])
        if cfg.gate:
            wg = sb("wg", [P, cfg.width])
            gate, gate_sig = sb("gate", [P, 2, TB, cfg.width]), sb("gate_sig", [P, TB, cfg.width])
        xcur = sb("xcur", [P, 2, T])
        flat, rest = sb("flat", [P, 2, T]), sb("rest", [P, T])
        parts = sb("parts", [P, TILES, 3, T], BF16)
        q, k = sb("q", [P, 2, CH, QT, T], BF16), sb("k", [P, 2, CH, KT, T], BF16)
        keep = sb("keep", [P, 1])
        v = sb("v", [P, 2, TB, KV, ST])
        v_cols = v[:].rearrange("p b j h d -> p (b j h) d")
        out_T = sb("out_T", [P, T])
        maxima = sb("maxima", [P, TB, HG])
        max_parts = sb("max_parts", [P, TB, MAX_TILES, P], BF16)
        max_cols = max_parts[:].rearrange("p j t (e s) -> p j (t e) s", e=cfg.lanes)
        probs = sb("probs", [P, SLOTS, T])
        recip = sb("recip", [P, 2, TB, HG])
        y, yT = sb("y", [P, TB, cfg.width]), sb("yT", [P, cfg.halves, T])

        max_bank = core.psum(ctx, "max_bank", [P, 2, T])
        score_bank = core.psum(ctx, "score_bank", [P, SCORE_BANKS, T])
        out_bank = core.psum(ctx, "out_bank", [P, T])
        spare_banks = core.psum(ctx, "spare_banks", [P, 2, T])

        KW = cfg.kv_width
        loads = [(keep[:, :], w["keep"]), (wv[:, :], w["wv"]), (wo[:, :, :], w["wo"].rearrange("(h p) c -> p h c", p=P))]
        for place in range(2):
            for lane in range(cfg.lanes):
                row = lane * cfg.lane + cfg.max_row
                loads.append((k[row:row + MAX_PARTS, place, CH - 1], w["minus"]))
        for sw in range(1 + cfg.rope):
            tail = "_swap" if sw else ""
            loads.append((wq[:, sw], w["wq" + tail].rearrange("c (h p) -> c h p", p=P)))
            loads.append((wk[:, sw, 0:KW], w["wk" + tail]))
            if cfg.bias and cfg.rope:
                loads.append((qbias[:, sw, :], w["bq" + tail].rearrange("(p h) -> p h", h=1)))
                loads.append((kbias[:, sw:sw + 1], w["bk" + tail].rearrange("(p h) -> p h", h=1)))
        if cfg.rope:
            loads += [(cos[:, :], w["cos"]), (sin[:, :], w["sin"])]
        if cfg.bias:
            loads += [(vbias[:, :], w["bv"].rearrange("(a c) -> a c", a=1)), (obias[:, :], w["bo"].rearrange("(a c) -> a c", a=1))]
        if cfg.gate:
            loads.append((wg[:, :], w["wg"]))
        LOADED = 16 * len(loads)
        clears = [(max_parts[:], 0.0), (q[:, :, CH - 1], 0.0), (v_cols[:, :, D:D + 1], 1.0), (v_cols[:, :, D + 1:ST], 0.0)]
        if KW < P:
            clears.append((wk[:, :, KW:P], 0.0))
        if cfg.rope and not cfg.bias:
            clears += [(qbias[:], 0.0), (kbias[:], 0.0)]

        block = ctx.enter_context(nc.Block())

        @block.sync
        def _(sp):
            sp.dma_start(xcur[:, 0, :], core.xT[:, 0:T]).then_inc(xcur_ready[0], 16)
            for dst, src in loads:
                sp.dma_start(dst, src).then_inc(weights_loaded, 16)
            sp.dma_start(xcur[:, 1, :], core.xT[:, T:2 * T]).then_inc(xcur_ready[1], 16)

            def stack(b, place):
                for t in range(TILES):
                    sp.wait_ge(parts_ready, b * TILES + t + 1)
                    rows = KW if t == 0 else P
                    sp.dma_start(w["scratch"][place, t, :, 0:rows].rearrange("s p t -> p s t"), parts[0:rows, t])\
                      .then_inc(parts_written[t], 16)
                if not (isinstance(b, int) and b < 2):
                    sp.wait_ge(scores_full, (b - 1) * (G * NOPS))
                for what, tiles, width in (("k", k, KW), ("q", q, P)):
                    for t in range(1 if what == "k" else cfg.halves):
                        written = t + (what == "q")
                        sp.wait_ge(parts_written[written], b * 16 + 16)
                    for rows, c, part, lane in copies(what):
                        if what == "k":
                            src = w["scratch"][place, 0, part, 0:KW].rearrange("(h e d) t -> e d h t", e=cfg.lanes, d=D)[lane]
                            sp.dma_start(k[rows, place, c], src).then_inc(stacks_ready[place], 16)
                        else:
                            heads = QT // cfg.halves
                            src = w["scratch"][place, 1:1 + cfg.halves, part].rearrange(
                                "a (h e d) t -> e d a h t", e=cfg.lanes, d=D)[lane]
                            for a in range(cfg.halves):
                                sp.dma_start(q[rows, place, c, a * heads:(a + 1) * heads], src[:, a])\
                                  .then_inc(stacks_ready[place], 16)

            def refill(b, place):
                full(sp, b, -1)
                sp.dma_start(xcur[:, place, :], core.xT[:, ds((b + 2) * T, T)]).then_inc(xcur_ready[place], 16)

            sp.wait_ge(cleared, len(clears))
            stack(0, 0)
            refill(0, 0)
            stack(1, 1)
            with sp.Fori(0, (B - 4) // 2) as i:
                refill(i * 2 + 1, 1)
                stack(i * 2 + 2, 0)
                refill(i * 2 + 2, 0)
                stack(i * 2 + 3, 1)
            refill(B - 3, 1)
            stack(B - 2, 0)
            stack(B - 1, 1)
            for t in range(TILES):
                sp.wait_ge(parts_written[t], 16 * B)
            for place in range(2):
                sp.wait_ge(stacks_ready[place], 16 * READS * (B // 2))

        @block.tensor
        def _(pe):
            def bank_item(body, n, b, item, place):
                what, at, swapped = item
                bank, nth = slot(body, n)
                spare = spare_banks[:, bank, :]
                if not (isinstance(nth, int) and nth == 0):
                    pe.wait_ge(spare_free[bank], nth)
                if item == PREP[0]:
                    pe.wait_ge(xcur_ready[place], (b - place) * 8 + 16)
                if what in "qk":
                    weights = wq[:, swapped, at, :] if what == "q" else wk[:, swapped, :]
                    last = nc.tensor.matmul(spare, weights, xcur[:, place, :], start=True, stop=True)
                elif what == "v":
                    width = KV * D
                    for m, j in enumerate(cfg.v_blocks(at)):
                        out = spare[:, m * width:(m + 1) * width]
                        last = nc.tensor.matmul(out, xcur[:, place, j * P:(j + 1) * P], wv[:, :], start=True, stop=not cfg.bias)
                        if cfg.bias:
                            last = nc.tensor.matmul(out, core.ones_row[:, :], vbias[:, :], start=False, stop=True)
                elif what == "gate":
                    width = cfg.width
                    for j in range(2):
                        last = nc.tensor.matmul(spare[:, j * width:(j + 1) * width],
                                                xcur[:, place, (2 * at + j) * P:(2 * at + j + 1) * P],
                                                wg[:, :], start=True, stop=True)
                elif what == "turn_out":
                    pe.wait_ge(out_copied, b * G + at + 1)
                    for j in range(TB):
                        last = nc.tensor.transpose(spare[:, j * P:(j + 1) * P], out_T[:, j * P:(j + 1) * P], core.ident[:, :])
                elif what == "turn_y":
                    if at == 0 and cfg.gate:
                        pe.wait_ge(gated, b + 1)
                    elif at == 0:
                        out_of_bank(pe, body, n - 1)
                    for j in range(TB):
                        last = nc.tensor.transpose(spare[:, j * P:(j + 1) * P], y[:, j, at * P:(at + 1) * P], core.ident[:, :])
                elif what == "project":
                    out_of_bank(pe, body, n - 1)
                    for j in range(TB):
                        out = spare[:, j * P:(j + 1) * P]
                        for h in range(cfg.halves):
                            last = nc.tensor.matmul(out, yT[:, h, j * P:(j + 1) * P], wo[:, h, :], start=(h == 0),
                                                    stop=(h == cfg.halves - 1 and not cfg.bias))
                        if cfg.bias:
                            last = nc.tensor.matmul(out, core.ones_row[:, :], obias[:, :], start=False, stop=True)
                elif what == "norm":
                    pe.wait_ge(xn_ready, b + 1)
                    last = norm_turn(nc, core, spare)
                last.then_inc(spare_full[bank], 1)

            def unit(n, g, place, u):
                j, r = cfg.units[u]
                h = g * HG + r
                if not (isinstance(n, int) and n == 0 and u < 2):
                    pe.wait_ge(max_free, n * NUNITS + u - 1)
                cols = (j + 1) * P if cfg.causal else T
                bank = max_bank[:, u % 2, :]
                for c in range(CH):
                    rows = cfg.lane_rows(h, c, False)
                    last = nc.tensor.matmul(bank[:, 0:cols], q[rows, place, c, h // cfg.lanes, j * P:(j + 1) * P],
                                            k[rows, place, c, cfg.khead(h) // cfg.lanes, 0:cols],
                                            start=(c == 0), stop=(c == CH - 1 and not cfg.causal))
                if cfg.causal:
                    last = nc.tensor.matmul(bank[:, j * P:(j + 1) * P], core.ident16[:, :], core.mask_ij[:, :],
                                            start=False, stop=True)
                last.then_inc(max_full, 1)

            def turn_maxima(body, first, n):
                pe.wait_ge(max_parts_ready, n + 1)
                for m in range(MAX_TILES):
                    bank, nth = slot(body, first + m)
                    pe.wait_ge(spare_free[bank], nth)
                    for j in range(TB):
                        last = nc.tensor.matmul(spare_banks[:, bank, j * P:(j + 1) * P], max_parts[:, j, m, :],
                                                core.ident16[:, :], start=True, stop=True)
                    last.then_inc(spare_full[bank], 1)

            def scores(n, g, place, o, maxima_items):
                r, cut = cfg.ops[o]
                h = g * HG + r
                if o == 0:
                    for m in range(MAX_TILES):
                        out_of_bank(pe, maxima_items[0], maxima_items[1] + m)
                before = score_bank_before(n, o)
                if before is not None:
                    pe.wait_ge(exp_done, before)
                for j, first, at in cfg.segments(cut)[0]:
                    width = T - first * P
                    bank = score_bank[:, o % SCORE_BANKS, at:at + width]
                    for c in range(CH):
                        rows = cfg.lane_rows(h, c, True)
                        last = nc.tensor.matmul(bank, k[rows, place, c, cfg.khead(h) // cfg.lanes, j * P:(j + 1) * P],
                                                q[rows, place, c, h // cfg.lanes, first * P:T],
                                                start=(c == 0), stop=(c == CH - 1 and not cfg.causal))
                    if cfg.causal:
                        last = nc.tensor.matmul(bank[:, 0:P], core.ident16[:, :], core.mask_ji[:, :],
                                                start=False, stop=True)
                last.then_inc(scores_full, 1)

            def values(n, g, place, o):
                r, cut = cfg.ops[o]
                pe.wait_ge(exp_done, n * NOPS + o + 1)
                if o == 0 and not (isinstance(n, int) and n == 0):
                    pe.wait_ge(out_copied, n)
                for j, first, at in cfg.segments(cut)[0]:
                    last = nc.tensor.matmul(out_bank[ST * r:ST * (r + 1), first * P:T], v[:, place, j, cfg.khead(g * HG + r), :],
                                            probs[:, (g * NOPS + o) % SLOTS, at:at + T - first * P],
                                            start=(j == 0), stop=(cut == cfg.ops[-1][1] and j == cut[-1]),
                                            skip_group_check=True)
                last.then_inc(pv_done, 1)

            def body(b, place, epilogue, prep):
                plan = cfg.plan(epilogue, prep)
                index = 0
                if isinstance(b, int) and b == 0:
                    maxima_items = (-1, len(PREP))
                else:
                    maxima_items = (b, -MAX_TILES)
                for g in range(G):
                    n = b * G + g
                    more = prep or g < G - 1
                    g1, place1, b1 = (g + 1, place, b) if g < G - 1 else (0, 1 - place, b + 1)
                    for o in range(NOPS):
                        scores(n, g, place, o, maxima_items)
                        if more:
                            if o == 0 and g == G - 1:
                                pe.wait_ge(stacks_ready[place1], (b1 - place1) * (8 * READS) + 16 * READS)
                            for u in units_at(o):
                                unit(n + 1, g1, place1, u)
                        for item in plan[g][o]:
                            bank_item(b, index, cfg.batch_of(item, b, g), item, 1 - place)
                            index += 1
                        if o > 0:
                            values(n, g, place, o - 1)
                        elif g > 0:
                            values(n - 1, g - 1, place, NOPS - 1)
                        elif epilogue:
                            values(n - 1, G - 1, 1 - place, NOPS - 1)
                    if more:
                        turn_maxima(b, index, n + 1)
                        maxima_items = (b, index)
                        index += MAX_TILES

            pe.wait_ge(weights_loaded, LOADED)
            pe.wait_ge(cleared, len(clears))
            for n, item in enumerate(PREP):
                bank_item(-1, n, 0, item, 0)
            pe.wait_ge(stacks_ready[0], 16 * READS)
            for u in range(NUNITS):
                unit(0, 0, 0, u)
            turn_maxima(-1, len(PREP), 0)
            bodies(pe, body)
            values(B * G - 1, G - 1, 1, NOPS - 1)
            for n, item in enumerate(cfg.end()):
                bank_item(B - 1, LAST + n, B - 1, item, 1)

        @block.scalar
        def _(act):
            def bank_item(body, n, b, item, place, tile):
                what, at, swapped = item
                bank, nth = slot(body, n)
                spare = spare_banks[:, bank, :]
                if what in ("turn_y", "norm", "v", "gate") or (what in "qk" and not cfg.rope):
                    act.wait_ge(spare_full[bank], nth + 1)
                if what == "turn_y":
                    nc.scalar.copy(yT[:, at, :], spare).then_inc(spare_free[bank], 1)
                elif what == "norm":
                    nc.scalar.copy(core.xT[:, ds(b * T, T)], spare).then_inc(spare_free[bank], 1)
                elif what == "v":
                    blocks = cfg.v_blocks(at)
                    nc.scalar.copy(v[:, place, blocks[0]:blocks[-1] + 1, :, 0:D],
                                   spare[:, 0:len(blocks) * KV * D].rearrange("p (j h d) -> p j h d", j=len(blocks), h=KV))\
                      .then_inc(spare_free[bank], 1)
                elif what == "gate":
                    raw = spare.rearrange("p (j c) -> p j c", j=2)
                    nc.scalar.activation(gate_sig[:, 2 * at:2 * at + 2, :], raw, ACT.Exp, scale=-1.0)
                    nc.scalar.copy(gate[:, place, 2 * at:2 * at + 2, :], raw).then_inc(spare_free[bank], 1)
                elif what in "qk" and not cfg.rope:
                    if not (isinstance(b, int) and b == 0):
                        act.wait_ge(parts_ready, b * TILES)
                    nc.scalar.copy(flat[:, tile, :], spare)
                    if not (isinstance(b, int) and b == 0):
                        act.wait_ge(parts_written[tile], b * 16)
                    nc.scalar.copy(parts[:, tile, HIGH], spare).then_inc(spare_free[bank], 1)
                    return 1
                return 0

            def exponentials(n, g, o):
                width = cfg.segments(cfg.ops[o][1])[1]
                act.wait_ge(scores_full, n * NOPS + o + 1)
                if not (isinstance(n, int) and n * NOPS + o < SLOTS):
                    act.wait_ge(pv_done, n * NOPS + o + 1 - SLOTS)
                nc.scalar.activation(probs[:, (g * NOPS + o) % SLOTS, 0:width], score_bank[:, o % SCORE_BANKS, 0:width], ACT.Exp,
                                     scale=cfg.scale).then_inc(exp_done, 1)

            def copy_outputs(n):
                act.wait_ge(pv_done, (n + 1) * NOPS)
                if not (isinstance(n, int) and n == 0):
                    act.wait_ge(recip_ready, n)
                nc.scalar.copy(out_T[:, :], out_bank[:, :]).then_inc(out_copied, 1)

            def body(b, place, epilogue, prep):
                plan = cfg.plan(epilogue, prep)
                index = tile = 0
                for g in range(G):
                    for o in range(NOPS):
                        exponentials(b * G + g, g, o)
                        if o == 0 and (g > 0 or epilogue):
                            copy_outputs(b * G + g - 1)
                        for item in plan[g][o]:
                            tile += bank_item(b, index, cfg.batch_of(item, b, g), item, 1 - place, tile)
                            index += 1
                    index += MAX_TILES

            tile = 0
            act.wait_ge(cleared, len(clears))
            for n, item in enumerate(PREP):
                tile += bank_item(-1, n, 0, item, 0, tile)
            bodies(act, body)
            copy_outputs(B * G - 1)
            for n, item in enumerate(cfg.end()):
                bank_item(B - 1, LAST + n, B - 1, item, 1, 0)

        @block.gpsimd
        def _(pool):
            for tile, value in clears:
                nc.gpsimd.memset(tile, value).then_inc(cleared, 1)

            def split(body, n, b, tile):
                whole, mine = flat[:, tile % 2, :], parts[:, tile]
                split_chain.at((b * TILES + tile) * SPLIT_STEPS)
                out_of_bank(pool, body, n)
                if cfg.rope:
                    if not (isinstance(b, int) and b == 0):
                        pool.wait_ge(parts_written[tile], b * 16)
                    nc.gpsimd.tensor_tensor(mine[:, HIGH], turned[:, tile % 2, 0, :], turned[:, tile % 2, 1, :], ALU.add)
                    split_chain.inc(nc.gpsimd.tensor_tensor(whole, turned[:, tile % 2, 0, :], turned[:, tile % 2, 1, :], ALU.add))
                    split_chain.settle(pool)
                elif not (isinstance(b, int) and b == 0 and tile == 0):
                    pool.wait_ge(parts_ready, b * TILES + tile)
                nc.gpsimd.tensor_tensor(mine[:, MIDDLE_PART], whole, mine[:, HIGH], ALU.subtract)
                split_chain.inc(nc.gpsimd.tensor_tensor(rest[:, :], whole, mine[:, HIGH], ALU.subtract))
                split_chain.settle(pool)
                nc.gpsimd.tensor_tensor(mine[:, LOW], rest[:, :], mine[:, MIDDLE_PART], ALU.subtract).then_inc(parts_ready, 1)

            def bank_item(body, n, b, item, place, tile):
                what, at, swapped = item
                if what in "qk" and swapped == cfg.rope:
                    split(body, n, b, tile)
                    return 1
                if what == "gate" and at == 1:
                    pool.wait_ge(gate_recip_ready, b + 1)
                    nc.gpsimd.tensor_tensor(gate[:, place], gate[:, place], gate_sig[:, :, :], ALU.mult).then_inc(gate_ready, 1)
                if what == "turn_out" and at == G - 1 and cfg.gate:
                    out_of_bank(pool, body, n)
                    pool.wait_ge(gate_ready, b + 1)
                    nc.gpsimd.tensor_tensor(y[:, :, :], y[:, :, :], gate[:, place], ALU.mult).then_inc(gated, 1)
                if what == "project":
                    pool.wait_ge(var_ready, b + 1)
                    norm_rstd(nc, core).then_inc(rstd_ready, 1)
                return 0

            def body(b, place, epilogue, prep):
                plan = cfg.plan(epilogue, prep)
                index = tile = 0
                for g in range(G):
                    for o in range(NOPS):
                        for item in plan[g][o]:
                            tile += bank_item(b, index, cfg.batch_of(item, b, g), item, 1 - place, tile)
                            index += 1
                    index += MAX_TILES

            tile = 0
            for n, item in enumerate(PREP):
                tile += bank_item(-1, n, 0, item, 0, tile)
            bodies(pool, body)
            for n, item in enumerate(cfg.end()):
                bank_item(B - 1, LAST + n, B - 1, item, 1, 0)

        @block.vector
        def _(dve):
            def bank_item(body, n, b, item, place, tile):
                what, at, swapped = item
                bank, nth = slot(body, n)
                spare = spare_banks[:, bank, :]
                if what in "qk" and cfg.rope:
                    dve.wait_ge(spare_full[bank], nth + 1)
                    if not swapped and not (isinstance(b, int) and b == 0 and tile < 2):
                        dve.wait_ge(parts_ready, b * TILES + max(tile - 1, 0))
                    bias = qbias[:, swapped, at:at + 1] if what == "q" else kbias[:, swapped:swapped + 1]
                    nc.vector.scalar_tensor_tensor(turned[:, tile % 2, swapped, :], spare, bias,
                                                   (sin if swapped else cos)[:, :], ALU.add, ALU.mult).then_inc(spare_free[bank], 1)
                    return swapped
                if what == "gate" and at == 1:
                    out_of_bank(dve, body, n)
                    nc.vector.tensor_scalar(gate_sig[:, :, :], gate_sig[:, :, :], 1.0, None, ALU.add).then_inc(gate_sum_ready, 1)
                    dve.wait_ge(gate_sum_ready, b + 1)
                    nc.vector.reciprocal(gate_sig[:, :, :], gate_sig[:, :, :]).then_inc(gate_recip_ready, 1)
                if what == "turn_out":
                    take_outputs(bank, nth, b * G + at, at)
                if what == "project":
                    dve.wait_ge(spare_full[bank], nth + 1)
                    tokens = core.x[:, ds(b * TB, TB), :]
                    nc.vector.tensor_tensor(tokens, spare.rearrange("p (j c) -> p j c", j=TB), tokens, ALU.add)\
                      .then_inc(spare_free[bank], 1)
                    out_of_bank(dve, body, n)
                    chain.at(b * NORM_STEPS)
                    norm_stats(nc, dve, core, chain, b).then_inc(var_ready, 1)
                return 0

            def reduce(n, u):
                j, r = cfg.units[u]
                dve.wait_ge(max_full, n * NUNITS + u + 1)
                cols = (j + 1) * P if cfg.causal else T
                nc.vector.tensor_reduce(maxima[:, j, r:r + 1], max_bank[:, u % 2, 0:cols], AX_X, ALU.max).then_inc(max_free, 1)

            def split_maxima(n):
                dve.wait_ge(max_free, (n + 1) * NUNITS)
                high, rest_of = (max_cols[:, :, :, cfg.max_row + m] for m in range(MAX_PARTS))
                nc.vector.tensor_copy(high, maxima[:, :, :]).then_inc(max_high_ready, 1)
                dve.wait_ge(max_high_ready, n + 1)
                nc.vector.tensor_tensor(rest_of, maxima[:, :, :], high, ALU.subtract).then_inc(max_parts_ready, 1)

            def add_maxima(body, first, g, place):
                for m in range(MAX_TILES):
                    full(dve, body, first + m)
                    bank, _ = slot(body, first + m)
                    tile = q[:, place, CH - 1, g * MAX_TILES + m, :]
                    nc.vector.scalar_tensor_tensor(tile, tile, keep[:, 0:1], spare_banks[:, bank, :], ALU.mult, ALU.add)\
                      .then_inc(spare_free[bank], 1)

            def take_outputs(bank, nth, n, g):
                outs = spare_banks[:, bank, :].rearrange("p (j r d) -> p j r d", j=TB, r=HG)
                dve.wait_ge(spare_full[bank], nth + 1)
                nc.vector.reciprocal(recip[:, g % 2], outs[:, :, :, D]).then_inc(recip_ready, 1)
                dve.wait_ge(recip_ready, n + 1)
                mine = y[:, :, g * HG * D:(g + 1) * HG * D].rearrange("p j (r d) -> p j r d", r=HG)
                nc.vector.tensor_tensor(mine, outs[:, :, :, 0:D], recip[:, g % 2].unsqueeze(3).to_broadcast([P, TB, HG, D]),
                                        ALU.mult).then_inc(spare_free[bank], 1)

            def apply_norm(b):
                dve.wait_ge(rstd_ready, b + 1)
                norm_apply(nc, core, b).then_inc(xn_ready, 1)

            def body(b, place, epilogue, prep):
                plan = cfg.plan(epilogue, prep)
                index = tile = 0
                for g in range(G):
                    n = b * G + g
                    more = prep or g < G - 1
                    g1, place1 = (g + 1, place) if g < G - 1 else (0, 1 - place)
                    for o in range(NOPS):
                        if more:
                            for u in units_at(o):
                                reduce(n + 1, u)
                        if epilogue and g == 1 and o == 0:
                            apply_norm(b - 1)
                        if more and o == NOPS - 1:
                            split_maxima(n + 1)
                        for item in plan[g][o]:
                            tile += bank_item(b, index, cfg.batch_of(item, b, g), item, 1 - place, tile)
                            index += 1
                    if more:
                        add_maxima(b, index, g1, place1)
                        index += MAX_TILES

            dve.wait_ge(weights_loaded, LOADED)
            dve.wait_ge(cleared, len(clears))
            tile = 0
            for n, item in enumerate(PREP):
                tile += bank_item(-1, n, 0, item, 0, tile)
            for u in range(NUNITS):
                reduce(0, u)
            split_maxima(0)
            add_maxima(-1, len(PREP), 0, 0)
            bodies(dve, body)
            for n, item in enumerate(cfg.end()):
                bank_item(B - 1, LAST + n, B - 1, item, 1, 0)
            apply_norm(B - 1)



def choose(nc, dve, chain, left, scratch, order, best, top, onehot):
    shape = [P, B * TB, left.shape[2]]
    chain.inc(nc.vector.tensor_reduce(top, left, AX_X, ALU.max))
    chain.settle(dve)
    chain.inc(nc.vector.tensor_tensor(scratch, left, top.unsqueeze(2).to_broadcast(shape), ALU.is_equal))
    chain.settle(dve)
    chain.inc(nc.vector.tensor_tensor(scratch, scratch, order.unsqueeze(1).to_broadcast(shape), ALU.mult))
    chain.settle(dve)
    chain.inc(nc.vector.tensor_reduce(best, scratch, AX_X, ALU.max))
    chain.settle(dve)
    chain.inc(nc.vector.tensor_tensor(onehot, scratch, best.unsqueeze(2).to_broadcast(shape), ALU.is_equal))
    chain.settle(dve)


def stage_ffn(core, w, experts, hidden):
    nc = core.nc
    E = experts
    gated = hidden is not None
    CHUNKS = -(-hidden // P) if gated else 0
    H = [min(P, hidden - c * P) for c in range(CHUNKS)] if gated else []
    names = ("weights_loaded", "xcur_even", "xcur_odd", "order_ready", "logits_full", "diff_ready", "exp_ready",
             "up_full", "silu_done", "hidden_done", "down_full", "combined", "var_ready", "rstd_ready", "xn_ready",
             "turned", "taken", "mixed_full", "mixed_taken")
    (weights_loaded, xcur_even, xcur_odd, order_ready, logits_full, diff_ready, exp_ready, up_full, silu_done,
     hidden_done, down_full, combined, var_ready, rstd_ready, xn_ready, turned, taken, mixed_full,
     mixed_taken) = (core.sem(n) for n in names)
    xcur_ready = [xcur_even, xcur_odd]
    route_chain, chain = Count(core.sem("route_chain")), Count(core.sem("ffn_chain"))

    with ExitStack() as ctx:
        def sb(name, shape, dtype=F32):
            return core.sbuf(ctx, name, shape, dtype)

        N = B * TB
        router = sb("router", [P, E])
        logits, scratch = sb("logits", [P, N, E]), sb("scratch", [P, N, E])
        first, second, gates = sb("first", [P, N, E]), sb("second", [P, N, E]), sb("gates", [P, N, E])
        top, best = sb("top", [P, 2, N]), sb("best", [P, N])
        share, total = sb("share", [P, 2, N]), sb("total", [P, N])
        order = sb("order", [P, E])
        xcur = sb("xcur", [P, 2, T])
        loads = [(router[:, :], w["router"])]
        if gated:
            wg, wu, wd = sb("wg", [P, E, hidden]), sb("wu", [P, E, hidden]), sb("wd", [P, E, CHUNKS, C])
            silu, hid = sb("silu", [P, 2, T]), sb("hidden", [P, 2, CHUNKS, T])
            gate_bank, up_bank = core.psum(ctx, "gate_bank", [P, 2, T]), core.psum(ctx, "up_bank", [P, 2, T])
            loads += [(wg[:, :, :], w["wg"].rearrange("e c i -> c e i")), (wu[:, :, :], w["wu"].rearrange("e c i -> c e i"))]
            loads += [(wd[0:H[c], :, c, :], w["wd"][:, c * P:c * P + H[c], :].rearrange("e i c -> i e c")) for c in range(CHUNKS)]
        else:
            F = w["w_in"].shape[1] // P
            w_in, w_out, both = sb("w_in", [P, E, F, C]), sb("w_out", [P, E, F, C]), sb("w_both", [P, E, C])
            mixed_bank = core.psum(ctx, "mixed_bank", [P, 2, T])
            loads += [(w_in[:, :, :, :], w["w_in"].rearrange("e (f p) c -> p e f c", p=P)),
                      (w_out[:, :, :, :], w["w_out"].rearrange("e (f p) c -> p e f c", p=P))]
        down_bank = core.psum(ctx, "down_bank", [P, 2, T])
        logits_bank, norm_bank = core.psum(ctx, "logits_bank", [P, T]), core.psum(ctx, "norm_bank", [P, T])
        logits_view = logits_bank[:, 0:N * E].rearrange("p (n e) -> p n e", e=E)

        def bodies(eng, emit):
            emit(0, 0, True)
            with eng.Fori(0, (B - 2) // 2) as i:
                emit(i * 2 + 1, 1, False)
                emit(i * 2 + 2, 0, False)
            emit(B - 1, 1, False)

        def e_parity(place, e):
            return (place * E + e) % 2

        def chunk_parity(place, m):
            return (place * E * CHUNKS + m) % 2

        block = ctx.enter_context(nc.Block())

        @block.sync
        def _(sp):
            for dst, src in loads:
                sp.dma_start(dst, src).then_inc(weights_loaded, 16)
            for b in (0, 1):
                sp.dma_start(xcur[:, b, :], core.xT[:, b * T:(b + 1) * T]).then_inc(xcur_ready[b], 16)
            with sp.Fori(0, (B - 2) // 2) as i:
                for u in range(2):
                    sp.wait_ge(down_full, (i * 2 + u + 1) * E)
                    sp.dma_start(xcur[:, u, :], core.xT[:, ds((i * 2 + u + 2) * T, T)]).then_inc(xcur_ready[u], 16)

        @block.gpsimd
        def _(pool):
            nc.gpsimd.iota(order[:, :], pattern=[[-1, E]], base=E, channel_multiplier=0,
                           allow_small_or_imprecise_dtypes=True).then_inc(order_ready, 1)
            with pool.Fori(0, B) as b:
                pool.wait_ge(var_ready, b + 1)
                norm_rstd(nc, core).then_inc(rstd_ready, 1)

        @block.tensor
        def _(pe):
            def down(b, place, e):
                if not (isinstance(b, int) and b == 0 and e < 2):
                    pe.wait_ge(combined, b * E + e - 1)
                if gated:
                    pe.wait_ge(hidden_done, (b * E + e + 1) * CHUNKS)
                for j in range(TB):
                    out = down_bank[:, e_parity(place, e), j * C:(j + 1) * C]
                    if gated:
                        for c in range(CHUNKS):
                            last = nc.tensor.matmul(out, hid[0:H[c], e_parity(place, e), c, j * P:(j + 1) * P],
                                                    wd[0:H[c], e, c, :], start=(c == 0), stop=(c == CHUNKS - 1))
                    else:
                        last = nc.tensor.matmul(out, xcur[:, place, j * P:(j + 1) * P], both[:, e, :], start=True, stop=True)
                last.then_inc(down_full, 1)

            def up(b, place, e):
                for c in range(CHUNKS):
                    m = e * CHUNKS + c
                    if not (isinstance(b, int) and b == 0 and m < 2):
                        pe.wait_ge(hidden_done, b * E * CHUNKS + m - 1)
                    cols = slice(c * P, c * P + H[c])
                    bank = chunk_parity(place, m)
                    nc.tensor.matmul(gate_bank[0:H[c], bank, :], wg[:, e, cols], xcur[:, place, :], start=True, stop=True)
                    nc.tensor.matmul(up_bank[0:H[c], bank, :], wu[:, e, cols], xcur[:, place, :],
                                     start=True, stop=True).then_inc(up_full, 1)

            def turn(b):
                pe.wait_ge(xn_ready, b + 1)
                if not (isinstance(b, int) and b == 0):
                    pe.wait_ge(taken, b)
                norm_turn(nc, core, norm_bank).then_inc(turned, 1)

            def body(b, place, is_first):
                pe.wait_ge(xcur_ready[place], (b - place) * 8 + 16)
                if gated:
                    up(b, place, 0)
                for e in range(E):
                    if gated and e + 1 < E:
                        up(b, place, e + 1)
                    down(b, place, e)
                    if e == 1 and not is_first:
                        turn(b - 1)

            pe.wait_ge(weights_loaded, 16 * len(loads))
            for n in range(N):
                last = nc.tensor.matmul(logits_view[:, n, :], core.xT[:, n * P:(n + 1) * P], router[:, :], start=True, stop=True)
            last.then_inc(logits_full, 1)
            if not gated:
                for e in range(E):
                    if e >= 2:
                        pe.wait_ge(mixed_taken, e - 1)
                    for f in range(F):
                        last = nc.tensor.matmul(mixed_bank[:, e % 2, 0:C], w_in[:, e, f, :], w_out[:, e, f, :],
                                                start=(f == 0), stop=(f == F - 1))
                    last.then_inc(mixed_full, 1)
                pe.wait_ge(mixed_taken, E)
            bodies(pe, body)
            turn(B - 1)

        @block.scalar
        def _(act):
            if not gated:
                for e in range(E):
                    act.wait_ge(mixed_full, e + 1)
                    nc.scalar.copy(both[:, e, :], mixed_bank[:, e % 2, 0:C]).then_inc(mixed_taken, 1)
            act.wait_ge(diff_ready, 1)
            nc.scalar.activation(share[:, 1, :], share[:, 1, :], ACT.Exp).then_inc(exp_ready, 1)

            def take(b):
                act.wait_ge(turned, b + 1)
                nc.scalar.copy(core.xT[:, ds(b * T, T)], norm_bank[:, :]).then_inc(taken, 1)

            def body(b, place, is_first):
                for m in range(E * CHUNKS):
                    rows = H[m % CHUNKS]
                    bank = chunk_parity(place, m)
                    act.wait_ge(up_full, b * E * CHUNKS + m + 1)
                    if not (isinstance(b, int) and b == 0 and m < 2):
                        act.wait_ge(hidden_done, b * E * CHUNKS + m - 1)
                    nc.scalar.activation(silu[0:rows, bank, :], gate_bank[0:rows, bank, :], ACT.Silu).then_inc(silu_done, 1)
                    if m == 3 * CHUNKS and not is_first:
                        take(b - 1)
                if not gated and not is_first:
                    take(b - 1)

            bodies(act, body)
            take(B - 1)

        @block.vector
        def _(dve):
            def multiply(b, place, e):
                for c in range(CHUNKS):
                    m = e * CHUNKS + c
                    bank = chunk_parity(place, m)
                    if c == 0 and not (isinstance(b, int) and b == 0 and e < 2):
                        dve.wait_ge(down_full, b * E + e - 1)
                    dve.wait_ge(silu_done, b * E * CHUNKS + m + 1)
                    nc.vector.tensor_tensor(hid[0:H[c], e_parity(place, e), c, :], up_bank[0:H[c], bank, :],
                                            silu[0:H[c], bank, :], ALU.mult).then_inc(hidden_done, 1)

            def combine(b, place, e):
                dve.wait_ge(down_full, b * E + e + 1)
                if not (isinstance(b, int) and b == 0 and e == 0):
                    dve.wait_ge(combined, b * E + e)
                for j in range(TB):
                    tokens = core.x[:, ds(b * TB + j, 1), :].rearrange("p a c -> p (a c)")
                    last = nc.vector.scalar_tensor_tensor(
                        tokens, down_bank[:, e_parity(place, e), j * C:(j + 1) * C],
                        gates[:, ds(b * TB + j, 1), e:e + 1].rearrange("p a c -> p (a c)"), tokens, ALU.mult, ALU.add)
                last.then_inc(combined, 1)

            def body(b, place, is_first):
                if gated:
                    multiply(b, place, 0)
                for e in range(E):
                    if gated and e + 1 < E:
                        multiply(b, place, e + 1)
                    combine(b, place, e)
                dve.wait_ge(combined, (b + 1) * E)
                chain.at(b * NORM_STEPS)
                norm_stats(nc, dve, core, chain, b).then_inc(var_ready, 1)
                dve.wait_ge(rstd_ready, b + 1)
                if not is_first:
                    dve.wait_ge(turned, b)
                norm_apply(nc, core, b).then_inc(xn_ready, 1)

            def step(instruction):
                route_chain.inc(instruction)
                route_chain.settle(dve)

            dve.wait_ge(order_ready, 1)
            dve.wait_ge(logits_full, 1)
            step(nc.vector.tensor_copy(logits[:, :, :], logits_view))
            choose(nc, dve, route_chain, logits[:, :, :], scratch[:, :, :], order[:, :], best[:, :], top[:, 0, :], first[:, :, :])
            step(nc.vector.scalar_tensor_tensor(logits[:, :, :], first[:, :, :], -3e38, logits[:, :, :], ALU.mult, ALU.add))
            choose(nc, dve, route_chain, logits[:, :, :], scratch[:, :, :], order[:, :], best[:, :], top[:, 1, :], second[:, :, :])
            nc.vector.tensor_tensor(share[:, 1, :], top[:, 1, :], top[:, 0, :], ALU.subtract).then_inc(diff_ready, 1)
            dve.wait_ge(exp_ready, 1)
            step(nc.vector.tensor_scalar(total[:, :], share[:, 1, :], 1.0, None, ALU.add))
            step(nc.vector.reciprocal(share[:, 0, :], total[:, :]))
            step(nc.vector.tensor_tensor(share[:, 1, :], share[:, 1, :], share[:, 0, :], ALU.mult))
            step(nc.vector.tensor_tensor(first[:, :, :], first[:, :, :], share[:, 0, :].unsqueeze(2).to_broadcast([P, N, E]), ALU.mult))
            step(nc.vector.tensor_tensor(second[:, :, :], second[:, :, :], share[:, 1, :].unsqueeze(2).to_broadcast([P, N, E]), ALU.mult))
            step(nc.vector.tensor_tensor(gates[:, :, :], first[:, :, :], second[:, :, :], ALU.add))
            bodies(dve, body)



def stage_decay(core, w):
    nc = core.nc
    H, DH = 16, 64
    UNROLL = 2
    BLOCKS = (3, 2, 1, 0)
    WIDTH = [(i + 1) * P for i in range(TB)]
    START = [0, P, 3 * P, 6 * P]
    TOTAL = 10 * P
    ITEMS = ("k", "k_swap", "q", "q_swap", "v", "knorm", "qnorm")
    FREE = (4, 3)
    TABLE_STEPS = 11
    TWO_PI = 6.283185307179586
    C1 = 6.28125
    C2 = float(np.round((TWO_PI - C1) * 2**21) / 2**21)
    C3 = TWO_PI - C1 - C2
    ROUND = 12582912.0
    HALF_PI, BOUND = TWO_PI / 4, 3.1415925

    names = ("inputs_loaded", "pack_even", "pack_odd", "wo_even", "wo_odd", "const_ready", "params_ready", "proj_full",
             "proj_free_0", "proj_free_1", "rotated", "squared", "g_ready", "s_full", "a1_done", "a2_done", "relu_done",
             "r_done", "ln_done", "logit_done", "max_done", "exp_done", "t_full", "pt_free_0", "pt_free_1", "pv_full",
             "ot_done", "y_full", "x_done", "recip_done", "angle_ready", "phase_ready", "z_ready", "etab_ready",
             "v_ready", "lnv_ready", "tables_ready", "var_ready", "rstd_ready", "xn_ready", "turned", "taken",
             "soft_exp", "soft_ln", "mu_exp")
    S = {n: core.sem(n) for n in names}
    proj_free, pt_free = (S["proj_free_0"], S["proj_free_1"]), (S["pt_free_0"], S["pt_free_1"])
    pack_ready, wo_ready = (S["pack_even"], S["pack_odd"]), (S["wo_even"], S["wo_odd"])
    table_chain, const_chain, chain = Count(core.sem("table_chain")), Count(core.sem("const_chain")), Count(core.sem("norm_chain"))

    def wait(eng, name, value):
        if not (isinstance(value, int) and value <= 0):
            eng.wait_ge(S[name] if isinstance(name, str) else name, value)

    with ExitStack() as ctx:
        def sb(name, shape, dtype=F32):
            return core.sbuf(ctx, name, shape, dtype)

        pack, wo = sb("pack", [P, 2, 5, P]), sb("wo", [P, 2, C])
        cos, sin = sb("cos", [P, 2, T]), sb("sin", [P, 2, T])
        e_tab, r_tab, l_tab = sb("e_tab", [P, 2, T]), sb("r_tab", [P, 2, T]), sb("l_tab", [P, 2, T])
        steps, dist, mask = sb("steps", [P, T]), sb("dist", [P, T]), sb("mask", [P, T])
        angle, turns, folded = sb("angle", [P, T]), sb("turns", [P, T]), sb("folded", [P, T])
        z, var, lnv = sb("z", [P, T]), sb("var", [P, T]), sb("lnv", [P, T])
        ones, quarter = sb("ones", [P, P]), sb("quarter", [P, 1])
        sign, half_pi = sb("sign", [P, 1]), sb("half_pi", [P, 1])
        omega = sb("omega", [P, H])
        raw, soft, tmp = sb("raw", [P, 4, H]), sb("soft", [P, 4, H]), sb("tmp", [P, 4, H])
        mu_raw, tau, mu = sb("mu_raw", [P, H]), sb("tau", [P, H]), sb("mu", [P, H])
        neg_mu, amp, floor, coef, mu_recip = (sb(n, [P, H]) for n in ("neg_mu", "amp", "floor", "coef", "mu_recip"))
        parts = sb("parts", [P, 2, 2, T])
        q, k = sb("q", [P, 2, T]), sb("k", [P, 2, T])
        qsq, ksq = sb("qsq", [P, T]), sb("ksq", [P, T])
        knorm, g = sb("knorm", [P, T]), sb("g", [P, 2, TOTAL])
        qnorm = sb("qnorm", [P, 2, TB])
        v = sb("v", [P, 4, TB, P])
        u = sb("u", [P, 4, TOTAL])
        neg_max, rowsum, recip = sb("neg_max", [P, 4, TB]), sb("rowsum", [P, 4, TB]), sb("recip", [P, 2, TB])
        pT, oT = sb("pT", [P, 2, TB, T]), sb("oT", [P, 2, T])

        proj_bank = core.psum(ctx, "proj_bank", [P, 2, T])
        s_bank, t_bank = core.psum(ctx, "s_bank", [P, 2, T]), core.psum(ctx, "t_bank", [P, 2, T])
        o_bank, y_bank = core.psum(ctx, "o_bank", [P, T]), core.psum(ctx, "y_bank", [P, T])

        inputs = [(raw[:, n, :], w[name].partition_broadcast(P)) for n, name in enumerate(("sigma", "eta", "gamma", "nu"))]
        inputs += [(mu_raw[:, :], w["mu"].partition_broadcast(P)), (tau[:, :], w["tau"].partition_broadcast(P))]
        inputs += [(omega[32 * r:32 * r + 32, :], w["omega"]) for r in range(4)]

        def part(tile, i):
            return tile[:, START[i]:START[i] + WIDTH[i]]

        def table(tab, h, i):
            return tab[:, h, T - WIDTH[i]:T]

        def pipeline(eng, step):
            def body(i, last):
                for m in range(UNROLL * B):
                    step(i * (UNROLL * B) + m, m, i * UNROLL + m // B, m % B, last and m == UNROLL * B - 1)
            body(0, False)
            with eng.Fori(1, H // UNROLL - 1) as i:
                body(i, False)
            body(H // UNROLL - 1, True)

        def exists(n):
            return not (isinstance(n, int) and n < 0)

        def tables_wanted(h):
            return not (isinstance(h, int) and h == H - 1)

        def head_of(m):
            return (m // B) % 2

        block = ctx.enter_context(nc.Block())

        @block.sync
        def _(sp):
            for dst, src in inputs:
                sp.dma_start(dst, src).then_inc(S["inputs_loaded"], 16)
            for h in range(2):
                sp.dma_start(pack[:, h], w["pack"][h]).then_inc(pack_ready[h], 16)
                sp.dma_start(wo[:, h, :], w["wo"][h]).then_inc(wo_ready[h], 16)
            with sp.Fori(0, H // 2 - 1) as i:
                for p in range(2):
                    h = i * 2 + p
                    sp.wait_ge(S["proj_full"], (h + 1) * (B * len(ITEMS)))
                    sp.dma_start(pack[:, p], w["pack"][ds(h + 2, 1)].rearrange("a c m n -> (a c) m n")).then_inc(pack_ready[p], 16)
                    sp.wait_ge(S["y_full"], (h + 1) * B)
                    sp.dma_start(wo[:, p, :], w["wo"][ds(h + 2, 1)].rearrange("a c n -> (a c) n")).then_inc(wo_ready[p], 16)

        @block.tensor
        def _(pe):
            def project(n, m, h, b, items):
                p = head_of(m)
                for idx in items:
                    what = ITEMS[idx]
                    if idx == 0 and b == 0:
                        pe.wait_ge(pack_ready[p], (h - p) * 8 + 16)
                    wait(pe, proj_free[idx % 2], n * FREE[idx % 2] + idx // 2)
                    bank = proj_bank[:, idx % 2, :]
                    if idx < 4:
                        last = nc.tensor.matmul(bank, pack[:, p, idx, :], core.xT[:, b * T:(b + 1) * T], start=True, stop=True)
                    elif what == "v":
                        for j in range(TB):
                            last = nc.tensor.matmul(bank[:, j * P:(j + 1) * P], core.xT[:, b * T + j * P:b * T + (j + 1) * P],
                                                    pack[:, p, 4, :], start=True, stop=True)
                    elif what == "knorm":
                        pe.wait_ge(S["squared"], n * 2 + 1)
                        last = nc.tensor.matmul(bank, ones[:, :], ksq[:, :], start=True, stop=True)
                    else:
                        pe.wait_ge(S["squared"], n * 2 + 2)
                        for j in range(TB):
                            last = nc.tensor.matmul(bank[:, j:j + 1], qsq[:, j * P:(j + 1) * P], quarter[:, :], start=True, stop=True)
                    last.then_inc(S["proj_full"], 1)

            def scores(n, m, s):
                i = BLOCKS[s]
                if s == 0:
                    pe.wait_ge(S["rotated"], n * 2 + 2)
                wait(pe, "a1_done", n * 4 + s - 1)
                nc.tensor.matmul(s_bank[:, s % 2, 0:WIDTH[i]], q[:, m % 2, i * P:(i + 1) * P], k[:, m % 2, 0:WIDTH[i]],
                                 start=True, stop=True).then_inc(S["s_full"], 1)

            def turn_probs(n, m, s):
                i = BLOCKS[s]
                pe.wait_ge(S["exp_done"], n * 4 + s + 1)
                wait(pe, pt_free[s % 2], n * 2 + s // 2)
                for j in range(i + 1):
                    last = nc.tensor.transpose(t_bank[:, s % 2, j * P:(j + 1) * P], part(u[:, m % 4], i)[:, j * P:(j + 1) * P],
                                               core.ident[:, :])
                last.then_inc(S["t_full"], 1)

            def values(n, m):
                pe.wait_ge(pt_free[0], n * 2 + 2)
                pe.wait_ge(pt_free[1], n * 2 + 2)
                wait(pe, "ot_done", n)
                for j in range(TB):
                    last = nc.tensor.matmul(o_bank[:, j * P:T], v[:, m % 4, j, :], pT[:, m % 2, j, j * P:T],
                                            start=(j == 0), stop=(j == TB - 1))
                last.then_inc(S["pv_full"], 1)

            def output(n, m, h, b):
                p = head_of(m)
                if b == 0:
                    pe.wait_ge(wo_ready[p], (h - p) * 8 + 16)
                pe.wait_ge(S["ot_done"], n + 1)
                wait(pe, "x_done", n)
                for j in range(TB):
                    last = nc.tensor.matmul(y_bank[:, j * P:(j + 1) * P], oT[:, m % 2, j * P:(j + 1) * P], wo[:, p, :],
                                            start=True, stop=True)
                last.then_inc(S["y_full"], 1)

            def step(n, m, h, b, last):
                nxt = (n + 1, (m + 1) % (UNROLL * B), h + (1 if b == B - 1 else 0), (b + 1) % B)
                old = (n - 2, (m - 2) % (UNROLL * B), h - (1 if b < 2 else 0), (b - 2) % B)
                scores(n, m, 0)
                scores(n, m, 1)
                if not last:
                    project(*nxt, (0, 1))
                scores(n, m, 2)
                scores(n, m, 3)
                if exists(old[0]):
                    turn_probs(*old[:2], 0)
                    turn_probs(*old[:2], 1)
                if not last:
                    project(*nxt, (2, 3))
                if exists(old[0]):
                    turn_probs(*old[:2], 2)
                    turn_probs(*old[:2], 3)
                if not last:
                    project(*nxt, (4,))
                if exists(old[0]):
                    values(*old[:2])
                if not last:
                    project(*nxt, (5, 6))
                if exists(old[0]):
                    output(*old)

            pe.wait_ge(S["const_ready"], 9)
            project(0, 0, 0, 0, range(7))
            pipeline(pe, step)
            for n in (H * B - 2, H * B - 1):
                m = n % (UNROLL * B)
                for s in range(4):
                    turn_probs(n, m, s)
                values(n, m)
                output(n, m, n // B, n % B)
            pe.sem_inc(S["turned"], 1)
            with pe.Fori(0, B) as b:
                pe.wait_ge(S["xn_ready"], b + 1)
                pe.wait_ge(S["taken"], b + 1)
                norm_turn(nc, core, proj_bank[:, 0, :]).then_inc(S["turned"], 1)


        def angles(dve, t, p):
            def count(instruction):
                table_chain.inc(instruction)
                table_chain.settle(dve)

            table_chain.at(t * TABLE_STEPS)
            om = omega[:, ds(t, 1)]
            wait(dve, "phase_ready", t)
            wait(dve, "etab_ready", t)
            count(nc.vector.tensor_scalar(angle[:, :], steps[:, :], om, None, ALU.mult))
            count(nc.vector.tensor_scalar(turns[:, :], angle[:, :], 1.0 / TWO_PI, ROUND, ALU.mult, ALU.add))
            count(nc.vector.tensor_scalar(turns[:, :], turns[:, :], ROUND, None, ALU.subtract))
            for c in (C1, C2, C3):
                count(nc.vector.scalar_tensor_tensor(angle[:, :], turns[:, :], -c, angle[:, :], ALU.mult, ALU.add))
            count(nc.vector.tensor_scalar(angle[:, :], angle[:, :], BOUND, -BOUND, ALU.min, ALU.max))
            nc.vector.scalar_tensor_tensor(folded[:, :], angle[:, :], -1.0, angle[:, :], ALU.mult, ALU.max).then_inc(S["angle_ready"], 1)
            nc.vector.tensor_scalar(z[:, :], dist[:, :], neg_mu[:, ds(t, 1)], -30.0, ALU.mult, ALU.max).then_inc(S["z_ready"], 1)

        def phases(act, t, p):
            act.wait_ge(S["angle_ready"], t + 1)
            wait(act, proj_free[1], (t - 1) * (B * FREE[1]))
            nc.scalar.activation(sin[:, p, :], angle[:, :], ACT.Sin, scale=sign[:, 0:1])
            nc.scalar.activation(cos[:, p, :], folded[:, :], ACT.Sin, scale=-1.0, bias=half_pi[:, 0:1]).then_inc(S["phase_ready"], 1)

        def decays(act, t, p):
            act.wait_ge(S["z_ready"], t + 1)
            wait(act, "a2_done", (t - 1) * (B * 4))
            wait(act, "g_ready", (t - 1) * B)
            nc.scalar.activation(e_tab[:, p, :], z[:, :], ACT.Exp).then_inc(S["etab_ready"], 1)

        def variances(dve, t, p):
            def count(instruction):
                table_chain.inc(instruction)
                table_chain.settle(dve)

            table_chain.at(t * TABLE_STEPS + 7)
            dve.wait_ge(S["etab_ready"], t + 1)
            wait(dve, "lnv_ready", t)
            wait(dve, "r_done", (t - 1) * (B * 4))
            count(nc.vector.tensor_tensor(var[:, :], e_tab[:, p, :], e_tab[:, p, :], ALU.mult))
            count(nc.vector.tensor_scalar(var[:, :], var[:, :], -1.0, 1.0, ALU.mult, ALU.add))
            nc.vector.tensor_scalar(var[:, :], var[:, :], amp[:, ds(t, 1)], floor[:, ds(t, 1)], ALU.mult, ALU.add).then_inc(S["v_ready"], 1)
            dve.wait_ge(S["v_ready"], t + 1)
            count(nc.vector.tensor_scalar(r_tab[:, p, :], var[:, :], soft[:, 3, ds(t, 1)], None, ALU.mult))
            count(nc.vector.reciprocal(r_tab[:, p, :], r_tab[:, p, :]))

        def log_variances(act, t, p):
            act.wait_ge(S["v_ready"], t + 1)
            wait(act, "tables_ready", t)
            nc.scalar.activation(lnv[:, :], var[:, :], ACT.Ln).then_inc(S["lnv_ready"], 1)

        def additive(dve, t, p):
            dve.wait_ge(S["lnv_ready"], t + 1)
            wait(dve, "logit_done", (t - 1) * (B * 4))
            nc.vector.scalar_tensor_tensor(l_tab[:, p, :], lnv[:, :], -0.5 * DH, mask[:, :], ALU.mult, ALU.add).then_inc(S["tables_ready"], 1)

        @block.vector
        def _(dve):
            def const(instruction):
                const_chain.inc(instruction)
                const_chain.settle(dve)

            def rotate(n, m, h, which):
                p = head_of(m)
                if which == 0 and m % B == 0:
                    dve.wait_ge(S["phase_ready"], h + 1)
                wait(dve, "rotated", n * 2 - 1 + which)
                for sw in range(2):
                    idx = 2 * which + sw
                    dve.wait_ge(S["proj_full"], n * len(ITEMS) + idx + 1)
                    nc.vector.scalar_tensor_tensor(parts[:, which, sw, :], proj_bank[:, sw, :], -2.0 if which else 1.0,
                                                   (sin if sw else cos)[:, p, :], ALU.mult, ALU.mult).then_inc(proj_free[sw], 1)

            def distances(n, m, s):
                i = BLOCKS[s]
                dve.wait_ge(S["s_full"], n * 4 + s + 1)
                if s == 0:
                    dve.wait_ge(S["g_ready"], n + 1)
                    wait(dve, "t_full", (n - 3) * 4)
                nc.vector.tensor_tensor(part(u[:, m % 4], i), s_bank[:, s % 2, 0:WIDTH[i]], part(g[:, m % 2], i), ALU.add)\
                  .then_inc(S["a1_done"], 1)

            def decay(n, m, s):
                i = BLOCKS[s]
                if s == 0:
                    dve.wait_ge(S["a1_done"], n * 4 + 4)
                here = part(u[:, m % 4], i)
                nc.vector.tensor_tensor(here, here, table(e_tab, head_of(m), i), ALU.mult).then_inc(S["a2_done"], 1)

            def logits(n, m, h, s):
                i = BLOCKS[s]
                if s == 0:
                    dve.wait_ge(S["ln_done"], n + 1)
                    if m % B == 0:
                        dve.wait_ge(S["tables_ready"], h + 1)
                here = part(u[:, m % 4], i)
                nc.vector.scalar_tensor_tensor(here, here, coef[:, ds(h, 1)], table(l_tab, head_of(m), i), ALU.mult, ALU.add)\
                  .then_inc(S["logit_done"], 1)

            def maximum(n, m, s):
                i = BLOCKS[s]
                if s == 0:
                    dve.wait_ge(S["logit_done"], n * 4 + 4)
                nc.vector.tensor_reduce(neg_max[:, m % 4, i:i + 1], part(u[:, m % 4], i), AX_X, ALU.max, negate=True)\
                  .then_inc(S["max_done"], 1)

            def take_turned(n, m, s):
                i = BLOCKS[s]
                dve.wait_ge(S["t_full"], n * 4 + s + 1)
                if s == 0:
                    wait(dve, "pv_full", n - 1)
                nc.vector.tensor_copy(pT[:, m % 2, 0:i + 1, i * P:(i + 1) * P],
                                      t_bank[:, 0, 0:WIDTH[i]].rearrange("p (j c) -> p j c", c=P)).then_inc(pt_free[0], 1)

            def accumulate(n, m, b):
                dve.wait_ge(S["exp_done"], n * 4 + 4)
                nc.vector.reciprocal(recip[:, m % 2, :], rowsum[:, m % 4, :]).then_inc(S["recip_done"], 1)
                dve.wait_ge(S["recip_done"], n + 1)
                dve.wait_ge(S["y_full"], n + 1)
                wait(dve, "x_done", n)
                for j in range(TB):
                    tokens = core.x[:, b * TB + j, :]
                    last = nc.vector.scalar_tensor_tensor(tokens, y_bank[:, j * P:(j + 1) * P], recip[:, m % 2, j:j + 1],
                                                          tokens, ALU.mult, ALU.add)
                last.then_inc(S["x_done"], 1)

            def step(n, m, h, b, last):
                old = (n - 2, (m - 2) % (UNROLL * B))
                mid_head = h - (1 if b == 0 else 0)
                if m % B == 0:
                    dve.wait_ge(S["etab_ready"], h + 1)
                for s in range(4):
                    distances(n, m, s)
                for s in range(4):
                    decay(n, m, s)
                if exists(n - 1):
                    for s in range(4):
                        logits(n - 1, (m - 1) % (UNROLL * B), mid_head, s)
                    for s in range(4):
                        maximum(n - 1, (m - 1) % (UNROLL * B), s)
                if not last:
                    next_head = h + (1 if b == B - 1 else 0)
                    rotate(n + 1, (m + 1) % (UNROLL * B), next_head, 0)
                if exists(old[0]):
                    take_turned(*old, 0)
                if not last:
                    rotate(n + 1, (m + 1) % (UNROLL * B), next_head, 1)
                if exists(old[0]):
                    take_turned(*old, 2)
                if tables_wanted(h):
                    p = 1 - head_of(m)
                    if b == 1:
                        angles(dve, h + 1, p)
                    if b == 4:
                        variances(dve, h + 1, p)
                    if b == 6:
                        additive(dve, h + 1, p)
                if exists(old[0]):
                    accumulate(*old, (b - 2) % B)

            dve.wait_ge(S["inputs_loaded"], 16 * len(inputs))
            for r in (1, 3):
                last = nc.vector.tensor_scalar(omega[32 * r:32 * r + 32, :], omega[32 * r:32 * r + 32, :], -1.0, None, ALU.mult)
            const(last)
            const(nc.vector.scalar_tensor_tensor(tmp[:, :, :], raw[:, :, :], -1.0, raw[:, :, :], ALU.mult, ALU.max))
            dve.wait_ge(S["soft_ln"], 1)
            const(nc.vector.scalar_tensor_tensor(soft[:, :, :], raw[:, :, :], 0.0, tmp[:, :, :], ALU.max, ALU.add))
            dve.wait_ge(S["mu_exp"], 1)
            const(nc.vector.tensor_scalar(mu[:, :], mu[:, :], 1.0, None, ALU.add))
            const(nc.vector.reciprocal(mu[:, :], mu[:, :]))
            const(nc.vector.tensor_scalar(mu[:, :], mu[:, :], 1e-4, None, ALU.add))
            const(nc.vector.tensor_scalar(neg_mu[:, :], mu[:, :], -1.0, None, ALU.mult))
            const(nc.vector.tensor_scalar(mu_recip[:, :], mu[:, :], 2.0, None, ALU.mult))
            const(nc.vector.reciprocal(mu_recip[:, :], mu_recip[:, :]))
            const(nc.vector.tensor_tensor(amp[:, :], soft[:, 0, :], mu_recip[:, :], ALU.mult))
            const(nc.vector.tensor_tensor(floor[:, :], soft[:, 1, :], soft[:, 2, :], ALU.add))
            const(nc.vector.tensor_scalar(coef[:, :], soft[:, 3, :], float(DH), -0.5, ALU.add, ALU.mult))
            const(nc.vector.tensor_tensor(coef[:, :], coef[:, :], tau[:, :], ALU.mult))
            dve.wait_ge(S["const_ready"], 9)
            const(nc.vector.scalar_tensor_tensor(dist[:, :], dist[:, :], -1.0, dist[:, :], ALU.mult, ALU.max))
            angles(dve, 0, 0)
            variances(dve, 0, 0)
            additive(dve, 0, 0)
            rotate(0, 0, 0, 0)
            rotate(0, 0, 0, 1)
            pipeline(dve, step)
            final = H * B
            for s in range(4):
                logits(final - 1, UNROLL * B - 1, H - 1, s)
            for s in range(4):
                maximum(final - 1, UNROLL * B - 1, s)
            for n in (final - 2, final - 1):
                take_turned(n, n % (UNROLL * B), 0)
                take_turned(n, n % (UNROLL * B), 2)
                accumulate(n, n % (UNROLL * B), n % B)
            dve.wait_ge(S["x_done"], final)
            with dve.Fori(0, B) as b:
                chain.at(b * NORM_STEPS)
                norm_stats(nc, dve, core, chain, b).then_inc(S["var_ready"], 1)
                dve.wait_ge(S["rstd_ready"], b + 1)
                dve.wait_ge(S["turned"], b + 1)
                norm_apply(nc, core, b).then_inc(S["xn_ready"], 1)

        @block.scalar
        def _(act):
            def squares(n, m, which):
                wait(act, "proj_full", n * len(ITEMS))
                act.wait_ge(S["rotated"], n * 2 + 1 + which)
                src, dst = (q, qsq) if which else (k, ksq)
                nc.scalar.activation(dst[:, :], src[:, m % 2, :], ACT.Square).then_inc(S["squared"], 1)

            def take(n, m, idx):
                act.wait_ge(S["proj_full"], n * len(ITEMS) + idx + 1)
                bank = proj_bank[:, idx % 2, :]
                if idx == 4:
                    nc.scalar.copy(v[:, m % 4, :, :], bank.rearrange("p (j d) -> p j d", j=TB)).then_inc(proj_free[0], 1)
                elif idx == 5:
                    wait(act, "g_ready", n)
                    nc.scalar.copy(knorm[:, :], bank).then_inc(proj_free[1], 1)
                else:
                    nc.scalar.copy(qnorm[:, m % 2, :], bank[:, 0:TB]).then_inc(proj_free[0], 1)

            def relu(n, m, s):
                i = BLOCKS[s]
                if s == 0:
                    act.wait_ge(proj_free[0], n * FREE[0] + FREE[0])
                act.wait_ge(S["a2_done"], n * 4 + s + 1)
                here = part(u[:, m % 4], i)
                nc.scalar.activation(here, here, ACT.Relu, bias=qnorm[:, m % 2, i:i + 1]).then_inc(S["relu_done"], 1)

            def log(n, m):
                act.wait_ge(S["r_done"], n * 4 + 4)
                nc.scalar.activation(u[:, m % 4, :], u[:, m % 4, :], ACT.Ln, bias=1.0).then_inc(S["ln_done"], 1)

            def exponentials(n, m, s):
                i = BLOCKS[s]
                act.wait_ge(S["max_done"], n * 4 + s + 1)
                here = part(u[:, m % 4], i)
                nc.scalar.activation(here, here, ACT.Exp, bias=neg_max[:, m % 4, i:i + 1],
                                     accum_out=rowsum[:, m % 4, i:i + 1]).then_inc(S["exp_done"], 1)

            def take_turned(n, m, s):
                i = BLOCKS[s]
                act.wait_ge(S["t_full"], n * 4 + s + 1)
                if s == 1:
                    wait(act, "pv_full", n - 1)
                nc.scalar.copy(pT[:, m % 2, 0:i + 1, i * P:(i + 1) * P],
                               t_bank[:, 1, 0:WIDTH[i]].rearrange("p (j c) -> p j c", c=P)).then_inc(pt_free[1], 1)

            def take_outputs(n, m):
                act.wait_ge(S["pv_full"], n + 1)
                wait(act, "y_full", n - 1)
                nc.scalar.copy(oT[:, m % 2, :], o_bank[:, :]).then_inc(S["ot_done"], 1)

            def step(n, m, h, b, last):
                nxt, mid, old = ((m + d) % (UNROLL * B) for d in (1, -1, -2))
                if exists(n - 1):
                    log(n - 1, mid)
                for s in range(4):
                    relu(n, m, s)
                if tables_wanted(h) and b == 5:
                    log_variances(act, h + 1, 1 - head_of(m))
                if exists(n - 1):
                    for s in range(4):
                        exponentials(n - 1, mid, s)
                if tables_wanted(h) and b == 3:
                    decays(act, h + 1, 1 - head_of(m))
                if exists(n - 2):
                    take_turned(n - 2, old, 1)
                if not last:
                    squares(n + 1, nxt, 0)
                if exists(n - 2):
                    take_turned(n - 2, old, 3)
                if not last:
                    squares(n + 1, nxt, 1)
                    take(n + 1, nxt, 4)
                if exists(n - 2):
                    take_outputs(n - 2, old)
                if not last:
                    take(n + 1, nxt, 5)
                    take(n + 1, nxt, 6)
                if tables_wanted(h) and b == 2:
                    phases(act, h + 1, 1 - head_of(m))

            act.wait_ge(const_chain.sem, 2)
            nc.scalar.activation(tmp[:, :, :], tmp[:, :, :], ACT.Exp, scale=-1.0).then_inc(S["soft_exp"], 1)
            nc.scalar.activation(mu[:, :], mu_raw[:, :], ACT.Exp, scale=-1.0).then_inc(S["mu_exp"], 1)
            act.wait_ge(S["soft_exp"], 1)
            nc.scalar.activation(tmp[:, :, :], tmp[:, :, :], ACT.Ln, bias=1.0).then_inc(S["soft_ln"], 1)
            act.wait_ge(S["const_ready"], 9)
            phases(act, 0, 0)
            decays(act, 0, 0)
            log_variances(act, 0, 0)
            squares(0, 0, 0)
            squares(0, 0, 1)
            for idx in (4, 5, 6):
                take(0, 0, idx)
            pipeline(act, step)
            final = H * B
            log(final - 1, UNROLL * B - 1)
            for s in range(4):
                exponentials(final - 1, UNROLL * B - 1, s)
            for n in (final - 2, final - 1):
                take_turned(n, n % (UNROLL * B), 1)
                take_turned(n, n % (UNROLL * B), 3)
                take_outputs(n, n % (UNROLL * B))
            act.sem_inc(S["taken"], 1)
            with act.Fori(0, B) as b:
                act.wait_ge(S["turned"], b + 2)
                nc.scalar.copy(core.xT[:, ds(b * T, T)], proj_bank[:, 0, :]).then_inc(S["taken"], 1)

        @block.gpsimd
        def _(pool):
            def rotated(n, m, which):
                pool.wait_ge(proj_free[1], n * FREE[1] + 1 + which)
                if which == 0:
                    wait(pool, "s_full", (n - 1) * 4)
                nc.gpsimd.tensor_tensor((q if which else k)[:, m % 2, :], parts[:, which, 0, :], parts[:, which, 1, :], ALU.add)\
                  .then_inc(S["rotated"], 1)

            def key_terms(n, m, h, b):
                pool.wait_ge(proj_free[1], n * FREE[1] + 3)
                if b == 0:
                    pool.wait_ge(S["etab_ready"], h + 1)
                wait(pool, "a1_done", (n - 1) * 4)
                for i in BLOCKS:
                    last = nc.gpsimd.tensor_tensor(part(g[:, m % 2], i), knorm[:, 0:WIDTH[i]], table(e_tab, head_of(m), i), ALU.mult)
                last.then_inc(S["g_ready"], 1)

            def over_variance(n, m, h, b, s):
                i = BLOCKS[s]
                if b == 0 and s == 0:
                    pool.wait_ge(S["tables_ready"], h + 1)
                pool.wait_ge(S["relu_done"], n * 4 + s + 1)
                here = part(u[:, m % 4], i)
                nc.gpsimd.tensor_tensor(here, here, table(r_tab, head_of(m), i), ALU.mult).then_inc(S["r_done"], 1)

            def step(n, m, h, b, last):
                nxt = (m + 1) % (UNROLL * B)
                for s in range(4):
                    over_variance(n, m, h, b, s)
                if not last:
                    rotated(n + 1, nxt, 0)
                    rotated(n + 1, nxt, 1)
                    key_terms(n + 1, nxt, h + (1 if b == B - 1 else 0), (b + 1) % B)

            nc.gpsimd.memset(ones[:, :], 1.0).then_inc(S["const_ready"], 1)
            nc.gpsimd.memset(quarter[:, :], 0.25).then_inc(S["const_ready"], 1)
            nc.gpsimd.memset(sign[:, :], 1.0).then_inc(S["const_ready"], 1)
            nc.gpsimd.memset(half_pi[:, :], HALF_PI).then_inc(S["const_ready"], 1)
            nc.gpsimd.memset(mask[:, :], 0.0).then_inc(S["const_ready"], 1)
            nc.gpsimd.iota(steps[:, :], pattern=[[1, T]], base=0, channel_multiplier=0,
                           allow_small_or_imprecise_dtypes=True).then_inc(S["const_ready"], 1)
            nc.gpsimd.iota(dist[:, :], pattern=[[-1, T]], base=T - P, channel_multiplier=1,
                           allow_small_or_imprecise_dtypes=True).then_inc(S["const_ready"], 1)
            pool.wait_ge(S["const_ready"], 7)
            nc.gpsimd.memset(sign[0:DH, :], -1.0).then_inc(S["const_ready"], 1)
            nc.gpsimd.affine_select(out=mask[:, :], in_=mask[:, :], compare_op=ALU.is_ge, fill=NEG, base=T - P,
                                    pattern=[[-1, T]], channel_multiplier=1).then_inc(S["const_ready"], 1)
            rotated(0, 0, 0)
            rotated(0, 0, 1)
            key_terms(0, 0, 0, 0)
            pipeline(pool, step)
            with pool.Fori(0, B) as b:
                pool.wait_ge(S["var_ready"], b + 1)
                norm_rstd(nc, core).then_inc(S["rstd_ready"], 1)


ROPE_CAUSAL = Attention(heads=16, dim=8, kv_heads=16, causal=True, rope=1, bias=True, gate=False)
GROUPED = Attention(heads=8, dim=32, kv_heads=2, causal=False, rope=1, bias=False, gate=True)
BILINEAR = Attention(heads=16, dim=8, kv_heads=16, causal=False, rope=0, bias=True, gate=False)


def build(nc, dram, plan):
    with ExitStack() as ctx:
        core = Core(nc, ctx, dram)
        stage_load(core)
        core.end_stage()
        for stage in plan:
            if stage == "attn_rope":
                stage_attention(core, ROPE_CAUSAL, {n: dram["a_" + n] for n in (
                    "wq", "wq_swap", "wk", "wk_swap", "bq", "bq_swap", "bk", "bk_swap", "wv", "bv", "wo", "bo", "cos", "sin", "keep", "minus", "scratch")})
            elif stage == "attn_gqa":
                stage_attention(core, GROUPED, {n: dram["g_" + n] for n in (
                    "wq", "wq_swap", "wk", "wk_swap", "wv", "wo", "wg", "cos", "sin", "keep", "minus", "scratch")})
            elif stage == "attn_bilinear":
                stage_attention(core, BILINEAR, {n: dram["v_" + n] for n in ("wq", "wk", "wv", "bv", "wo", "bo", "keep", "minus", "scratch")})
            elif stage == "attn_decay":
                stage_decay(core, {n: dram["d_" + n] for n in ("sigma", "eta", "gamma", "nu", "mu", "tau", "omega", "pack", "wo")})
            elif stage == "ffn_linear":
                stage_ffn(core, {n: dram["f_" + n] for n in ("router", "w_in", "w_out")}, 8, None)
            elif stage == "ffn_gated":
                stage_ffn(core, {n: dram["h_" + n] for n in ("router", "wg", "wu", "wd")}, 9, 352)
            core.end_stage()
        stage_store(core)
        core.end_stage()



def _tables(dim, rot, pairs_adjacent):
    half = rot // 2
    f = np.arange(half, dtype=np.float32)
    theta = np.power(np.float32(10000.0), (np.float32(-2.0) * f / np.float32(rot)).astype(np.float32)).astype(np.float32)
    ang = (np.arange(T, dtype=np.float32)[None, :] * theta[:, None]).astype(np.float32).astype(np.float64)
    cos, sin = np.ones((P, T), np.float32), np.zeros((P, T), np.float32)
    for c in range(P):
        d = c % dim
        if d < rot:
            n, low = (d // 2, d % 2 == 0) if pairs_adjacent else (d % half, d < half)
            cos[c] = np.cos(ang[n])
            sin[c] = -np.sin(ang[n]) if low else np.sin(ang[n])
    return cos, sin


def kernel(**inputs):
    import ml_dtypes
    import concourse.bacc as _bacc
    from concourse.bass_utils import run_bass_kernel_spmd as _run

    i = {n: np.asarray(a) for n, a in inputs.items()}
    a = {"x": i["L0_attn_a_x"]}
    eye, low = np.eye(P, dtype=np.float32), np.tril(np.ones((P, P), bool))
    a["ident"], a["ident16"] = eye, eye.astype(ml_dtypes.bfloat16)
    a["mask_ij"] = np.where(low, 0.0, NEG).astype(ml_dtypes.bfloat16)
    a["mask_ji"] = np.where(low.T, 0.0, NEG).astype(ml_dtypes.bfloat16)

    for n, cfg in (("a", ROPE_CAUSAL), ("g", GROUPED), ("v", BILINEAR)):
        a[f"{n}_keep"] = np.ones((P, 1), np.float32)
        for row in range(cfg.max_row, P, cfg.lane):
            a[f"{n}_keep"][row:row + MAX_PARTS] = 0.0
        a[f"{n}_minus"] = np.full((MAX_PARTS, max(cfg.kv_heads // cfg.lanes, 1), T), -1.0, ml_dtypes.bfloat16)

    partner = np.arange(C) ^ 1
    for n in "qk":
        wt = i["L0_attn_a_w" + n].T
        a[f"a_w{n}"], a[f"a_w{n}_swap"] = wt, wt[:, partner]
        for tail, bias in (("", i["L0_attn_a_b" + n]), ("_swap", i["L0_attn_a_b" + n][partner])):
            a[f"a_b{n}{tail}"] = bias
    a["a_wv"], a["a_bv"] = i["L0_attn_a_wv"].T, i["L0_attn_a_bv"]
    a["a_wo"], a["a_bo"] = i["L0_attn_a_wp"].T, i["L0_attn_a_bp"]
    a["a_cos"], a["a_sin"] = _tables(8, 8, True)

    d = np.arange(32)
    within = np.where(d < 8, (d + 4) % 8, d)
    a["g_wq"], a["g_wg"] = i["L1_attn_a_Wq"][:, :256], i["L1_attn_a_Wq"][:, 256:]
    a["g_wq_swap"] = a["g_wq"][:, (np.arange(8)[:, None] * 32 + within).ravel()]
    a["g_wk"] = i["L1_attn_a_Wk"]
    a["g_wk_swap"] = a["g_wk"][:, (np.arange(2)[:, None] * 32 + within).ravel()]
    a["g_wv"], a["g_wo"] = i["L1_attn_a_Wv"], i["L1_attn_a_Wo"]
    a["g_cos"], a["g_sin"] = _tables(32, 8, False)

    wq = np.zeros((C, C), np.float32)
    for h in range(16):
        wq[8 * h:8 * h + 8, 8 * h:8 * h + 8] = i["L1_attn_b_w_att_val"][h]
    a["v_wq"], a["v_wk"] = wq, eye
    a["v_wv"], a["v_bv"] = i["L1_attn_b_wv_w"].T, i["L1_attn_b_wv_b"]
    a["v_wo"], a["v_bo"] = i["L1_attn_b_out_w"].T, i["L1_attn_b_out_b"]

    def by_head(wt):
        return wt.reshape(C, 2, 16, 64).transpose(2, 0, 1, 3)
    wq, wk, wv = (by_head(i["L0_attn_b_W" + n]) for n in "qkv")
    a["d_pack"] = np.stack([t.reshape(16, C, P) for t in (wk, wk[:, :, ::-1], wq, wq[:, :, ::-1], wv)], axis=2)
    a["d_wo"] = i["L0_attn_b_Wo"].reshape(2, 16, 64, C).transpose(1, 0, 2, 3).reshape(16, P, C)
    for n, name in (("sigma", "sigma_raw"), ("eta", "eta_raw"), ("gamma", "gamma_raw"), ("nu", "nu_raw"), ("mu", "mu_raw"), ("tau", "tau")):
        a["d_" + n] = i["L0_attn_b_" + name]
    a["d_omega"] = i["L0_attn_b_omega"].T

    a["f_router"], a["f_w_in"], a["f_w_out"] = i["L0_ffn_w_gate"].T, i["L0_ffn_w_in"], i["L0_ffn_w_out"].transpose(0, 2, 1)
    for n, name in (("router", "Wr"), ("wg", "Wg"), ("wu", "Wu"), ("wd", "Wd")):
        a["h_" + n] = i["L1_ffn_" + name]

    nc = _bacc.Bacc("TRN2", target_bir_lowering=False, num_devices=1)
    arrays, dram = {}, {}
    for n, t in a.items():
        t = np.ascontiguousarray(t)
        arrays[f"in_{n}"] = t
        dram[n] = nc.dram_tensor(f"in_{n}", t.shape, mybir.dt.from_np(t.dtype), kind="ExternalInput").ap()
    for n, cfg in (("a", ROPE_CAUSAL), ("g", GROUPED), ("v", BILINEAR)):
        dram[f"{n}_scratch"] = nc.dram_tensor(f"{n}_scratch", (2, len(cfg.tiles), 3, P, T), BF16, kind="Internal").ap()
    dram["out"] = nc.dram_tensor("out_0_dram", (B, T, C), F32, kind="ExternalOutput").ap()
    build(nc, dram, PLAN)
    r = _run(nc, [arrays], core_ids=[0])
    return r.results[0]["out_0_dram"]
```

```python
from contextlib import ExitStack

import numpy as np

import concourse.bass as bass
from concourse import mybir

F32 = mybir.dt.float32
BF16 = mybir.dt.bfloat16
ALU = mybir.AluOpType
ACT = mybir.ActivationFunctionType
AX_X = mybir.AxisListType.X

P = 128
B, T, C = 8, 512, 128
TB = T // P
EPS = 1e-5
NORM_STEPS = 2
NEG = -1e30
PLAN = ["attn_rope", "ffn_linear", "attn_decay", "ffn_linear", "attn_gqa", "ffn_gated", "attn_bilinear", "ffn_gated"]


def ds(start, size):
    return bass.ds(start, size)


class Core:

    def __init__(self, nc, ctx, dram):
        self.nc, self.ctx, self.dram = nc, ctx, dram
        self.names = 0
        self.sems, self.open_sems = ExitStack(), []
        self.x = self.sbuf(ctx, "x", [P, B * TB, C])
        self.xT = self.sbuf(ctx, "xT", [P, B * T])
        self.ident = self.sbuf(ctx, "ident", [P, P])
        self.ident16 = self.sbuf(ctx, "ident16", [P, P], BF16)
        self.mask_ij = self.sbuf(ctx, "mask_ij", [P, P], BF16)
        self.mask_ji = self.sbuf(ctx, "mask_ji", [P, P], BF16)
        self.ones_row = self.sbuf(ctx, "ones_row", [1, P])
        self.minus_half = self.sbuf(ctx, "minus_half", [P, TB])
        self.stats = self.sbuf(ctx, "stats", [P, TB, 6])
        self.mean_var = self.sbuf(ctx, "mean_var", [P, TB, 2])
        self.var_eps = self.sbuf(ctx, "var_eps", [P, TB])
        self.pause = self.sbuf(ctx, "pause", [1, 1])
        self.rstd = self.sbuf(ctx, "rstd", [P, TB])
        self.xn = self.sbuf(ctx, "xn", [P, TB, C])

    def sbuf(self, ctx, name, shape, dtype=F32):
        self.names += 1
        return ctx.enter_context(self.nc.sbuf_tensor(f"{name}_{self.names}", shape, dtype))

    def psum(self, ctx, name, shape, dtype=F32):
        self.names += 1
        return ctx.enter_context(self.nc.psum_tensor(f"{name}_{self.names}", shape, dtype))

    def sem(self, name):
        self.names += 1
        made = self.sems.enter_context(self.nc.semaphore(f"{name}_{self.names}"))
        self.open_sems.append(made)
        return made

    def end_stage(self):
        numbers = sorted(s.num for s in self.open_sems)
        with self.nc.Block() as block:
            @block.sync
            def _(sp):
                first = numbers[0]
                for n, after in zip(numbers, numbers[1:] + [None]):
                    if after != n + 1:
                        sp.sem_clear(range(first, n + 1))
                        first = after
        self.sems.close()
        self.open_sems = []


class Count:

    def __init__(self, sem):
        self.sem, self.base, self.n = sem, 0, 0

    def at(self, base):
        self.base, self.n = base, 0

    def inc(self, instruction):
        instruction.then_inc(self.sem, 1)
        self.n += 1

    def settle(self, engine):
        engine.wait_ge(self.sem, self.base + self.n)



def norm_stats(nc, dve, core, chain, b):
    nc.vector.memset(core.pause[:, :], 0.0)
    for j in range(TB):
        last = nc.vector.bn_stats(core.stats[:, j, :], core.x[:, ds(b * TB + j, 1), :].rearrange("p a c -> p (a c)"))
    chain.inc(last)
    chain.settle(dve)
    nc.vector.memset(core.pause[:, :], 0.0)
    for j in range(TB):
        last = nc.vector.bn_aggr(core.mean_var[:, j, :], core.stats[:, j, :])
    chain.inc(last)
    chain.settle(dve)
    return nc.vector.tensor_scalar(core.var_eps[:, :], core.mean_var[:, :, 1], EPS, None, ALU.add)


def norm_rstd(nc, core):
    return nc.gpsimd.tensor_tensor(core.rstd[:, :], core.var_eps[:, :], core.minus_half[:, :], ALU.pow)


def norm_apply(nc, core, b):
    for j in range(TB):
        last = nc.vector.tensor_scalar(core.xn[:, j, :], core.x[:, ds(b * TB + j, 1), :].rearrange("p a c -> p (a c)"),
                                       core.mean_var[:, j, 0:1], core.rstd[:, j:j + 1], ALU.subtract, ALU.mult)
    return last


def norm_turn(nc, core, out):
    for j in range(TB):
        last = nc.tensor.transpose(out[:, j * P:(j + 1) * P], core.xn[:, j, :], core.ident[:, :])
    return last



def stage_load(core):
    nc, d = core.nc, core.dram
    loaded, const_loaded = core.sem("x_loaded"), core.sem("const_loaded")
    made = core.sem("constants_made")
    chain = Count(core.sem("load_chain"))
    var_ready, rstd_ready, xn_ready = core.sem("var_ready"), core.sem("rstd_ready"), core.sem("xn_ready")
    turned, taken = core.sem("turned"), core.sem("taken")
    x_tokens = d["x"].rearrange("b (j p) c -> p (b j) c", p=P)
    with ExitStack() as ctx:
        bank = core.psum(ctx, "turn_bank", [P, 2, T])
        block = ctx.enter_context(nc.Block())

        @block.sync
        def _(sp):
            sp.dma_start(core.ident[:, :], d["ident"]).then_inc(const_loaded, 16)
            sp.dma_start(core.ident16[:, :], d["ident16"]).then_inc(const_loaded, 16)
            sp.dma_start(core.mask_ij[:, :], d["mask_ij"]).then_inc(const_loaded, 16)
            sp.dma_start(core.mask_ji[:, :], d["mask_ji"]).then_inc(const_loaded, 16)
            sp.dma_start(core.x[:, :, :], x_tokens).then_inc(loaded, 16)

        @block.gpsimd
        def _(pool):
            nc.gpsimd.memset(core.minus_half[:, :], -0.5).then_inc(made, 1)
            nc.gpsimd.memset(core.ones_row[:, :], 1.0).then_inc(made, 1)
            pool.wait_ge(made, 2)
            with pool.Fori(0, B) as b:
                pool.wait_ge(var_ready, b + 1)
                norm_rstd(nc, core).then_inc(rstd_ready, 1)

        @block.vector
        def _(dve):
            dve.wait_ge(loaded, 16)
            with dve.Fori(0, B) as b:
                chain.at(b * NORM_STEPS)
                norm_stats(nc, dve, core, chain, b).then_inc(var_ready, 1)
                dve.wait_ge(rstd_ready, b + 1)
                dve.wait_ge(turned, b + 1)
                norm_apply(nc, core, b).then_inc(xn_ready, 1)

        @block.tensor
        def _(pe):
            pe.sem_inc(turned, 1)
            pe.wait_ge(const_loaded, 64)
            with pe.Fori(0, B // 2) as i:
                for u in range(2):
                    b = i * 2 + u
                    pe.wait_ge(xn_ready, b + 1)
                    pe.wait_ge(taken, b + 1)
                    norm_turn(nc, core, bank[:, u, :]).then_inc(turned, 1)

        @block.scalar
        def _(act):
            act.sem_inc(taken, 1)
            with act.Fori(0, B // 2) as i:
                for u in range(2):
                    b = i * 2 + u
                    act.wait_ge(turned, b + 2)
                    nc.scalar.copy(core.xT[:, ds(b * T, T)], bank[:, u, :]).then_inc(taken, 1)


def stage_store(core):
    nc = core.nc
    stored = core.sem("x_stored")
    with nc.Block() as block:
        @block.sync
        def _(sp):
            sp.dma_start(core.dram["out"].rearrange("b (j p) c -> p (b j) c", p=P), core.x[:, :, :]).then_inc(stored, 16)
            sp.wait_ge(stored, 16)



HIGH, MIDDLE_PART, LOW = 0, 1, 2
Q_PARTS = (HIGH, MIDDLE_PART, LOW, HIGH, MIDDLE_PART, HIGH)
K_PARTS = (HIGH, HIGH, HIGH, MIDDLE_PART, MIDDLE_PART, LOW)
MAX_PARTS = 2


class Attention:

    def __init__(self, heads, dim, kv_heads, causal, rope, bias, gate):
        self.heads, self.dim, self.kv_heads = heads, dim, kv_heads
        self.causal, self.rope, self.bias, self.gate = causal, rope, bias, gate
        self.groups = 4
        self.per_group = heads // self.groups
        self.stride = P // self.per_group
        self.width = heads * dim
        self.halves = self.width // P
        self.kv_width = kv_heads * dim
        self.scale = float(dim) ** -0.5
        self.lanes = 2 if len(Q_PARTS) * dim <= P // 2 else 1
        self.lane = P // self.lanes
        per_chunk = self.lane // dim
        self.chunk_parts = [range(c, min(c + per_chunk, len(Q_PARTS))) for c in range(0, len(Q_PARTS), per_chunk)]
        self.chunks = len(self.chunk_parts)
        self.max_row = self.lane - MAX_PARTS
        cuts = [[0], [1, 3], [2]] if causal else [[0], [1], [2], [3]]
        self.ops = [(r, cut) for r in range(self.per_group) for cut in cuts]
        self.units = []
        for j in reversed(range(TB)):
            fit = TB // (j + 1) if causal else 1
            for lane in range(self.lanes):
                heads = range(lane, self.per_group, self.lanes)
                self.units += [(j, heads[r:r + fit]) for r in range(0, len(heads), fit)]
        self.tiles = [("k", 0)] + [("q", c) for c in range(self.halves)]

    def khead(self, h):
        return h * self.kv_heads // self.heads

    def segments(self, cut):
        at, out = 0, []
        for j in cut:
            first = j if self.causal else 0
            out.append((j, first, at))
            at += (TB - first) * P
        return out, at

    def lane_rows(self, head, chunk, with_maximum):
        first = (head % self.lanes) * self.lane
        return slice(first, first + (self.lane if with_maximum or chunk < self.chunks - 1 else self.max_row))

    def prep(self):
        items = [(what, at, s) for what, at in self.tiles for s in range(1 + self.rope)]
        if self.gate:
            return items + [("v", 0, 0), ("v", 1, 0), ("gate", 0, 0), ("gate", 1, 0)]
        return items + [("v", 0, 0)]

    def v_blocks(self, at):
        return range(at * TB // 2, (at + 1) * TB // 2) if self.gate else range(TB)

    def end(self):
        return [("turn_out", self.groups - 1, 0)] + [("turn_y", h, 0) for h in range(self.halves)] + [("project", 0, 0), ("norm", 0, 0)]

    def batch_of(self, item, b, g):
        if item[0] == "turn_out" and g > 0:
            return b
        return b - 1 if item in self.end() else b + 1

    def plan(self, epilogue, prep):
        n_ops = len(self.ops)
        slots = [[[] for _ in range(n_ops)] for _ in range(self.groups)]
        if epilogue:
            for n, item in enumerate([("turn_y", h, 0) for h in range(self.halves)] + [("project", 0, 0)]):
                slots[0][min(2 + n, n_ops - 1)].append(item)
            slots[1][2].append(("norm", 0, 0))
        if prep:
            places = [(g, k) for g in range(2) for k in range(n_ops) if (g, k) >= (0, n_ops // 2)]
            items = self.prep()
            for n, item in enumerate(items):
                g, k = places[n * len(places) // len(items)]
                slots[g][k].append(item)
        for g in range(self.groups if prep else self.groups - 1):
            slots[g][n_ops - 2] += [("maxima", m, 0) for m in range(self.per_group // self.lanes)]
        for g in range(0 if epilogue else 1, self.groups):
            slots[g][1].insert(0, ("turn_out", (g - 1) % self.groups, 0))
        return slots


def stage_attention(core, cfg, w):
    nc = core.nc
    G, HG, D, NOPS, NUNITS = cfg.groups, cfg.per_group, cfg.dim, len(cfg.ops), len(cfg.units)
    KV, ST, QT, CH = cfg.kv_heads, cfg.stride, cfg.heads // cfg.lanes, cfg.chunks
    KT = max(KV // cfg.lanes, 1)
    TILES = len(cfg.tiles)
    SLOTS = 4
    SCORE_BANKS = 3
    MAX_TILES = HG // cfg.lanes
    PREP = cfg.prep()
    ENDS = len(cfg.end())
    TURNS = G * MAX_TILES
    MIDDLE = len(PREP) + ENDS + TURNS + G - 1
    BEFORE = len(PREP) + MAX_TILES
    assert MIDDLE % 2 == 0

    names = ("weights_loaded", "cleared", "xcur_even", "xcur_odd", "max_high_ready", "spare_full_even", "spare_full_odd",
             "spare_free_even", "spare_free_odd", "parts_ready", "stacks_even", "stacks_odd",
             "max_full", "max_free", "max_parts_ready", "scores_full", "exp_done", "pv_done", "out_copied", "recip_ready",
             "minus_loaded", "stacks_cleared", "gated", "var_ready", "rstd_ready", "xn_ready", "gate_sum_ready", "gate_recip_ready", "gate_ready")
    (weights_loaded, cleared, xcur_even, xcur_odd, max_high_ready, spare_full_even, spare_full_odd,
     spare_free_even, spare_free_odd, parts_ready, stacks_even, stacks_odd,
     max_full, max_free, max_parts_ready, scores_full, exp_done, pv_done, out_copied, recip_ready,
     minus_loaded, stacks_cleared, gated, var_ready, rstd_ready, xn_ready, gate_sum_ready, gate_recip_ready, gate_ready) = (core.sem(n) for n in names)
    xcur_ready, stacks_ready = [xcur_even, xcur_odd], [stacks_even, stacks_odd]
    spare_full, spare_free = [spare_full_even, spare_full_odd], [spare_free_even, spare_free_odd]
    parts_written = [core.sem(f"parts_written_{what}{at}") for what, at in cfg.tiles]
    split_chain, chain = Count(core.sem("split_chain")), Count(core.sem("end_chain"))
    SPLIT_STEPS = 1 + cfg.rope

    def slot(b, n):
        if isinstance(b, int) and b < 0:
            return n % 2, n // 2
        if isinstance(b, int) and b == 0:
            return (BEFORE + n) % 2, (BEFORE + n) // 2
        n += BEFORE + MIDDLE - ENDS
        return n % 2, (b - 1) * (MIDDLE // 2) + n // 2

    LAST = ENDS + TURNS - MAX_TILES + G - 1

    def full(eng, b, n):
        bank, nth = slot(b, n)
        eng.wait_ge(spare_full[bank], nth + 1)

    def out_of_bank(eng, b, n):
        bank, nth = slot(b, n)
        eng.wait_ge(spare_free[bank], nth + 1)

    def bodies(eng, emit):
        emit(0, 0, False, True)
        with eng.Fori(0, (B - 2) // 2) as i:
            emit(i * 2 + 1, 1, True, True)
            emit(i * 2 + 2, 0, True, True)
        emit(B - 1, 1, True, False)

    def units_at(o):
        work = [(j + 1) * len(heads) if cfg.causal else 1 for j, heads in cfg.units]
        done = [sum(work[:u]) * (NOPS - 3) // sum(work) for u in range(NUNITS)]
        return [u for u in range(NUNITS) if done[u] == o]

    def max_bank_of(g, u):
        return (g * NUNITS + u) % 2

    def score_bank_before(n, o):
        if o >= SCORE_BANKS:
            return n * NOPS + o - SCORE_BANKS + 1
        if isinstance(n, int) and n == 0:
            return None
        user = max(u for u in range(NOPS) if u % SCORE_BANKS == o % SCORE_BANKS)
        return (n - 1) * NOPS + user + 1

    def copies(what):
        out = []
        for lane in range(cfg.lanes):
            for c, numbers in enumerate(cfg.chunk_parts):
                for k, number in enumerate(numbers):
                    row = lane * cfg.lane + k * D
                    out.append((slice(row, row + D), c, (Q_PARTS if what == "q" else K_PARTS)[number], lane))
        return out

    READS = len(copies("q")) * cfg.halves + len(copies("k"))

    with ExitStack() as ctx:
        def sb(name, shape, dtype=F32):
            return core.sbuf(ctx, name, shape, dtype)

        wq, wk = sb("wq", [P, 1 + cfg.rope, cfg.halves, P]), sb("wk", [P, 1 + cfg.rope, P])
        wv, wo = sb("wv", [P, KV * D]), sb("wo", [P, cfg.halves, C])
        if cfg.rope:
            cos, sin = sb("cos", [P, T]), sb("sin", [P, T])
            turned = sb("turned", [P, 2, 2, T])
            qbias, kbias = sb("qbias", [P, 2, cfg.halves]), sb("kbias", [P, 2])
        if cfg.bias:
            vbias, obias = sb("vbias", [1, C]), sb("obias", [1, C])
        if cfg.gate:
            wg = sb("wg", [P, cfg.width])
            gate, gate_sig = sb("gate", [P, 2, TB, cfg.width]), sb("gate_sig", [P, TB, cfg.width])
        xcur = sb("xcur", [P, 2, T])
        flat, rest = sb("flat", [P, 2, T]), sb("rest", [P, T])
        parts = sb("parts", [P, TILES, 3, T], BF16)
        q, k = sb("q", [P, 2, CH, QT, T], BF16), sb("k", [P, 2, CH, KT, T], BF16)
        keep = sb("keep", [P, 1])
        v = sb("v", [P, 2, TB, KV, ST])
        v_cols = v[:].rearrange("p b j h d -> p (b j h) d")
        out_T = sb("out_T", [P, T])
        maxima = sb("maxima", [P, TB, HG])
        max_parts = sb("max_parts", [P, TB, MAX_TILES, P], BF16)
        max_cols = max_parts[:].rearrange("p j t (e s) -> p j (t e) s", e=cfg.lanes)
        probs = sb("probs", [P, SLOTS, T])
        recip = sb("recip", [P, 2, TB, HG])
        y, yT = sb("y", [P, TB, cfg.width]), sb("yT", [P, cfg.halves, T])

        max_bank = core.psum(ctx, "max_bank", [P, 2, T])
        score_bank = core.psum(ctx, "score_bank", [P, SCORE_BANKS, T])
        out_bank = core.psum(ctx, "out_bank", [P, T])
        spare_banks = core.psum(ctx, "spare_banks", [P, 2, T])

        KW = cfg.kv_width
        minus_loads = []
        loads = [(keep[:, :], w["keep"]), (wv[:, :], w["wv"]), (wo[:, :, :], w["wo"].rearrange("(h p) c -> p h c", p=P))]
        for place in range(2):
            for lane in range(cfg.lanes):
                row = lane * cfg.lane + cfg.max_row
                minus_loads.append((k[row:row + MAX_PARTS, place, CH - 1], w["minus"]))
        for sw in range(1 + cfg.rope):
            tail = "_swap" if sw else ""
            loads.append((wq[:, sw], w["wq" + tail].rearrange("c (h p) -> c h p", p=P)))
            loads.append((wk[:, sw, 0:KW], w["wk" + tail]))
            if cfg.bias and cfg.rope:
                loads.append((qbias[:, sw, :], w["bq" + tail].rearrange("(p h) -> p h", h=1)))
                loads.append((kbias[:, sw:sw + 1], w["bk" + tail].rearrange("(p h) -> p h", h=1)))
        if cfg.rope:
            loads += [(cos[:, :], w["cos"]), (sin[:, :], w["sin"])]
        if cfg.bias:
            loads += [(vbias[:, :], w["bv"].rearrange("(a c) -> a c", a=1)), (obias[:, :], w["bo"].rearrange("(a c) -> a c", a=1))]
        if cfg.gate:
            loads.append((wg[:, :], w["wg"]))
        LOADED = 16 * len(loads)
        clears = [(wk[:, :, KW:P], 0.0)] if KW < P else []
        clears += [(qbias[:], 0.0), (kbias[:], 0.0)] if cfg.rope and not cfg.bias else []
        WEIGHTS_CLEARED = len(clears)
        clears += [(max_parts[:], 0.0), (v_cols[:, :, D:D + 1], 1.0),
                   (v_cols[:, :, D + 1:ST], 0.0)]

        block = ctx.enter_context(nc.Block())

        @block.sync
        def _(sp):
            sp.dma_start(xcur[:, 0, :], core.xT[:, 0:T]).then_inc(xcur_ready[0], 16)
            for dst, src in loads:
                sp.dma_start(dst, src).then_inc(weights_loaded, 16)
            sp.dma_start(xcur[:, 1, :], core.xT[:, T:2 * T]).then_inc(xcur_ready[1], 16)
            sp.wait_ge(stacks_cleared, 2)
            for dst, src in minus_loads:
                sp.dma_start(dst, src).then_inc(minus_loaded, 16)

            def stack(b, place):
                for t, (what, at) in enumerate(cfg.tiles):
                    sp.wait_ge(parts_ready, b * TILES + t + 1)
                    rows = KW if what == "k" else P
                    sp.dma_start(w["scratch"][place, t, :, 0:rows].rearrange("s p t -> p s t"), parts[0:rows, t])\
                      .then_inc(parts_written[t], 16)
                    if t == 0 and not (isinstance(b, int) and b < 2):
                        sp.wait_ge(scores_full, (b - 1) * (G * NOPS))
                    sp.wait_ge(parts_written[t], b * 16 + 16)
                    stacks, heads = (k, KT) if what == "k" else (q, QT // cfg.halves)
                    for stack_rows, c, part, lane in copies(what):
                        src = w["scratch"][place, t, part, 0:rows].rearrange("(h e d) t -> e d h t", e=cfg.lanes, d=D)[lane]
                        sp.dma_start(stacks[stack_rows, place, c, at * heads:(at + 1) * heads], src)\
                          .then_inc(stacks_ready[place], 16)

            def refill(b, place):
                full(sp, b, -1)
                sp.dma_start(xcur[:, place, :], core.xT[:, ds((b + 2) * T, T)]).then_inc(xcur_ready[place], 16)

            stack(0, 0)
            refill(0, 0)
            stack(1, 1)
            with sp.Fori(0, (B - 4) // 2) as i:
                refill(i * 2 + 1, 1)
                stack(i * 2 + 2, 0)
                refill(i * 2 + 2, 0)
                stack(i * 2 + 3, 1)
            refill(B - 3, 1)
            stack(B - 2, 0)
            stack(B - 1, 1)
            for t in range(TILES):
                sp.wait_ge(parts_written[t], 16 * B)
            for place in range(2):
                sp.wait_ge(stacks_ready[place], 16 * READS * (B // 2))

        @block.tensor
        def _(pe):
            def bank_item(body, n, b, item, place):
                what, at, swapped = item
                bank, nth = slot(body, n)
                spare = spare_banks[:, bank, :]
                if not (isinstance(nth, int) and nth == 0):
                    pe.wait_ge(spare_free[bank], nth)
                if item == PREP[0]:
                    pe.wait_ge(xcur_ready[place], (b - place) * 8 + 16)
                if what in "qk":
                    weights = wq[:, swapped, at, :] if what == "q" else wk[:, swapped, :]
                    last = nc.tensor.matmul(spare, weights, xcur[:, place, :], start=True, stop=True)
                elif what == "v":
                    width = KV * D
                    for m, j in enumerate(cfg.v_blocks(at)):
                        out = spare[:, m * width:(m + 1) * width]
                        last = nc.tensor.matmul(out, xcur[:, place, j * P:(j + 1) * P], wv[:, :], start=True, stop=not cfg.bias)
                        if cfg.bias:
                            last = nc.tensor.matmul(out, core.ones_row[:, :], vbias[:, :], start=False, stop=True)
                elif what == "gate":
                    width = cfg.width
                    for j in range(2):
                        last = nc.tensor.matmul(spare[:, j * width:(j + 1) * width],
                                                xcur[:, place, (2 * at + j) * P:(2 * at + j + 1) * P],
                                                wg[:, :], start=True, stop=True)
                elif what == "turn_out":
                    pe.wait_ge(out_copied, b * G + at + 1)
                    for j in range(TB):
                        last = nc.tensor.transpose(spare[:, j * P:(j + 1) * P], out_T[:, j * P:(j + 1) * P], core.ident[:, :])
                elif what == "turn_y":
                    if at == 0 and cfg.gate:
                        pe.wait_ge(gated, b + 1)
                    elif at == 0:
                        out_of_bank(pe, body, n - 1)
                    for j in range(TB):
                        last = nc.tensor.transpose(spare[:, j * P:(j + 1) * P], y[:, j, at * P:(at + 1) * P], core.ident[:, :])
                elif what == "project":
                    out_of_bank(pe, body, n - 1)
                    for j in range(TB):
                        out = spare[:, j * P:(j + 1) * P]
                        for h in range(cfg.halves):
                            last = nc.tensor.matmul(out, yT[:, h, j * P:(j + 1) * P], wo[:, h, :], start=(h == 0),
                                                    stop=(h == cfg.halves - 1 and not cfg.bias))
                        if cfg.bias:
                            last = nc.tensor.matmul(out, core.ones_row[:, :], obias[:, :], start=False, stop=True)
                elif what == "norm":
                    pe.wait_ge(xn_ready, b + 1)
                    last = norm_turn(nc, core, spare)
                last.then_inc(spare_full[bank], 1)

            def unit(n, g, place, u):
                j, heads = cfg.units[u]
                if not (isinstance(n, int) and n == 0 and u < 2):
                    pe.wait_ge(max_free, n * NUNITS + u - 1)
                cols = (j + 1) * P if cfg.causal else T
                for at, r in enumerate(heads):
                    h = g * HG + r
                    bank = max_bank[:, max_bank_of(g, u), at * cols:(at + 1) * cols]
                    for c in range(CH):
                        rows = cfg.lane_rows(h, c, False)
                        last = nc.tensor.matmul(bank, q[rows, place, c, h // cfg.lanes, j * P:(j + 1) * P],
                                                k[rows, place, c, cfg.khead(h) // cfg.lanes, 0:cols],
                                                start=(c == 0), stop=(c == CH - 1 and not cfg.causal))
                    if cfg.causal:
                        last = nc.tensor.matmul(bank[:, j * P:(j + 1) * P], core.ident16[:, :], core.mask_ij[:, :],
                                                start=False, stop=True)
                last.then_inc(max_full, 1)

            def turn_maxima(body, index, m, n):
                if m == 0:
                    pe.wait_ge(max_parts_ready, n + 1)
                bank, nth = slot(body, index)
                pe.wait_ge(spare_free[bank], nth)
                for j in range(TB):
                    last = nc.tensor.matmul(spare_banks[:, bank, j * P:(j + 1) * P], max_parts[:, j, m, :],
                                            core.ident16[:, :], start=True, stop=True)
                last.then_inc(spare_full[bank], 1)

            def scores(n, g, place, o, maxima_items):
                r, cut = cfg.ops[o]
                h = g * HG + r
                if o == 0:
                    for m in range(MAX_TILES):
                        out_of_bank(pe, maxima_items[0], maxima_items[1] + m)
                before = score_bank_before(n, o)
                if before is not None:
                    pe.wait_ge(exp_done, before)
                for j, first, at in cfg.segments(cut)[0]:
                    width = T - first * P
                    bank = score_bank[:, o % SCORE_BANKS, at:at + width]
                    for c in range(CH):
                        rows = cfg.lane_rows(h, c, True)
                        last = nc.tensor.matmul(bank, k[rows, place, c, cfg.khead(h) // cfg.lanes, j * P:(j + 1) * P],
                                                q[rows, place, c, h // cfg.lanes, first * P:T],
                                                start=(c == 0), stop=(c == CH - 1 and not cfg.causal))
                    if cfg.causal:
                        last = nc.tensor.matmul(bank[:, 0:P], core.ident16[:, :], core.mask_ji[:, :],
                                                start=False, stop=True)
                last.then_inc(scores_full, 1)

            def values(n, g, place, o):
                r, cut = cfg.ops[o]
                pe.wait_ge(exp_done, n * NOPS + o + 1)
                if o == 0 and not (isinstance(n, int) and n == 0):
                    pe.wait_ge(out_copied, n)
                for j, first, at in cfg.segments(cut)[0]:
                    last = nc.tensor.matmul(out_bank[ST * r:ST * (r + 1), first * P:T], v[:, place, j, cfg.khead(g * HG + r), :],
                                            probs[:, (g * NOPS + o) % SLOTS, at:at + T - first * P],
                                            start=(j == 0), stop=(cut == cfg.ops[-1][1] and j == cut[-1]),
                                            skip_group_check=True)
                last.then_inc(pv_done, 1)

            def body(b, place, epilogue, prep):
                plan = cfg.plan(epilogue, prep)
                index = 0
                if isinstance(b, int) and b == 0:
                    maxima_items = (-1, len(PREP))
                else:
                    maxima_items = (b, -MAX_TILES)
                for g in range(G):
                    n = b * G + g
                    more = prep or g < G - 1
                    g1, place1, b1 = (g + 1, place, b) if g < G - 1 else (0, 1 - place, b + 1)
                    for o in range(NOPS):
                        if more and o == 0 and g == G - 1:
                            pe.wait_ge(stacks_ready[place1], (b1 - place1) * (8 * READS) + 16 * READS)
                        units = units_at(o) if more else []
                        for u in units[:len(units) // 2]:
                            unit(n + 1, g1, place1, u)
                        scores(n, g, place, o, maxima_items)
                        for u in units[len(units) // 2:]:
                            unit(n + 1, g1, place1, u)
                        for item in plan[g][o]:
                            if item[0] == "maxima":
                                turn_maxima(b, index, item[1], n + 1)
                                next_maxima = (b, index - item[1])
                            else:
                                bank_item(b, index, cfg.batch_of(item, b, g), item, 1 - place)
                            index += 1
                        if o > 0:
                            values(n, g, place, o - 1)
                        elif g > 0:
                            values(n - 1, g - 1, place, NOPS - 1)
                        elif epilogue:
                            values(n - 1, G - 1, 1 - place, NOPS - 1)
                    if more:
                        maxima_items = next_maxima

            pe.wait_ge(weights_loaded, LOADED)
            if WEIGHTS_CLEARED:
                pe.wait_ge(cleared, WEIGHTS_CLEARED)
            for n, item in enumerate(PREP):
                bank_item(-1, n, 0, item, 0)
            pe.wait_ge(cleared, len(clears))
            pe.wait_ge(minus_loaded, 16 * len(minus_loads))
            pe.wait_ge(stacks_ready[0], 16 * READS)
            for u in range(NUNITS):
                unit(0, 0, 0, u)
            for m in range(MAX_TILES):
                turn_maxima(-1, len(PREP) + m, m, 0)
            bodies(pe, body)
            values(B * G - 1, G - 1, 1, NOPS - 1)
            for n, item in enumerate(cfg.end()):
                bank_item(B - 1, LAST + n, B - 1, item, 1)

        @block.scalar
        def _(act):
            def bank_item(body, n, b, item, place, tile):
                what, at, swapped = item
                bank, nth = slot(body, n)
                spare = spare_banks[:, bank, :]
                if what in ("turn_y", "norm", "v", "gate") or (what in "qk" and not cfg.rope):
                    act.wait_ge(spare_full[bank], nth + 1)
                if what == "turn_y":
                    nc.scalar.copy(yT[:, at, :], spare).then_inc(spare_free[bank], 1)
                elif what == "norm":
                    nc.scalar.copy(core.xT[:, ds(b * T, T)], spare).then_inc(spare_free[bank], 1)
                elif what == "v":
                    blocks = cfg.v_blocks(at)
                    nc.scalar.copy(v[:, place, blocks[0]:blocks[-1] + 1, :, 0:D],
                                   spare[:, 0:len(blocks) * KV * D].rearrange("p (j h d) -> p j h d", j=len(blocks), h=KV))\
                      .then_inc(spare_free[bank], 1)
                elif what == "gate":
                    raw = spare.rearrange("p (j c) -> p j c", j=2)
                    nc.scalar.activation(gate_sig[:, 2 * at:2 * at + 2, :], raw, ACT.Exp, scale=-1.0)
                    nc.scalar.copy(gate[:, place, 2 * at:2 * at + 2, :], raw).then_inc(spare_free[bank], 1)
                elif what in "qk" and not cfg.rope:
                    if not (isinstance(b, int) and b == 0):
                        act.wait_ge(parts_ready, b * TILES)
                    nc.scalar.copy(flat[:, tile, :], spare)
                    if not (isinstance(b, int) and b == 0):
                        act.wait_ge(parts_written[tile], b * 16)
                    nc.scalar.copy(parts[:, tile, HIGH], spare).then_inc(spare_free[bank], 1)
                    return 1
                return 0

            def exponentials(n, g, o):
                width = cfg.segments(cfg.ops[o][1])[1]
                act.wait_ge(scores_full, n * NOPS + o + 1)
                if not (isinstance(n, int) and n * NOPS + o < SLOTS):
                    act.wait_ge(pv_done, n * NOPS + o + 1 - SLOTS)
                nc.scalar.activation(probs[:, (g * NOPS + o) % SLOTS, 0:width], score_bank[:, o % SCORE_BANKS, 0:width], ACT.Exp,
                                     scale=cfg.scale).then_inc(exp_done, 1)

            def copy_outputs(n):
                act.wait_ge(pv_done, (n + 1) * NOPS)
                if not (isinstance(n, int) and n == 0):
                    act.wait_ge(recip_ready, n)
                nc.scalar.copy(out_T[:, :], out_bank[:, :]).then_inc(out_copied, 1)

            def body(b, place, epilogue, prep):
                plan = cfg.plan(epilogue, prep)
                index = tile = 0
                for g in range(G):
                    for o in range(NOPS):
                        exponentials(b * G + g, g, o)
                        if o == 0 and (g > 0 or epilogue):
                            copy_outputs(b * G + g - 1)
                        for item in plan[g][o]:
                            tile += bank_item(b, index, cfg.batch_of(item, b, g), item, 1 - place, tile)
                            index += 1

            tile = 0
            for n, item in enumerate(PREP):
                tile += bank_item(-1, n, 0, item, 0, tile)
            bodies(act, body)
            copy_outputs(B * G - 1)
            for n, item in enumerate(cfg.end()):
                bank_item(B - 1, LAST + n, B - 1, item, 1, 0)

        @block.gpsimd
        def _(pool):
            for tile, value in clears:
                nc.gpsimd.memset(tile, value).then_inc(cleared, 1)

            def split(body, n, b, tile):
                whole, mine = flat[:, tile % 2, :], parts[:, tile]
                split_chain.at((b * TILES + tile) * SPLIT_STEPS)
                out_of_bank(pool, body, n)
                if cfg.rope:
                    if not (isinstance(b, int) and b == 0):
                        pool.wait_ge(parts_written[tile], b * 16)
                    nc.gpsimd.tensor_tensor(mine[:, HIGH], turned[:, tile % 2, 0, :], turned[:, tile % 2, 1, :], ALU.add)
                    split_chain.inc(nc.gpsimd.tensor_tensor(whole, turned[:, tile % 2, 0, :], turned[:, tile % 2, 1, :], ALU.add))
                    split_chain.settle(pool)
                elif not (isinstance(b, int) and b == 0 and tile == 0):
                    pool.wait_ge(parts_ready, b * TILES + tile)
                nc.gpsimd.tensor_tensor(mine[:, MIDDLE_PART], whole, mine[:, HIGH], ALU.subtract)
                split_chain.inc(nc.gpsimd.tensor_tensor(rest[:, :], whole, mine[:, HIGH], ALU.subtract))
                split_chain.settle(pool)
                nc.gpsimd.tensor_tensor(mine[:, LOW], rest[:, :], mine[:, MIDDLE_PART], ALU.subtract).then_inc(parts_ready, 1)

            def bank_item(body, n, b, item, place, tile):
                what, at, swapped = item
                if what in "qk" and swapped == cfg.rope:
                    split(body, n, b, tile)
                    return 1
                if what == "gate" and at == 1:
                    pool.wait_ge(gate_recip_ready, b + 1)
                    nc.gpsimd.tensor_tensor(gate[:, place], gate[:, place], gate_sig[:, :, :], ALU.mult).then_inc(gate_ready, 1)
                if what == "turn_out" and at == G - 1 and cfg.gate:
                    out_of_bank(pool, body, n)
                    pool.wait_ge(gate_ready, b + 1)
                    nc.gpsimd.tensor_tensor(y[:, :, :], y[:, :, :], gate[:, place], ALU.mult).then_inc(gated, 1)
                if what == "project":
                    pool.wait_ge(var_ready, b + 1)
                    norm_rstd(nc, core).then_inc(rstd_ready, 1)
                return 0

            def body(b, place, epilogue, prep):
                plan = cfg.plan(epilogue, prep)
                index = tile = 0
                for g in range(G):
                    for o in range(NOPS):
                        for item in plan[g][o]:
                            tile += bank_item(b, index, cfg.batch_of(item, b, g), item, 1 - place, tile)
                            index += 1

            tile = 0
            for n, item in enumerate(PREP):
                tile += bank_item(-1, n, 0, item, 0, tile)
            bodies(pool, body)
            for n, item in enumerate(cfg.end()):
                bank_item(B - 1, LAST + n, B - 1, item, 1, 0)

        @block.vector
        def _(dve):
            def bank_item(body, n, b, item, place, tile):
                what, at, swapped = item
                bank, nth = slot(body, n)
                spare = spare_banks[:, bank, :]
                if what in "qk" and cfg.rope:
                    dve.wait_ge(spare_full[bank], nth + 1)
                    if not swapped and not (isinstance(b, int) and b == 0 and tile < 2):
                        dve.wait_ge(parts_ready, b * TILES + max(tile - 1, 0))
                    bias = qbias[:, swapped, at:at + 1] if what == "q" else kbias[:, swapped:swapped + 1]
                    nc.vector.scalar_tensor_tensor(turned[:, tile % 2, swapped, :], spare, bias,
                                                   (sin if swapped else cos)[:, :], ALU.add, ALU.mult).then_inc(spare_free[bank], 1)
                    return swapped
                if what == "gate" and at == 1:
                    out_of_bank(dve, body, n)
                    nc.vector.tensor_scalar(gate_sig[:, :, :], gate_sig[:, :, :], 1.0, None, ALU.add).then_inc(gate_sum_ready, 1)
                    dve.wait_ge(gate_sum_ready, b + 1)
                    nc.vector.reciprocal(gate_sig[:, :, :], gate_sig[:, :, :]).then_inc(gate_recip_ready, 1)
                if what == "turn_out":
                    take_outputs(bank, nth, b * G + at, at)
                if what == "project":
                    dve.wait_ge(spare_full[bank], nth + 1)
                    tokens = core.x[:, ds(b * TB, TB), :]
                    nc.vector.tensor_tensor(tokens, spare.rearrange("p (j c) -> p j c", j=TB), tokens, ALU.add)\
                      .then_inc(spare_free[bank], 1)
                    out_of_bank(dve, body, n)
                    chain.at(b * NORM_STEPS)
                    norm_stats(nc, dve, core, chain, b).then_inc(var_ready, 1)
                return 0

            def reduce(n, g, u):
                j, heads = cfg.units[u]
                dve.wait_ge(max_full, n * NUNITS + u + 1)
                cols = (j + 1) * P if cfg.causal else T
                found = max_bank[:, max_bank_of(g, u), 0:len(heads) * cols].rearrange("p (r c) -> p r c", c=cols)
                nc.vector.tensor_reduce(maxima[:, j, heads[0]:heads[-1] + 1:cfg.lanes], found, AX_X, ALU.max).then_inc(max_free, 1)

            def split_maxima(n):
                dve.wait_ge(max_free, (n + 1) * NUNITS)
                high, rest_of = (max_cols[:, :, :, cfg.max_row + m] for m in range(MAX_PARTS))
                nc.vector.tensor_copy(high, maxima[:, :, :]).then_inc(max_high_ready, 1)
                dve.wait_ge(max_high_ready, n + 1)
                nc.vector.tensor_tensor(rest_of, maxima[:, :, :], high, ALU.subtract).then_inc(max_parts_ready, 1)

            def add_maxima(body, index, m, g, place):
                full(dve, body, index)
                bank, _ = slot(body, index)
                tile = q[:, place, CH - 1, g * MAX_TILES + m, :]
                nc.vector.scalar_tensor_tensor(tile, tile, keep[:, 0:1], spare_banks[:, bank, :], ALU.mult, ALU.add)\
                  .then_inc(spare_free[bank], 1)

            def take_outputs(bank, nth, n, g):
                outs = spare_banks[:, bank, :].rearrange("p (j r d) -> p j r d", j=TB, r=HG)
                dve.wait_ge(spare_full[bank], nth + 1)
                nc.vector.reciprocal(recip[:, g % 2], outs[:, :, :, D]).then_inc(recip_ready, 1)
                dve.wait_ge(recip_ready, n + 1)
                mine = y[:, :, g * HG * D:(g + 1) * HG * D].rearrange("p j (r d) -> p j r d", r=HG)
                nc.vector.tensor_tensor(mine, outs[:, :, :, 0:D], recip[:, g % 2].unsqueeze(3).to_broadcast([P, TB, HG, D]),
                                        ALU.mult).then_inc(spare_free[bank], 1)

            def apply_norm(b):
                dve.wait_ge(rstd_ready, b + 1)
                norm_apply(nc, core, b).then_inc(xn_ready, 1)

            def body(b, place, epilogue, prep):
                plan = cfg.plan(epilogue, prep)
                index = tile = 0
                for g in range(G):
                    n = b * G + g
                    more = prep or g < G - 1
                    g1, place1 = (g + 1, place) if g < G - 1 else (0, 1 - place)
                    for o in range(NOPS):
                        if more:
                            for u in units_at(o):
                                reduce(n + 1, g1, u)
                        if epilogue and g == 1 and o == 0:
                            apply_norm(b - 1)
                        for item in plan[g][o]:
                            if item[0] == "maxima":
                                add_maxima(b, index, item[1], g1, place1)
                            else:
                                tile += bank_item(b, index, cfg.batch_of(item, b, g), item, 1 - place, tile)
                            index += 1
                        if more and o == NOPS - 3:
                            split_maxima(n + 1)

            for tile in (k, q):
                nc.vector.memset(tile[:, :, CH - 1], 0.0).then_inc(stacks_cleared, 1)
            dve.wait_ge(weights_loaded, LOADED)
            if WEIGHTS_CLEARED:
                dve.wait_ge(cleared, WEIGHTS_CLEARED)
            tile = 0
            for n, item in enumerate(PREP):
                tile += bank_item(-1, n, 0, item, 0, tile)
            dve.wait_ge(cleared, len(clears))
            for u in range(NUNITS):
                reduce(0, 0, u)
            split_maxima(0)
            for m in range(MAX_TILES):
                add_maxima(-1, len(PREP) + m, m, 0, 0)
            bodies(dve, body)
            for n, item in enumerate(cfg.end()):
                bank_item(B - 1, LAST + n, B - 1, item, 1, 0)
            apply_norm(B - 1)



def choose(nc, dve, chain, left, scratch, order, best, top, onehot):
    shape = [P, B * TB, left.shape[2]]
    chain.inc(nc.vector.tensor_reduce(top, left, AX_X, ALU.max))
    chain.settle(dve)
    chain.inc(nc.vector.tensor_tensor(scratch, left, top.unsqueeze(2).to_broadcast(shape), ALU.is_equal))
    chain.settle(dve)
    chain.inc(nc.vector.tensor_tensor(scratch, scratch, order.unsqueeze(1).to_broadcast(shape), ALU.mult))
    chain.settle(dve)
    chain.inc(nc.vector.tensor_reduce(best, scratch, AX_X, ALU.max))
    chain.settle(dve)
    chain.inc(nc.vector.tensor_tensor(onehot, scratch, best.unsqueeze(2).to_broadcast(shape), ALU.is_equal))
    chain.settle(dve)


def stage_ffn(core, w, experts, hidden):
    nc = core.nc
    E = experts
    gated = hidden is not None
    CHUNKS = -(-hidden // P) if gated else 0
    H = [min(P, hidden - c * P) for c in range(CHUNKS)] if gated else []
    names = ("weights_loaded", "xcur_even", "xcur_odd", "order_ready", "logits_full", "diff_ready", "exp_ready",
             "up_full", "silu_done", "hidden_done", "down_full", "combined", "var_ready", "rstd_ready", "xn_ready",
             "turned", "taken", "mixed_full", "mixed_taken", "router_loaded")
    (weights_loaded, xcur_even, xcur_odd, order_ready, logits_full, diff_ready, exp_ready, up_full, silu_done,
     hidden_done, down_full, combined, var_ready, rstd_ready, xn_ready, turned, taken, mixed_full,
     mixed_taken, router_loaded) = (core.sem(n) for n in names)
    xcur_ready = [xcur_even, xcur_odd]
    route_chain, chain = Count(core.sem("route_chain")), Count(core.sem("ffn_chain"))

    with ExitStack() as ctx:
        def sb(name, shape, dtype=F32):
            return core.sbuf(ctx, name, shape, dtype)

        N = B * TB
        router = sb("router", [P, E])
        logits, scratch = sb("logits", [P, N, E]), sb("scratch", [P, N, E])
        first, second, gates = sb("first", [P, N, E]), sb("second", [P, N, E]), sb("gates", [P, N, E])
        top, best = sb("top", [P, 2, N]), sb("best", [P, N])
        share, total = sb("share", [P, 2, N]), sb("total", [P, N])
        order = sb("order", [P, E])
        xcur = sb("xcur", [P, 2, T])
        loads = []
        if gated:
            wg, wu, wd = sb("wg", [P, E, hidden]), sb("wu", [P, E, hidden]), sb("wd", [P, E, CHUNKS, C])
            silu, hid = sb("silu", [P, 2, T]), sb("hidden", [P, 2, CHUNKS, T])
            gate_bank, up_bank = core.psum(ctx, "gate_bank", [P, 2, T]), core.psum(ctx, "up_bank", [P, 2, T])
            loads += [(wg[:, :, :], w["wg"].rearrange("e c i -> c e i")), (wu[:, :, :], w["wu"].rearrange("e c i -> c e i"))]
            loads += [(wd[0:H[c], :, c, :], w["wd"][:, c * P:c * P + H[c], :].rearrange("e i c -> i e c")) for c in range(CHUNKS)]
        else:
            F = w["w_in"].shape[1] // P
            w_in, w_out, both = sb("w_in", [P, E, F, C]), sb("w_out", [P, E, F, C]), sb("w_both", [P, E, C])
            mixed_bank = core.psum(ctx, "mixed_bank", [P, 2, T])
            loads += [(w_in[:, :, :, :], w["w_in"].rearrange("e (f p) c -> p e f c", p=P)),
                      (w_out[:, :, :, :], w["w_out"].rearrange("e (f p) c -> p e f c", p=P))]
        down_bank = core.psum(ctx, "down_bank", [P, 2, T])
        logits_bank, norm_bank = core.psum(ctx, "logits_bank", [P, T]), core.psum(ctx, "norm_bank", [P, T])
        logits_view = logits_bank[:, 0:N * E].rearrange("p (n e) -> p n e", e=E)

        def bodies(eng, emit):
            emit(0, 0, True)
            with eng.Fori(0, (B - 2) // 2) as i:
                emit(i * 2 + 1, 1, False)
                emit(i * 2 + 2, 0, False)
            emit(B - 1, 1, False)

        def e_parity(place, e):
            return (place * E + e) % 2

        def chunk_parity(place, m):
            return (place * E * CHUNKS + m) % 2

        block = ctx.enter_context(nc.Block())

        @block.sync
        def _(sp):
            sp.dma_start(router[:, :], w["router"]).then_inc(router_loaded, 16)
            for dst, src in loads:
                sp.dma_start(dst, src).then_inc(weights_loaded, 16)
            for b in (0, 1):
                sp.dma_start(xcur[:, b, :], core.xT[:, b * T:(b + 1) * T]).then_inc(xcur_ready[b], 16)
            with sp.Fori(0, (B - 2) // 2) as i:
                for u in range(2):
                    sp.wait_ge(down_full, (i * 2 + u + 1) * E)
                    sp.dma_start(xcur[:, u, :], core.xT[:, ds((i * 2 + u + 2) * T, T)]).then_inc(xcur_ready[u], 16)

        @block.gpsimd
        def _(pool):
            nc.gpsimd.iota(order[:, :], pattern=[[-1, E]], base=E, channel_multiplier=0,
                           allow_small_or_imprecise_dtypes=True).then_inc(order_ready, 1)
            with pool.Fori(0, B) as b:
                pool.wait_ge(var_ready, b + 1)
                norm_rstd(nc, core).then_inc(rstd_ready, 1)

        @block.tensor
        def _(pe):
            def down(b, place, e):
                if not (isinstance(b, int) and b == 0 and e < 2):
                    pe.wait_ge(combined, b * E + e - 1)
                if gated:
                    pe.wait_ge(hidden_done, (b * E + e + 1) * CHUNKS)
                for j in range(TB):
                    out = down_bank[:, e_parity(place, e), j * C:(j + 1) * C]
                    if gated:
                        for c in range(CHUNKS):
                            last = nc.tensor.matmul(out, hid[0:H[c], e_parity(place, e), c, j * P:(j + 1) * P],
                                                    wd[0:H[c], e, c, :], start=(c == 0), stop=(c == CHUNKS - 1))
                    else:
                        last = nc.tensor.matmul(out, xcur[:, place, j * P:(j + 1) * P], both[:, e, :], start=True, stop=True)
                last.then_inc(down_full, 1)

            def up(b, place, e):
                for c in range(CHUNKS):
                    m = e * CHUNKS + c
                    if not (isinstance(b, int) and b == 0 and m < 2):
                        pe.wait_ge(hidden_done, b * E * CHUNKS + m - 1)
                    cols = slice(c * P, c * P + H[c])
                    bank = chunk_parity(place, m)
                    nc.tensor.matmul(gate_bank[0:H[c], bank, :], wg[:, e, cols], xcur[:, place, :], start=True, stop=True)
                    nc.tensor.matmul(up_bank[0:H[c], bank, :], wu[:, e, cols], xcur[:, place, :],
                                     start=True, stop=True).then_inc(up_full, 1)

            def turn(b):
                pe.wait_ge(xn_ready, b + 1)
                if not (isinstance(b, int) and b == 0):
                    pe.wait_ge(taken, b)
                norm_turn(nc, core, norm_bank).then_inc(turned, 1)

            def body(b, place, is_first):
                pe.wait_ge(xcur_ready[place], (b - place) * 8 + 16)
                if gated:
                    up(b, place, 0)
                for e in range(E):
                    if gated and e + 1 < E:
                        up(b, place, e + 1)
                    down(b, place, e)
                    if e == 1 and not is_first:
                        turn(b - 1)

            pe.wait_ge(router_loaded, 16)
            for n in range(N):
                last = nc.tensor.matmul(logits_view[:, n, :], core.xT[:, n * P:(n + 1) * P], router[:, :], start=True, stop=True)
            last.then_inc(logits_full, 1)
            pe.wait_ge(weights_loaded, 16 * len(loads))
            if not gated:
                for e in range(E):
                    if e >= 2:
                        pe.wait_ge(mixed_taken, e - 1)
                    for f in range(F):
                        last = nc.tensor.matmul(mixed_bank[:, e % 2, 0:C], w_in[:, e, f, :], w_out[:, e, f, :],
                                                start=(f == 0), stop=(f == F - 1))
                    last.then_inc(mixed_full, 1)
                pe.wait_ge(mixed_taken, E)
            bodies(pe, body)
            turn(B - 1)

        @block.scalar
        def _(act):
            if not gated:
                for e in range(E):
                    act.wait_ge(mixed_full, e + 1)
                    nc.scalar.copy(both[:, e, :], mixed_bank[:, e % 2, 0:C]).then_inc(mixed_taken, 1)
            act.wait_ge(diff_ready, 1)
            nc.scalar.activation(share[:, 1, :], share[:, 1, :], ACT.Exp).then_inc(exp_ready, 1)

            def take(b):
                act.wait_ge(turned, b + 1)
                nc.scalar.copy(core.xT[:, ds(b * T, T)], norm_bank[:, :]).then_inc(taken, 1)

            def body(b, place, is_first):
                for m in range(E * CHUNKS):
                    rows = H[m % CHUNKS]
                    bank = chunk_parity(place, m)
                    act.wait_ge(up_full, b * E * CHUNKS + m + 1)
                    if not (isinstance(b, int) and b == 0 and m < 2):
                        act.wait_ge(hidden_done, b * E * CHUNKS + m - 1)
                    nc.scalar.activation(silu[0:rows, bank, :], gate_bank[0:rows, bank, :], ACT.Silu).then_inc(silu_done, 1)
                    if m == 3 * CHUNKS and not is_first:
                        take(b - 1)
                if not gated and not is_first:
                    take(b - 1)

            bodies(act, body)
            take(B - 1)

        @block.vector
        def _(dve):
            def multiply(b, place, e):
                for c in range(CHUNKS):
                    m = e * CHUNKS + c
                    bank = chunk_parity(place, m)
                    if c == 0 and not (isinstance(b, int) and b == 0 and e < 2):
                        dve.wait_ge(down_full, b * E + e - 1)
                    dve.wait_ge(silu_done, b * E * CHUNKS + m + 1)
                    nc.vector.tensor_tensor(hid[0:H[c], e_parity(place, e), c, :], up_bank[0:H[c], bank, :],
                                            silu[0:H[c], bank, :], ALU.mult).then_inc(hidden_done, 1)

            def combine(b, place, e):
                dve.wait_ge(down_full, b * E + e + 1)
                if not (isinstance(b, int) and b == 0 and e == 0):
                    dve.wait_ge(combined, b * E + e)
                for j in range(TB):
                    tokens = core.x[:, ds(b * TB + j, 1), :].rearrange("p a c -> p (a c)")
                    last = nc.vector.scalar_tensor_tensor(
                        tokens, down_bank[:, e_parity(place, e), j * C:(j + 1) * C],
                        gates[:, ds(b * TB + j, 1), e:e + 1].rearrange("p a c -> p (a c)"), tokens, ALU.mult, ALU.add)
                last.then_inc(combined, 1)

            def body(b, place, is_first):
                if gated:
                    multiply(b, place, 0)
                for e in range(E):
                    if gated and e + 1 < E:
                        multiply(b, place, e + 1)
                    combine(b, place, e)
                dve.wait_ge(combined, (b + 1) * E)
                chain.at(b * NORM_STEPS)
                norm_stats(nc, dve, core, chain, b).then_inc(var_ready, 1)
                dve.wait_ge(rstd_ready, b + 1)
                if not is_first:
                    dve.wait_ge(turned, b)
                norm_apply(nc, core, b).then_inc(xn_ready, 1)

            def step(instruction):
                route_chain.inc(instruction)
                route_chain.settle(dve)

            dve.wait_ge(order_ready, 1)
            dve.wait_ge(logits_full, 1)
            step(nc.vector.tensor_copy(logits[:, :, :], logits_view))
            choose(nc, dve, route_chain, logits[:, :, :], scratch[:, :, :], order[:, :], best[:, :], top[:, 0, :], first[:, :, :])
            step(nc.vector.scalar_tensor_tensor(logits[:, :, :], first[:, :, :], -3e38, logits[:, :, :], ALU.mult, ALU.add))
            choose(nc, dve, route_chain, logits[:, :, :], scratch[:, :, :], order[:, :], best[:, :], top[:, 1, :], second[:, :, :])
            nc.vector.tensor_tensor(share[:, 1, :], top[:, 1, :], top[:, 0, :], ALU.subtract).then_inc(diff_ready, 1)
            dve.wait_ge(exp_ready, 1)
            step(nc.vector.tensor_scalar(total[:, :], share[:, 1, :], 1.0, None, ALU.add))
            step(nc.vector.reciprocal(share[:, 0, :], total[:, :]))
            step(nc.vector.tensor_tensor(share[:, 1, :], share[:, 1, :], share[:, 0, :], ALU.mult))
            step(nc.vector.tensor_tensor(first[:, :, :], first[:, :, :], share[:, 0, :].unsqueeze(2).to_broadcast([P, N, E]), ALU.mult))
            step(nc.vector.tensor_tensor(second[:, :, :], second[:, :, :], share[:, 1, :].unsqueeze(2).to_broadcast([P, N, E]), ALU.mult))
            step(nc.vector.tensor_tensor(gates[:, :, :], first[:, :, :], second[:, :, :], ALU.add))
            bodies(dve, body)



def stage_decay(core, w):
    nc = core.nc
    H, DH = 16, 64
    UNROLL = 2
    BLOCKS = (3, 2, 1, 0)
    WIDTH = [(i + 1) * P for i in range(TB)]
    START = [0, P, 3 * P, 6 * P]
    TOTAL = 10 * P
    ITEMS = (("qnorm", 0), ("knorm", 1), ("q", 1), ("q_swap", 1), ("k", 2), ("k_swap", 2), ("v", 1))
    AHEAD = (("k", 0), ("k_swap", 0), ("q", 0), ("q_swap", 0), ("v", 0), ("knorm", 0), ("k", 1), ("k_swap", 1))
    PACKED = ("k", "k_swap", "q", "q_swap", "v")
    FREE = (4, 3)
    TABLE_STEPS = 10
    TWO_PI = 6.283185307179586
    C1 = 6.28125
    C2 = float(np.round((TWO_PI - C1) * 2**21) / 2**21)
    C3 = TWO_PI - C1 - C2
    ROUND = 12582912.0
    HALF_PI, BOUND = TWO_PI / 4, 3.1415925

    names = ("inputs_loaded", "pack_even", "pack_odd", "wo_even", "wo_odd", "const_ready", "proj_full",
             "proj_free_0", "proj_free_1", "k_rotated", "q_rotated", "k_squared", "q_squared", "g_ready", "s_full", "a1_done", "a2_done", "relu_done",
             "r_done", "ln_done", "logit_done", "max_done", "exp_done", "t_full", "pt_free_0", "pt_free_1", "pv_full",
             "ot_done", "y_full", "x_done", "recip_done", "angle_ready", "phase_ready", "z_ready", "etab_ready",
             "v_ready", "lnv_ready", "tables_ready", "var_ready", "rstd_ready", "xn_ready", "turned", "taken",
             "soft_exp", "soft_ln", "mu_exp", "rtab_ready",
             "y_scaled")
    S = {n: core.sem(n) for n in names}
    proj_free, pt_free = (S["proj_free_0"], S["proj_free_1"]), (S["pt_free_0"], S["pt_free_1"])
    pack_ready, wo_ready = (S["pack_even"], S["pack_odd"]), (S["wo_even"], S["wo_odd"])
    table_chain, const_chain, chain = Count(core.sem("table_chain")), Count(core.sem("const_chain")), Count(core.sem("norm_chain"))

    def wait(eng, name, value):
        if not (isinstance(value, int) and value <= 0):
            eng.wait_ge(S[name] if isinstance(name, str) else name, value)

    def has_item(n, idx):
        return not (isinstance(n, int) and n + ITEMS[idx][1] >= H * B)

    def at(n, idx):
        bank = idx % 2
        left_out = [(s, t) for s in (H * B - 2, H * B - 1) for t in range(len(ITEMS)) if not has_item(s, t)]
        before = [t for s, t in left_out if isinstance(n, int) and (s, t) < (n, idx)]
        return (bank, len(AHEAD) // 2 + n * FREE[bank] + idx // 2 - len([t for t in before if t % 2 == bank]),
                len(AHEAD) + n * len(ITEMS) + idx + 1 - len(before))

    def ahead(idx):
        return idx % 2, idx // 2, idx + 1

    with ExitStack() as ctx:
        def sb(name, shape, dtype=F32):
            return core.sbuf(ctx, name, shape, dtype)

        pack, wo = sb("pack", [P, 2, 5, P]), sb("wo", [P, 2, C])
        cos, sin = sb("cos", [P, 2, T]), sb("sin", [P, 2, T])
        e_tab, r_tab, l_tab = sb("e_tab", [P, 2, T]), sb("r_tab", [P, 2, T]), sb("l_tab", [P, 2, T])
        steps, dist, mask = sb("steps", [P, T]), sb("dist", [P, T]), sb("mask", [P, T])
        angle, turns, folded = sb("angle", [P, T]), sb("turns", [P, T]), sb("folded", [P, T])
        z, var, lnv = sb("z", [P, T]), sb("var", [P, T]), sb("lnv", [P, T])
        ones, quarter = sb("ones", [P, P]), sb("quarter", [P, 1])
        sign, half_pi = sb("sign", [P, 1]), sb("half_pi", [P, 1])
        omega = sb("omega", [P, H])
        raw, soft, tmp = sb("raw", [P, 4, H]), sb("soft", [P, 4, H]), sb("tmp", [P, 4, H])
        mu_raw, tau, mu = sb("mu_raw", [P, H]), sb("tau", [P, H]), sb("mu", [P, H])
        neg_mu, amp, floor, coef, mu_recip = (sb(n, [P, H]) for n in ("neg_mu", "amp", "floor", "coef", "mu_recip"))
        parts = sb("parts", [P, 2, 2, T])
        q, k = sb("q", [P, 2, T]), sb("k", [P, 4, T])
        qsq, ksq = sb("qsq", [P, T]), sb("ksq", [P, T])
        knorm, g = sb("knorm", [P, T]), sb("g", [P, 2, TOTAL])
        qnorm = sb("qnorm", [P, 2, TB])
        v = sb("v", [P, 4, TB, P])
        u = sb("u", [P, 4, TOTAL])
        neg_max, rowsum, recip = sb("neg_max", [P, 4, TB]), sb("rowsum", [P, 4, TB]), sb("recip", [P, 2, TB])
        scaled = sb("scaled", [P, 2, TB, C])
        pT, oT = sb("pT", [P, 2, TB, T]), sb("oT", [P, 2, T])

        proj_bank = core.psum(ctx, "proj_bank", [P, 2, T])
        s_bank, t_bank = core.psum(ctx, "s_bank", [P, 2, T]), core.psum(ctx, "t_bank", [P, 2, T])
        o_bank, y_bank = core.psum(ctx, "o_bank", [P, T]), core.psum(ctx, "y_bank", [P, T])

        inputs = [(raw[:, n, :], w[name].partition_broadcast(P)) for n, name in enumerate(("sigma", "eta", "gamma", "nu"))]
        inputs += [(mu_raw[:, :], w["mu"].partition_broadcast(P)), (tau[:, :], w["tau"].partition_broadcast(P))]
        inputs += [(omega[32 * r:32 * r + 32, :], w["omega"]) for r in range(4)]

        def part(tile, i):
            return tile[:, START[i]:START[i] + WIDTH[i]]

        def table(tab, h, i):
            return tab[:, h, T - WIDTH[i]:T]

        def pipeline(eng, step):
            def body(i, last):
                for m in range(UNROLL * B):
                    step(i * (UNROLL * B) + m, m, i * UNROLL + m // B, m % B, last and m == UNROLL * B - 1)
            body(0, False)
            with eng.Fori(1, H // UNROLL - 1) as i:
                body(i, False)
            body(H // UNROLL - 1, True)

        def exists(n):
            return not (isinstance(n, int) and n < 0)

        def tables_wanted(h):
            return not (isinstance(h, int) and h == H - 1)

        def head_of(m):
            return (m // B) % 2

        block = ctx.enter_context(nc.Block())

        @block.sync
        def _(sp):
            for dst, src in inputs:
                sp.dma_start(dst, src).then_inc(S["inputs_loaded"], 16)
            for h in range(2):
                sp.dma_start(pack[:, h], w["pack"][h]).then_inc(pack_ready[h], 16)
                sp.dma_start(wo[:, h, :], w["wo"][h]).then_inc(wo_ready[h], 16)
            with sp.Fori(0, H // 2 - 1) as i:
                for p in range(2):
                    h = i * 2 + p
                    sp.wait_ge(S["proj_full"], at((h + 1) * B - 2, len(ITEMS) - 1)[2])
                    sp.dma_start(pack[:, p], w["pack"][ds(h + 2, 1)].rearrange("a c m n -> (a c) m n")).then_inc(pack_ready[p], 16)
                    sp.wait_ge(S["y_full"], (h + 1) * B)
                    sp.dma_start(wo[:, p, :], w["wo"][ds(h + 2, 1)].rearrange("a c n -> (a c) n")).then_inc(wo_ready[p], 16)

        @block.tensor
        def _(pe):
            def project(place, what, n, m, h, b):
                p = head_of(m)
                bank, before, _ = place
                if what == "k" and b == 0:
                    pe.wait_ge(pack_ready[p], (h - p) * 8 + 16)
                wait(pe, proj_free[bank], before)
                out = proj_bank[:, bank, :]
                if what == "v":
                    for j in range(TB):
                        last = nc.tensor.matmul(out[:, j * P:(j + 1) * P], core.xT[:, b * T + j * P:b * T + (j + 1) * P],
                                                pack[:, p, PACKED.index(what), :], start=True, stop=True)
                elif what == "knorm":
                    pe.wait_ge(S["k_squared"], n + 1)
                    last = nc.tensor.matmul(out, ones[:, :], ksq[:, :], start=True, stop=True)
                elif what == "qnorm":
                    pe.wait_ge(S["q_squared"], n + 1)
                    for j in range(TB):
                        last = nc.tensor.matmul(out[:, j:j + 1], qsq[:, j * P:(j + 1) * P], quarter[:, :], start=True, stop=True)
                else:
                    last = nc.tensor.matmul(out, pack[:, p, PACKED.index(what), :], core.xT[:, b * T:(b + 1) * T],
                                            start=True, stop=True)
                last.then_inc(S["proj_full"], 1)

            def scores(n, m, s):
                i = BLOCKS[s]
                if s == 0:
                    pe.wait_ge(S["q_rotated"], n + 1)
                    pe.wait_ge(S["k_rotated"], n + 1)
                wait(pe, "a1_done", n * 4 + s - 1)
                nc.tensor.matmul(s_bank[:, s % 2, 0:WIDTH[i]], q[:, m % 2, i * P:(i + 1) * P], k[:, m % 4, 0:WIDTH[i]],
                                 start=True, stop=True).then_inc(S["s_full"], 1)

            def turn_probs(n, m, s):
                i = BLOCKS[s]
                pe.wait_ge(S["exp_done"], n * 4 + s + 1)
                wait(pe, pt_free[s % 2], n * 2 + s // 2)
                for j in range(i + 1):
                    last = nc.tensor.transpose(t_bank[:, s % 2, j * P:(j + 1) * P], part(u[:, m % 4], i)[:, j * P:(j + 1) * P],
                                               core.ident[:, :])
                last.then_inc(S["t_full"], 1)

            def values(n, m):
                pe.wait_ge(pt_free[0], n * 2 + 2)
                pe.wait_ge(pt_free[1], n * 2 + 2)
                wait(pe, "ot_done", n)
                for j in range(TB):
                    last = nc.tensor.matmul(o_bank[:, j * P:T], v[:, m % 4, j, :], pT[:, m % 2, j, j * P:T],
                                            start=(j == 0), stop=(j == TB - 1))
                last.then_inc(S["pv_full"], 1)

            def output(n, m, h, b):
                p = head_of(m)
                if b == 0:
                    pe.wait_ge(wo_ready[p], (h - p) * 8 + 16)
                pe.wait_ge(S["ot_done"], n + 1)
                wait(pe, "y_scaled", n)
                for j in range(TB):
                    last = nc.tensor.matmul(y_bank[:, j * P:(j + 1) * P], oT[:, m % 2, j * P:(j + 1) * P], wo[:, p, :],
                                            start=True, stop=True)
                last.then_inc(S["y_full"], 1)

            def step(n, m, h, b, last):
                old = (n - 2, (m - 2) % (UNROLL * B))
                done = (n - 3, (m - 3) % (UNROLL * B), h - (1 if b < 3 else 0), (b - 3) % B)

                def items(*numbers):
                    for idx in numbers:
                        what, off = ITEMS[idx]
                        if has_item(n, idx):
                            project(at(n, idx), what, n + off, (m + off) % (UNROLL * B), h + (b + off) // B, (b + off) % B)

                items(0)
                scores(n, m, 0)
                scores(n, m, 1)
                items(1)
                scores(n, m, 2)
                scores(n, m, 3)
                items(2, 3)
                if exists(old[0]):
                    turn_probs(*old, 0)
                    turn_probs(*old, 1)
                if exists(done[0]):
                    values(*done[:2])
                items(4, 5)
                if exists(old[0]):
                    turn_probs(*old, 2)
                    turn_probs(*old, 3)
                items(6)
                if exists(done[0]):
                    output(*done)

            pe.wait_ge(S["const_ready"], 9)
            for idx, (what, unit) in enumerate(AHEAD):
                project(ahead(idx), what, unit, unit, 0, unit)
            pipeline(pe, step)
            final = H * B
            for n in (final - 3, final - 2, final - 1):
                m = n % (UNROLL * B)
                if n > final - 3:
                    for s in range(4):
                        turn_probs(n, m, s)
                values(n, m)
                output(n, m, n // B, n % B)
            pe.sem_inc(S["turned"], 1)
            with pe.Fori(0, B) as b:
                pe.wait_ge(S["xn_ready"], b + 1)
                pe.wait_ge(S["taken"], b + 1)
                norm_turn(nc, core, proj_bank[:, 0, :]).then_inc(S["turned"], 1)


        def count_table(dve, instruction):
            table_chain.inc(instruction)
            table_chain.settle(dve)

        def angles(dve, t, p):
            table_chain.at(t * TABLE_STEPS)
            wait(dve, "phase_ready", t)
            count_table(dve, nc.vector.tensor_scalar(angle[:, :], steps[:, :], omega[:, ds(t, 1)], None, ALU.mult))
            count_table(dve, nc.vector.tensor_scalar(turns[:, :], angle[:, :], 1.0 / TWO_PI, ROUND, ALU.mult, ALU.add))
            count_table(dve, nc.vector.tensor_scalar(turns[:, :], turns[:, :], ROUND, None, ALU.subtract))

        def fold_angles(dve, t, p):
            table_chain.at(t * TABLE_STEPS + 3)
            for c in (C1, C2, C3):
                count_table(dve, nc.vector.scalar_tensor_tensor(angle[:, :], turns[:, :], -c, angle[:, :], ALU.mult, ALU.add))
            count_table(dve, nc.vector.tensor_scalar(angle[:, :], angle[:, :], BOUND, -BOUND, ALU.min, ALU.max))
            nc.vector.scalar_tensor_tensor(folded[:, :], angle[:, :], -1.0, angle[:, :], ALU.mult, ALU.max).then_inc(S["angle_ready"], 1)
            wait(dve, "etab_ready", t)
            nc.vector.tensor_scalar(z[:, :], dist[:, :], neg_mu[:, ds(t, 1)], -30.0, ALU.mult, ALU.max).then_inc(S["z_ready"], 1)

        def phases(act, t, p):
            act.wait_ge(S["angle_ready"], t + 1)
            wait(act, "k_rotated", (t - 1) * B)
            wait(act, "q_rotated", (t - 1) * B)
            nc.scalar.activation(sin[:, p, :], angle[:, :], ACT.Sin, scale=sign[:, 0:1])
            nc.scalar.activation(cos[:, p, :], folded[:, :], ACT.Sin, scale=-1.0, bias=half_pi[:, 0:1]).then_inc(S["phase_ready"], 1)

        def decays(act, t, p):
            act.wait_ge(S["z_ready"], t + 1)
            wait(act, "a2_done", (t - 1) * (B * 4))
            wait(act, "g_ready", (t - 1) * B)
            nc.scalar.activation(e_tab[:, p, :], z[:, :], ACT.Exp).then_inc(S["etab_ready"], 1)

        def variances(dve, t, p):
            table_chain.at(t * TABLE_STEPS + 7)
            dve.wait_ge(S["etab_ready"], t + 1)
            wait(dve, "lnv_ready", t)
            wait(dve, "r_done", (t - 1) * (B * 4))
            count_table(dve, nc.vector.tensor_tensor(var[:, :], e_tab[:, p, :], e_tab[:, p, :], ALU.mult))
            count_table(dve, nc.vector.tensor_scalar(var[:, :], var[:, :], -1.0, 1.0, ALU.mult, ALU.add))
            nc.vector.tensor_scalar(var[:, :], var[:, :], amp[:, ds(t, 1)], floor[:, ds(t, 1)], ALU.mult, ALU.add).then_inc(S["v_ready"], 1)
            dve.wait_ge(S["v_ready"], t + 1)
            count_table(dve, nc.vector.tensor_scalar(r_tab[:, p, :], var[:, :], soft[:, 3, ds(t, 1)], None, ALU.mult))

        def inverse_variances(dve, t, p, quarter):
            columns = r_tab[:, p, quarter * P:(quarter + 1) * P]
            nc.vector.reciprocal(columns, columns).then_inc(S["rtab_ready"], 1)

        def log_variances(act, t, p):
            act.wait_ge(S["v_ready"], t + 1)
            wait(act, "tables_ready", t)
            nc.scalar.activation(lnv[:, :], var[:, :], ACT.Ln).then_inc(S["lnv_ready"], 1)

        def additive(dve, t, p):
            dve.wait_ge(S["lnv_ready"], t + 1)
            wait(dve, "logit_done", (t - 1) * (B * 4))
            nc.vector.scalar_tensor_tensor(l_tab[:, p, :], lnv[:, :], -0.5 * DH, mask[:, :], ALU.mult, ALU.add).then_inc(S["tables_ready"], 1)

        @block.vector
        def _(dve):
            def const(instruction):
                const_chain.inc(instruction)
                const_chain.settle(dve)

            def rotate(swap_place, n, m, h, which):
                p = head_of(m)
                if which == 0 and m % B == 0:
                    dve.wait_ge(S["phase_ready"], h + 1)
                wait(dve, "q_rotated" if which else "k_rotated", n)
                for sw in range(2):
                    dve.wait_ge(S["proj_full"], swap_place[2] - 1 + sw)
                    nc.vector.scalar_tensor_tensor(parts[:, which, sw, :], proj_bank[:, sw, :], -2.0 if which else 1.0,
                                                   (sin if sw else cos)[:, p, :], ALU.mult, ALU.mult).then_inc(proj_free[sw], 1)

            def distances(n, m, s):
                i = BLOCKS[s]
                dve.wait_ge(S["s_full"], n * 4 + s + 1)
                if s == 0:
                    dve.wait_ge(S["g_ready"], n + 1)
                    wait(dve, "t_full", (n - 3) * 4)
                nc.vector.tensor_tensor(part(u[:, m % 4], i), s_bank[:, s % 2, 0:WIDTH[i]], part(g[:, m % 2], i), ALU.add)\
                  .then_inc(S["a1_done"], 1)

            def decay(n, m, s):
                i = BLOCKS[s]
                if s == 0:
                    dve.wait_ge(S["a1_done"], n * 4 + 4)
                here = part(u[:, m % 4], i)
                nc.vector.tensor_tensor(here, here, table(e_tab, head_of(m), i), ALU.mult).then_inc(S["a2_done"], 1)

            def logits(n, m, h, s):
                i = BLOCKS[s]
                if s == 0:
                    dve.wait_ge(S["ln_done"], n + 1)
                    if m % B == 0:
                        dve.wait_ge(S["tables_ready"], h + 1)
                here = part(u[:, m % 4], i)
                nc.vector.scalar_tensor_tensor(here, here, coef[:, ds(h, 1)], table(l_tab, head_of(m), i), ALU.mult, ALU.add)\
                  .then_inc(S["logit_done"], 1)

            def maximum(n, m, s):
                i = BLOCKS[s]
                if s == 0:
                    dve.wait_ge(S["logit_done"], n * 4 + 4)
                nc.vector.tensor_reduce(neg_max[:, m % 4, i:i + 1], part(u[:, m % 4], i), AX_X, ALU.max, negate=True)\
                  .then_inc(S["max_done"], 1)

            def take_turned(n, m, s):
                i = BLOCKS[s]
                dve.wait_ge(S["t_full"], n * 4 + s + 1)
                if s == 0:
                    wait(dve, "pv_full", n - 1)
                nc.vector.tensor_copy(pT[:, m % 2, 0:i + 1, i * P:(i + 1) * P],
                                      t_bank[:, 0, 0:WIDTH[i]].rearrange("p (j c) -> p j c", c=P)).then_inc(pt_free[0], 1)

            def scale_outputs(n, m):
                dve.wait_ge(S["exp_done"], n * 4 + 4)
                nc.vector.reciprocal(recip[:, m % 2, :], rowsum[:, m % 4, :]).then_inc(S["recip_done"], 1)
                dve.wait_ge(S["recip_done"], n + 1)
                dve.wait_ge(S["y_full"], n + 1)
                wait(dve, "x_done", n - 1)
                nc.vector.tensor_tensor(scaled[:, m % 2], y_bank[:, :].rearrange("p (j c) -> p j c", j=TB),
                                        recip[:, m % 2, :].unsqueeze(2).to_broadcast([P, TB, C]), ALU.mult).then_inc(S["y_scaled"], 1)

            def step(n, m, h, b, last):
                old = (n - 2, (m - 2) % (UNROLL * B))
                mid_head = h - (1 if b == 0 else 0)
                if m % B == 0:
                    dve.wait_ge(S["etab_ready"], h + 1)
                for s in range(4):
                    distances(n, m, s)
                for s in range(4):
                    decay(n, m, s)
                if exists(n - 4):
                    scale_outputs(n - 4, (m - 4) % (UNROLL * B))
                if has_item(n, 3):
                    rotate(at(n, 3), n + 1, (m + 1) % (UNROLL * B), h + (b + 1) // B, 1)
                if exists(n - 1):
                    for s in range(4):
                        logits(n - 1, (m - 1) % (UNROLL * B), mid_head, s)
                if exists(old[0]):
                    take_turned(*old, 0)
                if has_item(n, 5):
                    rotate(at(n, 5), n + 2, (m + 2) % (UNROLL * B), h + (b + 2) // B, 0)
                if exists(n - 1):
                    for s in range(4):
                        maximum(n - 1, (m - 1) % (UNROLL * B), s)
                if exists(old[0]):
                    take_turned(*old, 2)
                if tables_wanted(h):
                    p = 1 - head_of(m)
                    if b == 0:
                        angles(dve, h + 1, p)
                    if b == 1:
                        fold_angles(dve, h + 1, p)
                    if b == 3:
                        variances(dve, h + 1, p)
                    if b >= 4:
                        inverse_variances(dve, h + 1, p, b - 4)
                    if b == 6:
                        additive(dve, h + 1, p)

            dve.wait_ge(S["inputs_loaded"], 16 * len(inputs))
            for r in (1, 3):
                last = nc.vector.tensor_scalar(omega[32 * r:32 * r + 32, :], omega[32 * r:32 * r + 32, :], -1.0, None, ALU.mult)
            const(last)
            const(nc.vector.scalar_tensor_tensor(tmp[:, :, :], raw[:, :, :], -1.0, raw[:, :, :], ALU.mult, ALU.max))
            dve.wait_ge(S["soft_ln"], 1)
            const(nc.vector.scalar_tensor_tensor(soft[:, :, :], raw[:, :, :], 0.0, tmp[:, :, :], ALU.max, ALU.add))
            dve.wait_ge(S["mu_exp"], 1)
            const(nc.vector.tensor_scalar(mu[:, :], mu[:, :], 1.0, None, ALU.add))
            const(nc.vector.reciprocal(mu[:, :], mu[:, :]))
            const(nc.vector.tensor_scalar(mu[:, :], mu[:, :], 1e-4, None, ALU.add))
            const(nc.vector.tensor_scalar(neg_mu[:, :], mu[:, :], -1.0, None, ALU.mult))
            const(nc.vector.tensor_scalar(mu_recip[:, :], mu[:, :], 2.0, None, ALU.mult))
            const(nc.vector.reciprocal(mu_recip[:, :], mu_recip[:, :]))
            const(nc.vector.tensor_tensor(amp[:, :], soft[:, 0, :], mu_recip[:, :], ALU.mult))
            const(nc.vector.tensor_tensor(floor[:, :], soft[:, 1, :], soft[:, 2, :], ALU.add))
            const(nc.vector.tensor_scalar(coef[:, :], soft[:, 3, :], float(DH), -0.5, ALU.add, ALU.mult))
            const(nc.vector.tensor_tensor(coef[:, :], coef[:, :], tau[:, :], ALU.mult))
            dve.wait_ge(S["const_ready"], 9)
            const(nc.vector.scalar_tensor_tensor(dist[:, :], dist[:, :], -1.0, dist[:, :], ALU.mult, ALU.max))
            angles(dve, 0, 0)
            fold_angles(dve, 0, 0)
            variances(dve, 0, 0)
            for quarter_of in range(TB):
                inverse_variances(dve, 0, 0, quarter_of)
            additive(dve, 0, 0)
            rotate(ahead(1), 0, 0, 0, 0)
            rotate(ahead(3), 0, 0, 0, 1)
            rotate(ahead(7), 1, 1, 0, 0)
            pipeline(dve, step)
            final = H * B
            for n in (final - 4, final - 3):
                scale_outputs(n, n % (UNROLL * B))
            for s in range(4):
                logits(final - 1, UNROLL * B - 1, H - 1, s)
            for s in range(4):
                maximum(final - 1, UNROLL * B - 1, s)
            for n in (final - 2, final - 1):
                take_turned(n, n % (UNROLL * B), 0)
                take_turned(n, n % (UNROLL * B), 2)
                scale_outputs(n, n % (UNROLL * B))
            dve.wait_ge(S["x_done"], final)
            with dve.Fori(0, B) as b:
                chain.at(b * NORM_STEPS)
                norm_stats(nc, dve, core, chain, b).then_inc(S["var_ready"], 1)
                dve.wait_ge(S["rstd_ready"], b + 1)
                dve.wait_ge(S["turned"], b + 1)
                norm_apply(nc, core, b).then_inc(S["xn_ready"], 1)

        @block.scalar
        def _(act):
            def squares(n, m, which):
                if which:
                    act.wait_ge(S["q_rotated"], n + 1)
                    nc.scalar.activation(qsq[:, :], q[:, m % 2, :], ACT.Square).then_inc(S["q_squared"], 1)
                else:
                    act.wait_ge(S["k_rotated"], n + 1)
                    nc.scalar.activation(ksq[:, :], k[:, m % 4, :], ACT.Square).then_inc(S["k_squared"], 1)

            def take(place, what, n, m):
                bank, _, up_to = place
                act.wait_ge(S["proj_full"], up_to)
                out = proj_bank[:, bank, :]
                if what == "v":
                    nc.scalar.copy(v[:, m % 4, :, :], out.rearrange("p (j d) -> p j d", j=TB)).then_inc(proj_free[bank], 1)
                elif what == "knorm":
                    wait(act, "g_ready", n)
                    nc.scalar.copy(knorm[:, :], out).then_inc(proj_free[bank], 1)
                else:
                    nc.scalar.copy(qnorm[:, m % 2, :], out[:, 0:TB]).then_inc(proj_free[bank], 1)

            def relu(n, m, s):
                i = BLOCKS[s]
                if s == 0:
                    bank, before, _ = at(n, 0)
                    act.wait_ge(proj_free[bank], before + 1)
                act.wait_ge(S["a2_done"], n * 4 + s + 1)
                here = part(u[:, m % 4], i)
                nc.scalar.activation(here, here, ACT.Relu, bias=qnorm[:, m % 2, i:i + 1]).then_inc(S["relu_done"], 1)

            def log(n, m):
                act.wait_ge(S["r_done"], n * 4 + 4)
                nc.scalar.activation(u[:, m % 4, :], u[:, m % 4, :], ACT.Ln, bias=1.0).then_inc(S["ln_done"], 1)

            def exponentials(n, m, s):
                i = BLOCKS[s]
                act.wait_ge(S["max_done"], n * 4 + s + 1)
                here = part(u[:, m % 4], i)
                nc.scalar.activation(here, here, ACT.Exp, bias=neg_max[:, m % 4, i:i + 1],
                                     accum_out=rowsum[:, m % 4, i:i + 1]).then_inc(S["exp_done"], 1)

            def take_turned(n, m, s):
                i = BLOCKS[s]
                act.wait_ge(S["t_full"], n * 4 + s + 1)
                if s == 1:
                    wait(act, "pv_full", n - 1)
                nc.scalar.copy(pT[:, m % 2, 0:i + 1, i * P:(i + 1) * P],
                               t_bank[:, 1, 0:WIDTH[i]].rearrange("p (j c) -> p j c", c=P)).then_inc(pt_free[1], 1)

            def take_outputs(n, m):
                act.wait_ge(S["pv_full"], n + 1)
                wait(act, "y_full", n - 1)
                nc.scalar.copy(oT[:, m % 2, :], o_bank[:, :]).then_inc(S["ot_done"], 1)

            def step(n, m, h, b, last):
                after, nxt, mid, old = ((m + d) % (UNROLL * B) for d in (2, 1, -1, -2))
                if exists(n - 2):
                    for s in range(4):
                        exponentials(n - 2, old, s)
                if tables_wanted(h) and b == 2:
                    decays(act, h + 1, 1 - head_of(m))
                take(at(n, 0), "qnorm", n, m)
                if has_item(n, 1):
                    take(at(n, 1), "knorm", n + 1, nxt)
                if exists(n - 1):
                    log(n - 1, mid)
                if tables_wanted(h) and b == 4:
                    log_variances(act, h + 1, 1 - head_of(m))
                if exists(n - 2):
                    take_turned(n - 2, old, 1)
                for s in range(4):
                    relu(n, m, s)
                if exists(n - 3):
                    take_outputs(n - 3, (m - 3) % (UNROLL * B))
                if has_item(n, 3):
                    squares(n + 1, nxt, 1)
                if exists(n - 2):
                    take_turned(n - 2, old, 3)
                if has_item(n, 6):
                    take(at(n, 6), "v", n + 1, nxt)
                if has_item(n, 5):
                    squares(n + 2, after, 0)
                if tables_wanted(h) and b == 3:
                    phases(act, h + 1, 1 - head_of(m))

            act.wait_ge(const_chain.sem, 2)
            nc.scalar.activation(tmp[:, :, :], tmp[:, :, :], ACT.Exp, scale=-1.0).then_inc(S["soft_exp"], 1)
            nc.scalar.activation(mu[:, :], mu_raw[:, :], ACT.Exp, scale=-1.0).then_inc(S["mu_exp"], 1)
            act.wait_ge(S["soft_exp"], 1)
            nc.scalar.activation(tmp[:, :, :], tmp[:, :, :], ACT.Ln, bias=1.0).then_inc(S["soft_ln"], 1)
            act.wait_ge(S["const_ready"], 9)
            phases(act, 0, 0)
            decays(act, 0, 0)
            log_variances(act, 0, 0)
            squares(0, 0, 0)
            squares(0, 0, 1)
            take(ahead(4), "v", 0, 0)
            take(ahead(5), "knorm", 0, 0)
            squares(1, 1, 0)
            pipeline(act, step)
            final = H * B
            take_outputs(final - 3, (final - 3) % (UNROLL * B))
            for n in (final - 2, final - 1):
                m = n % (UNROLL * B)
                for s in range(4):
                    exponentials(n, m, s)
                if n < final - 1:
                    log(final - 1, UNROLL * B - 1)
                take_turned(n, m, 1)
                take_turned(n, m, 3)
                take_outputs(n, m)
            act.sem_inc(S["taken"], 1)
            with act.Fori(0, B) as b:
                act.wait_ge(S["turned"], b + 2)
                nc.scalar.copy(core.xT[:, ds(b * T, T)], proj_bank[:, 0, :]).then_inc(S["taken"], 1)

        @block.gpsimd
        def _(pool):
            def rotated(swap_place, n, m, which):
                bank, before, _ = swap_place
                pool.wait_ge(proj_free[bank], before + 1)
                wait(pool, "s_full", (n - (1 if which else 3)) * 4)
                out = q[:, m % 2, :] if which else k[:, m % 4, :]
                nc.gpsimd.tensor_tensor(out, parts[:, which, 0, :], parts[:, which, 1, :], ALU.add)\
                  .then_inc(S["q_rotated" if which else "k_rotated"], 1)

            def key_terms(place, n, m, h, b):
                bank, before, _ = place
                pool.wait_ge(proj_free[bank], before + 1)
                if b == 0:
                    pool.wait_ge(S["etab_ready"], h + 1)
                wait(pool, "a1_done", (n - 1) * 4)
                for i in BLOCKS:
                    last = nc.gpsimd.tensor_tensor(part(g[:, m % 2], i), knorm[:, 0:WIDTH[i]], table(e_tab, head_of(m), i), ALU.mult)
                last.then_inc(S["g_ready"], 1)

            def add_outputs(n, m, b):
                pool.wait_ge(S["y_scaled"], n + 1)
                wait(pool, "x_done", n)
                tokens = core.x[:, b * TB:(b + 1) * TB, :]
                nc.gpsimd.tensor_tensor(tokens, tokens, scaled[:, m % 2], ALU.add).then_inc(S["x_done"], 1)

            def over_variance(n, m, h, b, s):
                i = BLOCKS[s]
                if b == 0 and s == 0:
                    pool.wait_ge(S["rtab_ready"], h * TB + TB)
                pool.wait_ge(S["relu_done"], n * 4 + s + 1)
                here = part(u[:, m % 4], i)
                nc.gpsimd.tensor_tensor(here, here, table(r_tab, head_of(m), i), ALU.mult).then_inc(S["r_done"], 1)

            def step(n, m, h, b, last):
                nxt = (m + 1) % (UNROLL * B)
                if has_item(n, 1):
                    key_terms(at(n, 1), n + 1, nxt, h + (b + 1) // B, (b + 1) % B)
                if has_item(n, 3):
                    rotated(at(n, 3), n + 1, nxt, 1)
                if has_item(n, 5):
                    rotated(at(n, 5), n + 2, (m + 2) % (UNROLL * B), 0)
                if exists(n - 4):
                    add_outputs(n - 4, (m - 4) % (UNROLL * B), (b - 4) % B)
                for s in range(4):
                    over_variance(n, m, h, b, s)

            nc.gpsimd.memset(ones[:, :], 1.0).then_inc(S["const_ready"], 1)
            nc.gpsimd.memset(quarter[:, :], 0.25).then_inc(S["const_ready"], 1)
            nc.gpsimd.memset(sign[:, :], 1.0).then_inc(S["const_ready"], 1)
            nc.gpsimd.memset(half_pi[:, :], HALF_PI).then_inc(S["const_ready"], 1)
            nc.gpsimd.memset(mask[:, :], 0.0).then_inc(S["const_ready"], 1)
            nc.gpsimd.iota(steps[:, :], pattern=[[1, T]], base=0, channel_multiplier=0,
                           allow_small_or_imprecise_dtypes=True).then_inc(S["const_ready"], 1)
            nc.gpsimd.iota(dist[:, :], pattern=[[-1, T]], base=T - P, channel_multiplier=1,
                           allow_small_or_imprecise_dtypes=True).then_inc(S["const_ready"], 1)
            pool.wait_ge(S["const_ready"], 7)
            nc.gpsimd.memset(sign[0:DH, :], -1.0).then_inc(S["const_ready"], 1)
            nc.gpsimd.affine_select(out=mask[:, :], in_=mask[:, :], compare_op=ALU.is_ge, fill=NEG, base=T - P,
                                    pattern=[[-1, T]], channel_multiplier=1).then_inc(S["const_ready"], 1)
            rotated(ahead(1), 0, 0, 0)
            rotated(ahead(3), 0, 0, 1)
            key_terms(ahead(5), 0, 0, 0, 0)
            rotated(ahead(7), 1, 1, 0)
            pipeline(pool, step)
            for n in range(H * B - 4, H * B):
                add_outputs(n, n % (UNROLL * B), n % B)
            with pool.Fori(0, B) as b:
                pool.wait_ge(S["var_ready"], b + 1)
                norm_rstd(nc, core).then_inc(S["rstd_ready"], 1)


ROPE_CAUSAL = Attention(heads=16, dim=8, kv_heads=16, causal=True, rope=1, bias=True, gate=False)
GROUPED = Attention(heads=8, dim=32, kv_heads=2, causal=False, rope=1, bias=False, gate=True)
BILINEAR = Attention(heads=16, dim=8, kv_heads=16, causal=False, rope=0, bias=True, gate=False)


def build(nc, dram, plan):
    with ExitStack() as ctx:
        core = Core(nc, ctx, dram)
        stage_load(core)
        core.end_stage()
        for stage in plan:
            if stage == "attn_rope":
                stage_attention(core, ROPE_CAUSAL, {n: dram["a_" + n] for n in (
                    "wq", "wq_swap", "wk", "wk_swap", "bq", "bq_swap", "bk", "bk_swap", "wv", "bv", "wo", "bo", "cos", "sin", "keep", "minus", "scratch")})
            elif stage == "attn_gqa":
                stage_attention(core, GROUPED, {n: dram["g_" + n] for n in (
                    "wq", "wq_swap", "wk", "wk_swap", "wv", "wo", "wg", "cos", "sin", "keep", "minus", "scratch")})
            elif stage == "attn_bilinear":
                stage_attention(core, BILINEAR, {n: dram["v_" + n] for n in ("wq", "wk", "wv", "bv", "wo", "bo", "keep", "minus", "scratch")})
            elif stage == "attn_decay":
                stage_decay(core, {n: dram["d_" + n] for n in ("sigma", "eta", "gamma", "nu", "mu", "tau", "omega", "pack", "wo")})
            elif stage == "ffn_linear":
                stage_ffn(core, {n: dram["f_" + n] for n in ("router", "w_in", "w_out")}, 8, None)
            elif stage == "ffn_gated":
                stage_ffn(core, {n: dram["h_" + n] for n in ("router", "wg", "wu", "wd")}, 9, 352)
            core.end_stage()
        stage_store(core)
        core.end_stage()



def _tables(dim, rot, pairs_adjacent):
    half = rot // 2
    f = np.arange(half, dtype=np.float32)
    theta = np.power(np.float32(10000.0), (np.float32(-2.0) * f / np.float32(rot)).astype(np.float32)).astype(np.float32)
    ang = (np.arange(T, dtype=np.float32)[None, :] * theta[:, None]).astype(np.float32).astype(np.float64)
    cos, sin = np.ones((P, T), np.float32), np.zeros((P, T), np.float32)
    for c in range(P):
        d = c % dim
        if d < rot:
            n, low = (d // 2, d % 2 == 0) if pairs_adjacent else (d % half, d < half)
            cos[c] = np.cos(ang[n])
            sin[c] = -np.sin(ang[n]) if low else np.sin(ang[n])
    return cos, sin


def kernel(**inputs):
    import ml_dtypes
    import concourse.bacc as _bacc
    from concourse.bass_utils import run_bass_kernel_spmd as _run

    i = {n: np.asarray(a) for n, a in inputs.items()}
    a = {"x": i["L0_attn_a_x"]}
    eye, low = np.eye(P, dtype=np.float32), np.tril(np.ones((P, P), bool))
    a["ident"], a["ident16"] = eye, eye.astype(ml_dtypes.bfloat16)
    a["mask_ij"] = np.where(low, 0.0, NEG).astype(ml_dtypes.bfloat16)
    a["mask_ji"] = np.where(low.T, 0.0, NEG).astype(ml_dtypes.bfloat16)

    for n, cfg in (("a", ROPE_CAUSAL), ("g", GROUPED), ("v", BILINEAR)):
        a[f"{n}_keep"] = np.ones((P, 1), np.float32)
        for row in range(cfg.max_row, P, cfg.lane):
            a[f"{n}_keep"][row:row + MAX_PARTS] = 0.0
        a[f"{n}_minus"] = np.full((MAX_PARTS, max(cfg.kv_heads // cfg.lanes, 1), T), -1.0, ml_dtypes.bfloat16)

    partner = np.arange(C) ^ 1
    for n in "qk":
        wt = i["L0_attn_a_w" + n].T
        a[f"a_w{n}"], a[f"a_w{n}_swap"] = wt, wt[:, partner]
        for tail, bias in (("", i["L0_attn_a_b" + n]), ("_swap", i["L0_attn_a_b" + n][partner])):
            a[f"a_b{n}{tail}"] = bias
    a["a_wv"], a["a_bv"] = i["L0_attn_a_wv"].T, i["L0_attn_a_bv"]
    a["a_wo"], a["a_bo"] = i["L0_attn_a_wp"].T, i["L0_attn_a_bp"]
    a["a_cos"], a["a_sin"] = _tables(8, 8, True)

    d = np.arange(32)
    within = np.where(d < 8, (d + 4) % 8, d)
    a["g_wq"], a["g_wg"] = i["L1_attn_a_Wq"][:, :256], i["L1_attn_a_Wq"][:, 256:]
    a["g_wq_swap"] = a["g_wq"][:, (np.arange(8)[:, None] * 32 + within).ravel()]
    a["g_wk"] = i["L1_attn_a_Wk"]
    a["g_wk_swap"] = a["g_wk"][:, (np.arange(2)[:, None] * 32 + within).ravel()]
    a["g_wv"], a["g_wo"] = i["L1_attn_a_Wv"], i["L1_attn_a_Wo"]
    a["g_cos"], a["g_sin"] = _tables(32, 8, False)

    wq = np.zeros((C, C), np.float32)
    for h in range(16):
        wq[8 * h:8 * h + 8, 8 * h:8 * h + 8] = i["L1_attn_b_w_att_val"][h]
    a["v_wq"], a["v_wk"] = wq, eye
    a["v_wv"], a["v_bv"] = i["L1_attn_b_wv_w"].T, i["L1_attn_b_wv_b"]
    a["v_wo"], a["v_bo"] = i["L1_attn_b_out_w"].T, i["L1_attn_b_out_b"]

    def by_head(wt):
        return wt.reshape(C, 2, 16, 64).transpose(2, 0, 1, 3)
    wq, wk, wv = (by_head(i["L0_attn_b_W" + n]) for n in "qkv")
    a["d_pack"] = np.stack([t.reshape(16, C, P) for t in (wk, wk[:, :, ::-1], wq, wq[:, :, ::-1], wv)], axis=2)
    a["d_wo"] = i["L0_attn_b_Wo"].reshape(2, 16, 64, C).transpose(1, 0, 2, 3).reshape(16, P, C)
    for n, name in (("sigma", "sigma_raw"), ("eta", "eta_raw"), ("gamma", "gamma_raw"), ("nu", "nu_raw"), ("mu", "mu_raw"), ("tau", "tau")):
        a["d_" + n] = i["L0_attn_b_" + name]
    a["d_omega"] = i["L0_attn_b_omega"].T

    a["f_router"], a["f_w_in"], a["f_w_out"] = i["L0_ffn_w_gate"].T, i["L0_ffn_w_in"], i["L0_ffn_w_out"].transpose(0, 2, 1)
    for n, name in (("router", "Wr"), ("wg", "Wg"), ("wu", "Wu"), ("wd", "Wd")):
        a["h_" + n] = i["L1_ffn_" + name]

    nc = _bacc.Bacc("TRN2", target_bir_lowering=False, num_devices=1)
    arrays, dram = {}, {}
    for n, t in a.items():
        t = np.ascontiguousarray(t)
        arrays[f"in_{n}"] = t
        dram[n] = nc.dram_tensor(f"in_{n}", t.shape, mybir.dt.from_np(t.dtype), kind="ExternalInput").ap()
    for n, cfg in (("a", ROPE_CAUSAL), ("g", GROUPED), ("v", BILINEAR)):
        dram[f"{n}_scratch"] = nc.dram_tensor(f"{n}_scratch", (2, len(cfg.tiles), 3, P, T), BF16, kind="Internal").ap()
    dram["out"] = nc.dram_tensor("out_0_dram", (B, T, C), F32, kind="ExternalOutput").ap()
    build(nc, dram, PLAN)
    r = _run(nc, [arrays], core_ids=[0])
    return r.results[0]["out_0_dram"]
```
